# Optimizing a Trainium2 kernel written in Bass

```python
import numpy as np
import jax
import jax.numpy as jnp

def _softmax(x, axis=-1):
    return jax.nn.softmax(x, axis=axis)

def _gelu(x):
    return jax.nn.gelu(x, approximate=True)

def _silu(x):
    return jax.nn.silu(x)

def _sigmoid(x):
    return jax.nn.sigmoid(x)

def _layernorm(x, axis=-1, eps=1e-05):
    m = jnp.mean(x, axis=axis, keepdims=True)
    v = jnp.var(x, axis=axis, keepdims=True)
    return (x - m) / jnp.sqrt(v + eps)

def _scatter_add(tgt, idx, src, axis=0):
    return tgt.at[idx].add(src)

def _segment_sum(src, seg, n):
    return jax.ops.segment_sum(src, seg, n)
kernel_name = 'mk_decoder_postln_d2_seqx_r8_3af2d2'

def setup_inputs(seed: int=0):
    np.random.seed(seed)
    _w = jnp.asarray

    def _rec_inputs():
        import jax
        import jax.numpy as jnp
        _rk = jax.random.key(seed)
        x = -0.0002928 + 1 * jax.random.normal(jax.random.fold_in(_rk, 1), (32, 64, 128), jnp.float32)
        _lenS = 64 - jax.random.randint(jax.random.fold_in(_rk, 7), (32,), 0, max(1, 64 // 4) + 1, jnp.int32)
        _lenS2 = 64 - jax.random.randint(jax.random.fold_in(_rk, 8), (32,), 0, max(1, 64 // 4) + 1, jnp.int32)
        _ctx_1024P = jax.random.normal(jax.random.fold_in(_rk, 11), (32, 16, 128), jnp.float32)
        _ctx_1024c = jax.random.dirichlet(jax.random.fold_in(_rk, 511), 0.3 * jnp.ones((16,), jnp.float32), (32, 64))
        _ctx_1024t = jnp.einsum('bsk,bkd->bsd', _ctx_1024c, _ctx_1024P)
        _ctx_1024t = _ctx_1024t * jax.lax.rsqrt(jnp.mean(jnp.square(_ctx_1024t)) + 1e-12) * 0.953939
        ctx_1024 = -1.39393e-06 + 0.999914 * (_ctx_1024t + 0.3 * jax.random.normal(jax.random.fold_in(_rk, 611), (32, 64, 128), jnp.float32))
        _validS = jnp.arange(64)[None, :] < _lenS[:, None]
        _validS2 = jnp.arange(64)[None, :] < _lenS2[:, None]
        _causal = jnp.tril(jnp.ones((64, 64), dtype=bool))
        mask_BxS2_ik0 = jnp.where(jnp.broadcast_to(_validS2[:, :], (32, 64)), 0, 1).astype(jnp.int32)
        return (x, ctx_1024, mask_BxS2_ik0)
    x, ctx_1024, mask_BxS2_ik0 = _rec_inputs()

    def _L0_attn_setup():
        import jax, jax.numpy as jnp
        import numpy as np
        B, T, C = (4, 256, 128)
        NH = 16
        HS = C // NH
        key = jax.random.key(seed)
        ks = jax.random.split(key, 6)
        s = 1.0 / np.sqrt(C)
        return {'x': jax.random.normal(ks[0], (B, T, C), dtype=jnp.float32), 'Wk': jax.random.normal(ks[1], (C, C), dtype=jnp.float32) * s, 'Wq': jax.random.normal(ks[2], (C, C), dtype=jnp.float32) * s, 'Wv': jax.random.normal(ks[3], (C, C), dtype=jnp.float32) * s, 'Wo': jax.random.normal(ks[4], (C, C), dtype=jnp.float32) * s, 'bo': jnp.zeros((C,), dtype=jnp.float32)}
    _L0_attn_all = _L0_attn_setup()
    _L0_attn_in = {k: v for k, v in _L0_attn_all.items() if k in ('Wk', 'Wq', 'Wv', 'Wo', 'bo')}
    del _L0_attn_all

    def _L0_xattn_setup():
        import jax, jax.numpy as jnp
        import numpy as np
        DIM = 128
        NUM_HEADS = 16
        HEAD_DIM = DIM // NUM_HEADS
        key = jax.random.key(seed)
        ks = jax.random.split(key, 8)
        B, Nq, Nkv = (2, 256, 256)
        s = 1.0 / np.sqrt(DIM)
        return {'feat1_query': jax.random.normal(ks[0], (B, Nq, DIM), dtype=jnp.float32), 'feat2_key_value': jax.random.normal(ks[1], (B, Nkv, DIM), dtype=jnp.float32), 'Wq': jax.random.normal(ks[2], (DIM, DIM), dtype=jnp.float32) * s, 'Wk': jax.random.normal(ks[3], (DIM, DIM), dtype=jnp.float32) * s, 'Wv': jax.random.normal(ks[4], (DIM, DIM), dtype=jnp.float32) * s, 'Wo': jax.random.normal(ks[5], (DIM, DIM), dtype=jnp.float32) * s, 'bo': jnp.zeros((DIM,), dtype=jnp.float32), 'mask': jax.random.randint(ks[6], (B, Nkv), 0, 2, dtype=jnp.int32)}
    _L0_xattn_all = _L0_xattn_setup()
    _L0_xattn_in = {k: v for k, v in _L0_xattn_all.items() if k in ('Wq', 'Wk', 'Wv', 'Wo', 'bo')}
    del _L0_xattn_all

    def _L0_ffn_setup():
        import jax, jax.numpy as jnp
        import numpy as np
        TOP_K = 2
        key = jax.random.key(seed)
        kx, kg, k1, k2 = jax.random.split(key, 4)
        B, T, D, E, H = (4, 128, 128, 8, 256)
        x = jax.random.normal(kx, (B, T, D), dtype=jnp.float32)
        Wg = jax.random.normal(kg, (D, E), dtype=jnp.float32) * 0.02
        W1 = jax.random.normal(k1, (E, D, H), dtype=jnp.float32) * 0.02
        W2 = jax.random.normal(k2, (E, H, D), dtype=jnp.float32) * 0.02
        return {'x': x, 'Wg': Wg, 'W1': W1, 'W2': W2}
    _L0_ffn_all = _L0_ffn_setup()
    _L0_ffn_in = {k: v for k, v in _L0_ffn_all.items() if k in ('Wg', 'W1', 'W2')}
    del _L0_ffn_all

    def _L1_attn_setup():
        import jax, jax.numpy as jnp
        import numpy as np
        import math
        E = 128
        H = 16
        B = 2
        T = 256

        def _rotary(x):
            D = x.shape[-1]
            inv_freq = 1.0 / 10000.0 ** (jnp.arange(0, D, 2, dtype=jnp.float32) / D)
            t = jnp.arange(x.shape[-2], dtype=jnp.float32)
            freqs = t[:, None] * inv_freq[None, :]
            emb = jnp.concatenate([freqs, freqs], axis=-1)
            cos = jnp.cos(emb)
            sin = jnp.sin(emb)
            x1 = x[..., ::2]
            x2 = x[..., 1::2]
            x_rot = jnp.stack([-x2, x1], axis=-1).reshape(x.shape)
            return x * cos + x_rot * sin
        key = jax.random.key(seed)
        ks = jax.random.split(key, 10)
        s = 0.02
        inp = {'x': jax.random.normal(ks[0], (B, T, E), dtype=jnp.float32), 'Wq': jax.random.normal(ks[1], (E, E), dtype=jnp.float32) * s, 'bq': jnp.zeros((E,), jnp.float32), 'Wk': jax.random.normal(ks[2], (E, E), dtype=jnp.float32) * s, 'bk': jnp.zeros((E,), jnp.float32), 'Wv': jax.random.normal(ks[3], (E, E), dtype=jnp.float32) * s, 'bv': jnp.zeros((E,), jnp.float32), 'Wg': jax.random.normal(ks[4], (E, E), dtype=jnp.float32) * s, 'bg': jnp.zeros((E,), jnp.float32), 'gamma': jax.random.normal(ks[5], (H,), dtype=jnp.float32)}
        return inp
    _L1_attn_all = _L1_attn_setup()
    _L1_attn_in = {k: v for k, v in _L1_attn_all.items() if k in ('Wq', 'bq', 'Wk', 'bk', 'Wv', 'bv', 'Wg', 'bg', 'gamma')}
    del _L1_attn_all

    def _L1_xattn_setup():
        import jax, jax.numpy as jnp
        import numpy as np
        B, SD, SE, D, H = (4, 256, 256, 128, 16)
        HD = D // H

        def _mha(xq, xk, xv, Wq, bq, Wk, bk, Wv, bv, Wo, bo, causal):
            q = jnp.einsum('bsd,hde->bhse', xq, Wq) + bq[None, :, None, :]
            k = jnp.einsum('bsd,hde->bhse', xk, Wk) + bk[None, :, None, :]
            v = jnp.einsum('bsd,hde->bhse', xv, Wv) + bv[None, :, None, :]
            scale = 1.0 / jnp.sqrt(jnp.asarray(HD, q.dtype))
            scores = jnp.einsum('bhqe,bhke->bhqk', q, k) * scale
            if causal:
                mask = jnp.tril(jnp.ones((q.shape[2], k.shape[2]), bool))
                scores = jnp.where(mask, scores, jnp.finfo(scores.dtype).min)
            w = jax.nn.softmax(scores, axis=-1)
            out = jnp.einsum('bhqk,bhke->bhqe', w, v)
            out = out.transpose(0, 2, 1, 3).reshape(out.shape[0], out.shape[2], D)
            return out @ Wo + bo
        key = jax.random.key(seed)
        ks = jax.random.split(key, 19)
        sd = 1.0 / np.sqrt(D)
        n = lambda k, shape, s: jax.random.normal(k, shape, jnp.float32) * s
        inp = {'x': n(ks[0], (B, SD, D), 1.0), 'encoder_k': n(ks[1], (B, SE, D), 1.0), 'encoder_v': n(ks[2], (B, SE, D), 1.0), 'Wq1': n(ks[3], (H, D, HD), sd), 'bq1': jnp.zeros((H, HD), jnp.float32), 'Wk1': n(ks[4], (H, D, HD), sd), 'bk1': jnp.zeros((H, HD), jnp.float32), 'Wv1': n(ks[5], (H, D, HD), sd), 'bv1': jnp.zeros((H, HD), jnp.float32), 'Wo1': n(ks[6], (D, D), sd), 'bo1': jnp.zeros((D,), jnp.float32), 'Wq2': n(ks[7], (H, D, HD), sd), 'bq2': jnp.zeros((H, HD), jnp.float32), 'Wk2': n(ks[8], (H, D, HD), sd), 'bk2': jnp.zeros((H, HD), jnp.float32), 'Wv2': n(ks[9], (H, D, HD), sd), 'bv2': jnp.zeros((H, HD), jnp.float32), 'Wo2': n(ks[10], (D, D), sd), 'bo2': jnp.zeros((D,), jnp.float32)}
        return inp
    _L1_xattn_all = _L1_xattn_setup()
    _L1_xattn_in = {k: v for k, v in _L1_xattn_all.items() if k in ('Wq1', 'bq1', 'Wk1', 'bk1', 'Wv1', 'bv1', 'Wo1', 'bo1', 'Wq2', 'bq2', 'Wk2', 'bk2', 'Wv2', 'bv2', 'Wo2', 'bo2')}
    del _L1_xattn_all

    def _L1_ffn_setup():
        import jax, jax.numpy as jnp
        import numpy as np
        B, S, H, F, E = (8, 256, 128, 512, 8)
        INIT_LAMBDA = 0.2
        key = jax.random.key(seed)
        ks = jax.random.split(key, 12)
        std = 0.02
        return {'hidden_states': jax.random.normal(ks[0], (B, S, H), jnp.float32), 'gate_w1': jax.random.normal(ks[1], (H, H), jnp.float32) * 0.01, 'gate_b1': jnp.zeros((H,), jnp.float32), 'gate_w2': jax.random.normal(ks[2], (E, H), jnp.float32) * 0.01, 'gate_b2': jnp.full((E,), INIT_LAMBDA, jnp.float32), 'W1': jax.random.normal(ks[3], (F, H), jnp.float32) * std, 'b1': jax.random.normal(ks[4], (F,), jnp.float32) * std, 'W2': jax.random.normal(ks[5], (H, F), jnp.float32) * std, 'b2': jax.random.normal(ks[6], (H,), jnp.float32) * std, 'TW1': jax.random.normal(ks[7], (E, F, H), jnp.float32) * std, 'Tb1': jax.random.normal(ks[8], (E, F), jnp.float32) * std, 'TW2': jax.random.normal(ks[9], (E, H, F), jnp.float32) * std, 'Tb2': jax.random.normal(ks[10], (E, H), jnp.float32) * std}
    _L1_ffn_all = _L1_ffn_setup()
    _L1_ffn_in = {k: v for k, v in _L1_ffn_all.items() if k in ('gate_w1', 'gate_b1', 'gate_w2', 'gate_b2', 'W1', 'b1', 'W2', 'b2', 'TW1', 'Tb1', 'TW2', 'Tb2')}
    del _L1_ffn_all
    return {'x': x, 'ctx_1024': ctx_1024, 'mask_BxS2_ik0': mask_BxS2_ik0, 'L0_attn_Wk': _L0_attn_in['Wk'], 'L0_attn_Wq': _L0_attn_in['Wq'], 'L0_attn_Wv': _L0_attn_in['Wv'], 'L0_attn_Wo': _L0_attn_in['Wo'], 'L0_attn_bo': _L0_attn_in['bo'], 'L0_xattn_Wq': _L0_xattn_in['Wq'], 'L0_xattn_Wk': _L0_xattn_in['Wk'], 'L0_xattn_Wv': _L0_xattn_in['Wv'], 'L0_xattn_Wo': _L0_xattn_in['Wo'], 'L0_xattn_bo': _L0_xattn_in['bo'], 'L0_ffn_Wg': _L0_ffn_in['Wg'], 'L0_ffn_W1': _L0_ffn_in['W1'], 'L0_ffn_W2': _L0_ffn_in['W2'], 'L1_attn_Wq': _L1_attn_in['Wq'], 'L1_attn_bq': _L1_attn_in['bq'], 'L1_attn_Wk': _L1_attn_in['Wk'], 'L1_attn_bk': _L1_attn_in['bk'], 'L1_attn_Wv': _L1_attn_in['Wv'], 'L1_attn_bv': _L1_attn_in['bv'], 'L1_attn_Wg': _L1_attn_in['Wg'], 'L1_attn_bg': _L1_attn_in['bg'], 'L1_attn_gamma': _L1_attn_in['gamma'], 'L1_xattn_Wq1': _L1_xattn_in['Wq1'], 'L1_xattn_bq1': _L1_xattn_in['bq1'], 'L1_xattn_Wk1': _L1_xattn_in['Wk1'], 'L1_xattn_bk1': _L1_xattn_in['bk1'], 'L1_xattn_Wv1': _L1_xattn_in['Wv1'], 'L1_xattn_bv1': _L1_xattn_in['bv1'], 'L1_xattn_Wo1': _L1_xattn_in['Wo1'], 'L1_xattn_bo1': _L1_xattn_in['bo1'], 'L1_xattn_Wq2': _L1_xattn_in['Wq2'], 'L1_xattn_bq2': _L1_xattn_in['bq2'], 'L1_xattn_Wk2': _L1_xattn_in['Wk2'], 'L1_xattn_bk2': _L1_xattn_in['bk2'], 'L1_xattn_Wv2': _L1_xattn_in['Wv2'], 'L1_xattn_bv2': _L1_xattn_in['bv2'], 'L1_xattn_Wo2': _L1_xattn_in['Wo2'], 'L1_xattn_bo2': _L1_xattn_in['bo2'], 'L1_ffn_gate_w1': _L1_ffn_in['gate_w1'], 'L1_ffn_gate_b1': _L1_ffn_in['gate_b1'], 'L1_ffn_gate_w2': _L1_ffn_in['gate_w2'], 'L1_ffn_gate_b2': _L1_ffn_in['gate_b2'], 'L1_ffn_W1': _L1_ffn_in['W1'], 'L1_ffn_b1': _L1_ffn_in['b1'], 'L1_ffn_W2': _L1_ffn_in['W2'], 'L1_ffn_b2': _L1_ffn_in['b2'], 'L1_ffn_TW1': _L1_ffn_in['TW1'], 'L1_ffn_Tb1': _L1_ffn_in['Tb1'], 'L1_ffn_TW2': _L1_ffn_in['TW2'], 'L1_ffn_Tb2': _L1_ffn_in['Tb2']}

def reference(x, ctx_1024, mask_BxS2_ik0, L0_attn_Wk, L0_attn_Wq, L0_attn_Wv, L0_attn_Wo, L0_attn_bo, L0_xattn_Wq, L0_xattn_Wk, L0_xattn_Wv, L0_xattn_Wo, L0_xattn_bo, L0_ffn_Wg, L0_ffn_W1, L0_ffn_W2, L1_attn_Wq, L1_attn_bq, L1_attn_Wk, L1_attn_bk, L1_attn_Wv, L1_attn_bv, L1_attn_Wg, L1_attn_bg, L1_attn_gamma, L1_xattn_Wq1, L1_xattn_bq1, L1_xattn_Wk1, L1_xattn_bk1, L1_xattn_Wv1, L1_xattn_bv1, L1_xattn_Wo1, L1_xattn_bo1, L1_xattn_Wq2, L1_xattn_bq2, L1_xattn_Wk2, L1_xattn_bk2, L1_xattn_Wv2, L1_xattn_bv2, L1_xattn_Wo2, L1_xattn_bo2, L1_ffn_gate_w1, L1_ffn_gate_b1, L1_ffn_gate_w2, L1_ffn_gate_b2, L1_ffn_W1, L1_ffn_b1, L1_ffn_W2, L1_ffn_b2, L1_ffn_TW1, L1_ffn_Tb1, L1_ffn_TW2, L1_ffn_Tb2):
    import jax
    import jax.numpy as jnp

    def _L0_attn_ref(x, Wk, Wq, Wv, Wo, bo):
        import jax, jax.numpy as jnp
        import numpy as np
        B, T, C = (4, 256, 128)
        NH = 16
        HS = C // NH
        b, t, c = x.shape
        nh, hs = (NH, c // NH)
        k = (x @ Wk.T).reshape(b, t, nh, hs).transpose(0, 2, 1, 3)
        q = (x @ Wq.T).reshape(b, t, nh, hs).transpose(0, 2, 1, 3)
        v = (x @ Wv.T).reshape(b, t, nh, hs).transpose(0, 2, 1, 3)
        att = jnp.einsum('bhqd,bhkd->bhqk', q, k) * (1.0 / np.sqrt(hs))
        causal = jnp.tril(jnp.ones((t, t), dtype=bool))
        att = jnp.where(causal, att, jnp.float32(-jnp.inf))
        att = jax.nn.softmax(att, axis=-1)
        y = jnp.einsum('bhqk,bhkd->bhqd', att, v)
        y = y.transpose(0, 2, 1, 3).reshape(b, t, c)
        return y @ Wo.T + bo

    def _L0_xattn_ref(feat1_query, feat2_key_value, Wq, Wk, Wv, Wo, bo, mask):
        import jax, jax.numpy as jnp
        import numpy as np
        DIM = 128
        NUM_HEADS = 16
        HEAD_DIM = DIM // NUM_HEADS
        B, Nq, C = feat1_query.shape
        Nkv = feat2_key_value.shape[1]
        H, Dh = (NUM_HEADS, HEAD_DIM)
        Q = (feat1_query @ Wq.T).reshape(B, Nq, H, Dh).transpose(0, 2, 1, 3)
        K = (feat2_key_value @ Wk.T).reshape(B, Nkv, H, Dh).transpose(0, 2, 1, 3)
        V = (feat2_key_value @ Wv.T).reshape(B, Nkv, H, Dh).transpose(0, 2, 1, 3)
        dots = jnp.einsum('bhqd,bhkd->bhqk', Q, K) / jnp.sqrt(jnp.float32(Dh))
        dots = jnp.where(mask[:, None, None, :] == 0, jnp.float32(-1000000000.0), dots)
        attn = jax.nn.softmax(dots, axis=-1)
        out = jnp.einsum('bhqk,bhkd->bhqd', attn, V)
        out = out.transpose(0, 2, 1, 3).reshape(B, Nq, C)
        return out @ Wo.T + bo

    def _L0_ffn_ref(x, Wg, W1, W2):
        import jax, jax.numpy as jnp
        import numpy as np
        TOP_K = 2
        B, T, D = x.shape
        E = W1.shape[0]
        logits = jnp.einsum('btd,de->bte', x, Wg)
        probs = jax.nn.softmax(logits, axis=-1)
        top_w, top_i = jax.lax.top_k(probs, TOP_K)
        top_w = top_w / (jnp.sum(top_w, axis=-1, keepdims=True) + 1e-08)
        N = B * T
        oh = jax.nn.one_hot(top_i.reshape(N, TOP_K), E, dtype=x.dtype)
        combine = jnp.sum(oh * top_w.reshape(N, TOP_K)[..., None], axis=1)
        xt = x.reshape(N, D)
        h = jnp.einsum('td,edh->teh', xt, W1)
        h = jnp.square(jax.nn.relu(h))
        y = jnp.einsum('teh,ehd->ted', h, W2)
        out = jnp.einsum('te,ted->td', combine, y)
        return out.reshape(B, T, D)

    def _L1_attn_ref(x, Wq, bq, Wk, bk, Wv, bv, Wg, bg, gamma):
        import jax, jax.numpy as jnp
        import numpy as np
        import math
        E = 128
        H = 16
        B = 2
        T = 256

        def _rotary(x):
            D = x.shape[-1]
            inv_freq = 1.0 / 10000.0 ** (jnp.arange(0, D, 2, dtype=jnp.float32) / D)
            t = jnp.arange(x.shape[-2], dtype=jnp.float32)
            freqs = t[:, None] * inv_freq[None, :]
            emb = jnp.concatenate([freqs, freqs], axis=-1)
            cos = jnp.cos(emb)
            sin = jnp.sin(emb)
            x1 = x[..., ::2]
            x2 = x[..., 1::2]
            x_rot = jnp.stack([-x2, x1], axis=-1).reshape(x.shape)
            return x * cos + x_rot * sin
        Bb, Tt, Ee = x.shape
        Hh = gamma.shape[0]
        Dd = Ee // Hh

        def proj(W, b):
            return (x @ W.T + b).reshape(Bb, Tt, Hh, Dd).transpose(0, 2, 1, 3)
        Q = _rotary(proj(Wq, bq))
        K = _rotary(proj(Wk, bk))
        V = proj(Wv, bv)
        g = jax.nn.sigmoid(gamma)
        idx = jnp.arange(Tt)
        diff = jnp.clip(idx[:, None] - idx[None, :], 0, None).astype(jnp.float32)
        t_w = jnp.exp(-g[:, None, None] * diff)
        scores = jnp.einsum('bhtd,bhsd->bhts', Q, K) / math.sqrt(Dd)
        out = jnp.einsum('bhts,bhsd->bhtd', scores * t_w[None], V)
        out = out.transpose(0, 2, 1, 3).reshape(Bb, Tt, Ee)
        gate = jax.nn.silu(x @ Wg.T + bg)
        return gate * out

    def _L1_xattn_ref(x, encoder_k, encoder_v, Wq1, bq1, Wk1, bk1, Wv1, bv1, Wo1, bo1, Wq2, bq2, Wk2, bk2, Wv2, bv2, Wo2, bo2):
        import jax, jax.numpy as jnp
        import numpy as np
        B, SD, SE, D, H = (4, 256, 256, 128, 16)
        HD = D // H

        def _mha(xq, xk, xv, Wq, bq, Wk, bk, Wv, bv, Wo, bo, causal):
            q = jnp.einsum('bsd,hde->bhse', xq, Wq) + bq[None, :, None, :]
            k = jnp.einsum('bsd,hde->bhse', xk, Wk) + bk[None, :, None, :]
            v = jnp.einsum('bsd,hde->bhse', xv, Wv) + bv[None, :, None, :]
            scale = 1.0 / jnp.sqrt(jnp.asarray(HD, q.dtype))
            scores = jnp.einsum('bhqe,bhke->bhqk', q, k) * scale
            if causal:
                mask = jnp.tril(jnp.ones((q.shape[2], k.shape[2]), bool))
                scores = jnp.where(mask, scores, jnp.finfo(scores.dtype).min)
            w = jax.nn.softmax(scores, axis=-1)
            out = jnp.einsum('bhqk,bhke->bhqe', w, v)
            out = out.transpose(0, 2, 1, 3).reshape(out.shape[0], out.shape[2], D)
            return out @ Wo + bo
        h = _mha(x, x, x, Wq1, bq1, Wk1, bk1, Wv1, bv1, Wo1, bo1, causal=True)
        out = _mha(h, encoder_k, encoder_v, Wq2, bq2, Wk2, bk2, Wv2, bv2, Wo2, bo2, causal=False)
        return out

    def _L1_ffn_ref(hidden_states, gate_w1, gate_b1, gate_w2, gate_b2, W1, b1, W2, b2, TW1, Tb1, TW2, Tb2):
        import jax, jax.numpy as jnp
        import numpy as np
        B, S, H, F, E = (8, 256, 128, 512, 8)
        INIT_LAMBDA = 0.2
        x = hidden_states
        h = jax.nn.relu(jnp.einsum('bsh,oh->bso', x, gate_w1) + gate_b1)
        g = jnp.einsum('bso,eo->bse', h, gate_w2) + gate_b2
        g = g.mean(axis=1)
        mW1 = W1 + jnp.einsum('be,efh->bfh', g, TW1)
        mb1 = b1 + g @ Tb1
        mW2 = W2 + jnp.einsum('be,ehf->bhf', g, TW2)
        mb2 = b2 + g @ Tb2
        u = jax.nn.gelu(jnp.einsum('bsh,bfh->bsf', x, mW1) + mb1[:, None, :])
        out = jnp.einsum('bsf,bhf->bsh', u, mW2) + mb2[:, None, :]
        return out
    x = _layernorm(x + _L0_attn_ref(x, L0_attn_Wk, L0_attn_Wq, L0_attn_Wv, L0_attn_Wo, L0_attn_bo), axis=-1)
    x = _layernorm(x + _L0_xattn_ref(x, ctx_1024, L0_xattn_Wq, L0_xattn_Wk, L0_xattn_Wv, L0_xattn_Wo, L0_xattn_bo, mask_BxS2_ik0), axis=-1)
    x = _layernorm(x + _L0_ffn_ref(x, L0_ffn_Wg, L0_ffn_W1, L0_ffn_W2), axis=-1)
    x = _layernorm(x + _L1_attn_ref(x, L1_attn_Wq, L1_attn_bq, L1_attn_Wk, L1_attn_bk, L1_attn_Wv, L1_attn_bv, L1_attn_Wg, L1_attn_bg, L1_attn_gamma), axis=-1)
    x = _layernorm(x + _L1_xattn_ref(x, ctx_1024, ctx_1024, L1_xattn_Wq1, L1_xattn_bq1, L1_xattn_Wk1, L1_xattn_bk1, L1_xattn_Wv1, L1_xattn_bv1, L1_xattn_Wo1, L1_xattn_bo1, L1_xattn_Wq2, L1_xattn_bq2, L1_xattn_Wk2, L1_xattn_bk2, L1_xattn_Wv2, L1_xattn_bv2, L1_xattn_Wo2, L1_xattn_bo2), axis=-1)
    x = _layernorm(x + _L1_ffn_ref(x, L1_ffn_gate_w1, L1_ffn_gate_b1, L1_ffn_gate_w2, L1_ffn_gate_b2, L1_ffn_W1, L1_ffn_b1, L1_ffn_W2, L1_ffn_b2, L1_ffn_TW1, L1_ffn_Tb1, L1_ffn_TW2, L1_ffn_Tb2), axis=-1)
    return x

_drawn_inputs = setup_inputs


def setup_inputs(seed=0):
    import zlib

    import numpy as np

    out = dict(_drawn_inputs(seed))
    spreads = {'L0_attn_bo': (0.0, 0.1),
     'L0_xattn_bo': (0.0, 0.1),
     'L1_attn_bq': (0.0, 0.674),
     'L1_attn_bk': (0.0, 0.554),
     'L1_attn_bv': (0.0, 0.55),
     'L1_attn_bg': (0.0, 0.756),
     'L1_xattn_bq1': (0.0, 2.0),
     'L1_xattn_bk1': (0.0, 2.0),
     'L1_xattn_bv1': (0.0, 0.405),
     'L1_xattn_bo1': (0.0, 0.371),
     'L1_xattn_bq2': (0.0, 0.429),
     'L1_xattn_bk2': (0.0, 2.0),
     'L1_xattn_bv2': (0.0, 0.1),
     'L1_xattn_bo2': (0.0, 0.1),
     'L1_ffn_gate_b1': (0.0, 0.8),
     'L1_ffn_gate_b2': (0.20000000298023224, 0.6)}
    factors = {'L0_ffn_Wg': 5.303,
     'L0_ffn_W1': 5.053,
     'L0_ffn_W2': 4.636,
     'L1_attn_Wq': 2.7,
     'L1_attn_Wk': 3.067,
     'L1_attn_Wv': 2.898,
     'L1_attn_gamma': 8.0,
     'L1_ffn_gate_w1': 8.0,
     'L1_ffn_gate_w2': 8.0,
     'L1_ffn_b1': 8.0,
     'L1_ffn_b2': 2.673,
     'L1_ffn_Tb1': 8.0,
     'L1_ffn_Tb2': 4.686}
    for name, (base, spread) in spreads.items():
        noise = np.random.default_rng([zlib.crc32(name.encode()), seed]).standard_normal(out[name].shape)
        drawn = base * np.exp(spread * noise) if base else spread * noise
        out[name] = jnp.asarray(drawn.astype(out[name].dtype))
    for name, factor in factors.items():
        out[name] = (out[name] * factor).astype(out[name].dtype)
    return out
```

```python
from contextlib import ExitStack

import numpy as np
import concourse.bass as bass
from concourse import mybir

ALU = mybir.AluOpType
ACT = mybir.ActivationFunctionType
AX = mybir.AxisListType
F32 = mybir.dt.float32
I32 = mybir.dt.int32
U32 = mybir.dt.uint32

B, SEQ, D, H = 32, 64, 128, 16
HD = D // H
GB = 4
GT = GB * SEQ
TT = GT // 128
GROUPS = B // GB
E0, HID0 = 8, 256
E1, HID1 = 8, 512
FT = HID1 // 128
ROOT8 = float(np.sqrt(np.float32(HD)))
SCALE = 1.0 / ROOT8
EPS = 1e-5
GELU_A, GELU_C = 0.044715, float(np.sqrt(2.0 / np.pi))
MINUS = -1e30
MASKED = ("a0", "c0", "s1")
ROUTE_STEPS = 10

SQUARES = ["a0q", "a0k", "a0v", "a0o", "c0q", "c0k", "c0v", "c0o", "r1q", "r1k", "r1v", "r1g",
           "s1q", "s1k", "s1v", "s1o", "c1q", "c1k", "c1v", "c1o", "f1g"]
N_SQ0 = 8
CONSTS = {"ident": 128, "causal": 512, "jmask": 4, "ones": 64, "iota": 8, "neghalf": 2}
CONSTS1 = {"cos": 64, "sin": 64, "diff": 512, "id32": 32, "sign": 1}
COLS = {"bq_r": 1, "bk_r": 1, "bqp_r": 1, "bkp_r": 1, "bq_s": 1, "bk_s": 1, "bo_s": 1, "bq_c": 1,
        "bk_c": 1, "gb1": 1, "b1": 4, "gb2": 2, "gamma": 4}
ROWS = {"bo_a": 128, "bo_c0": 128, "bg_r": 128, "bo_c1": 128, "b2": 128, "bv_r": 128, "bv_s": 128,
        "bv_c": 128}


def places(widths):
    at, out = 0, {}
    for name, w in widths.items():
        out[name] = (at, at + w)
        at += w
    return out, at


def attention(l, last):
    o = [("proj", l, 0), ("projv", l, 0), ("qk", l, 0), ("qk", l, 1), ("tp", l, 0)]
    if l == "r1":
        o.insert(2, ("gate", l, 0))
    o += [("qk", l, 2), ("pv", l, 0), ("tp", l, 1), ("qk", l, 3), ("pv", l, 1), ("norm", l, 0),
          ("tp", l, 2), ("pv", l, 2), ("tp", l, 3), ("pv", l, 3), ("norm", l, 1), ("oproj", l, 0)]
    if l == "s1":
        return o
    o += [("ln1", l, 0), ("ln2", l, 0), ("xt", l, 0)]
    return o + ([] if l == "c0" else [("xb", l, 0)])


def experts():
    o = [("logit", "m0", 0), ("w1", "m0", 0), ("route", "m0", 0), ("w1", "m0", 1)]
    for e in range(E0):
        o.append(("w2", "m0", e))
        if e + 2 < E0:
            o.append(("w1", "m0", e + 2))
    return o + [("ln1", "m0", 0), ("ln2", "m0", 0), ("xt", "m0", 0)]


def feedforward():
    f = "f1"
    return [("g1", f, 0), ("gcol", f, 0), ("mb", f, 0), ("gen1", f, 0), ("gen1", f, 1), ("gen2", f, 0),
            ("u", f, 0), ("gen2", f, 1), ("gen1", f, 2), ("ut", f, 0), ("gen1", f, 3), ("gen2", f, 2),
            ("u", f, 1), ("gelu", f, 0), ("gen2", f, 3), ("act", f, 0), ("ut", f, 1), ("out", f, 0), ("gelu", f, 1),
            ("act", f, 1), ("out", f, 1), ("ln1", f, 0), ("ln2", f, 0), ("store", f, 0)]


FIRST = [("load", "in", 0), ("xb", "in", 0), ("mask", "in", 0)] + attention("a0", 0) + attention("c0", 0) + experts()
SECOND = [("load", "in", 0)] + attention("r1", 0) + attention("s1", 0) + attention("c1", 0) + feedforward()
COST = {"proj": 90, "projv": 110, "gate": 45, "qk": 90, "tp": 50, "pv": 110, "norm": 1, "oproj": 45,
        "ln1": 1, "ln2": 60, "xt": 30, "logit": 20, "w1": 90, "w2": 90, "route": 1, "g1": 45,
        "gcol": 20, "mb": 60, "gen1": 190, "gen2": 190, "u": 90, "ut": 50, "gelu": 1, "out": 140,
        "store": 1, "act": 1, "xb": 1, "mask": 1, "load": 1}


def merged(first, second):
    def paced(stream, stages):
        whole = sum(COST[s[0]] for s in stages)
        done, out = 0, []
        for s in stages:
            out.append((done / whole, stream, s))
            done += COST[s[0]]
        return out
    both = sorted(paced(0, first) + paced(1, second), key=lambda x: (x[0], x[1]))
    return [(stream, stage) for _, stream, stage in both]


def signals(stage):
    s, l, b = stage
    if s == "load":
        return {"loaded_x": 16, "loaded_xT": 16, "loaded_mask": 16, "loaded_ctx": 16}
    if s == "xb":
        return {"xb": 1}
    if s == "mask":
        return {"keep": 2}
    if s == "proj":
        return {"r1": {"full_M": 1, "free_M": 1, "full_T": 1, "free_T": 1, "rope": 1, "blocks": 2},
                "c0": {"full_M": 1, "free_M": 1, "full_T": 1, "free_T": 1, "blocks": 1}}.get(
                    l, {"full_M": 1, "free_M": 1, "full_T": 1, "free_T": 1})
    if s == "gate":
        return {"full_Y": 1, "free_Y": 1, "gtanh": 1, "gate": 1}
    if s == "qk":
        return {"full_S": 1, "free_S": 1} | ({} if l == "r1" else {"rowmax": 1, "p": 1}) | (
            {"shifted": 1} if l in MASKED else {})
    if s == "pv":
        return {"full_Y": 1} if b % 2 else {}
    if s == "norm":
        return {"free_Y": 1} | ({} if l == "r1" else {"recip": 1})
    if s == "oproj":
        return {"full_M": 1, "free_M": 1} | ({"resid": 1} if l == "r1" else {})
    if s == "ln1":
        return {"stats": 1, "moments": 1, "vareps": 1, "rstd": 1}
    if s == "ln2":
        return {"x": 1}
    if s == "logit":
        return {"full_M": 1, "lmax": 1, "free_M": 1, "lexp": 1}
    if s == "route":
        return {"routed": ROUTE_STEPS, "comb": 1}
    if s == "w1":
        return {f"full_{'ST'[b % 2]}": 1, f"free_{'ST'[b % 2]}": 1, "hid": 1}
    if s == "w2":
        return {f"full_{'YM'[b % 2]}": 1, f"free_{'YM'[b % 2]}": 1}
    if s == "g1":
        return {"full_M": 1, "free_M": 1, "hmean": 1}
    if s == "gcol":
        return {"full_M": 1, "free_M": 1, "gdiag": 1}
    if s == "gelu":
        return {"zsq": 1, "zcub": 1, "tanh": 1}
    if s == "act":
        return {"act": 1}
    if s == "store":
        return {"stored": 16}
    bank = {"projv": "M", "xt": "M", "tp": "T", "mb": "M", "gen1": "S", "gen2": "T", "u": "M", "ut": "Y", "out": "M"}[s]
    return {"full_" + bank: 1, "free_" + bank: 1}


class Tally:

    def __init__(self, stages):
        self.stages, self.total, self.events = stages, {}, {}
        for stage in stages:
            for name, k in signals(stage).items():
                self.total[name] = self.total.get(name, 0) + k
                self.events.setdefault(name, []).append((stage, self.total[name]))

    def after(self, name, stage):
        return dict(self.events[name])[stage]

    def previous(self, name, stage):
        ev = self.events[name]
        i = [s for s, _ in ev].index(stage) - 1
        return (0, ev[i][1]) if i >= 0 else (1, ev[-1][1])

    def same_kind(self, stage, lag):
        kind = [s for s in self.stages if s[0] == stage[0]]
        i = kind.index(stage) - lag
        return (0, kind[i]) if i >= 0 else (1, kind[i])


def decoder_kernel(nc, x, xT, ctxT, mask, squares, consts, consts1, cols, rows, moe_g, moe_w1, moe_w2,
                   gw2r, ff_w1, ff_w2, ff_tw1, ff_tw2, ff_tb1, ff_tb2, out):
    c_at, c_n = places(CONSTS)
    c1_at, c1_n = places(CONSTS1)
    v_at, v_n = places(COLS)
    r_at, r_n = places(ROWS)

    x_d = x.rearrange("(g tt p) d -> g p tt d", tt=TT, p=128)
    xT_d = xT.rearrange("d (g t) -> g d t", t=GT)
    ctxT_d = ctxT.rearrange("d (g t) -> g d t", t=GT)
    mask_d = mask.rearrange("(g b) s -> g (b s)", b=GB)
    out_d = out.rearrange("(g tt p) d -> g p tt d", tt=TT, p=128)

    with ExitStack() as ctx:
        def sb(name, shape, dt=F32):
            return ctx.enter_context(nc.sbuf_tensor(name, shape, dt))

        def semaphore(name):
            return ctx.enter_context(nc.semaphore(name))

        sq = sb("sq", [128, len(SQUARES), 128])
        con = sb("con", [128, c_n])
        con1 = sb("con1", [128, c1_n])
        col = sb("col", [128, v_n])
        row = sb("row", [128, r_n])
        wg_sb = sb("wg_sb", [128, E0])
        w1_sb = sb("w1_sb", [128, E0, HID0])
        w2_sb = sb("w2_sb", [128, 2 * E0, D])
        gw2_sb = sb("gw2_sb", [128, 2, 128])
        base1 = sb("base1", [128, HID1])
        base2 = sb("base2", [128, HID1])
        tw1_sb = sb("tw1_sb", [128, 4, 2, HID1])
        tw2_sb = sb("tw2_sb", [128, 4, 2, HID1])
        tb1_sb = sb("tb1_sb", [128, 2, HID1])
        tb2_sb = sb("tb2_sb", [128, 2, D])
        wrot = sb("wrot", [128, 2, 128])
        brot = sb("brot", [128, 2])
        bk_s = sb("bk_s", [128, 4])
        bk_c = sb("bk_c", [128, 4])
        decay = sb("decay", [128, 512])
        dtmp = sb("dtmp", [128, 4, 4])
        half2 = sb("half2", [128, HID1])

        def W(name):
            return sq[:, SQUARES.index(name), :]

        def C(name):
            a, b = c_at[name]
            return con[:, a:b]

        def C1(name):
            a, b = c1_at[name]
            return con1[:, a:b]

        def V(name, p0=0, p1=128):
            a, b = v_at[name]
            return col[p0:p1, a:b]

        def R(name, p0=0, p1=128, n=128):
            a, _ = r_at[name]
            return row[p0:p1, a:a + n]

        ident = C("ident")

        class Stream:
            pass

        def stream(tag, stages):
            s = Stream()
            s.tag = tag
            s.tally = Tally(stages)
            s.sem = {k: semaphore(f"{tag}_{k}") for k in s.tally.total}
            s.bank = {k: ctx.enter_context(nc.psum_tensor(f"{tag}_{k}", [128, 512], F32)) for k in "MSTY"}
            s.Q = sb(f"{tag}_Q", [128, GB * 2, 4, 32])
            s.K = sb(f"{tag}_K", [128, GB, 4, SEQ])
            s.V = sb(f"{tag}_V", [128, GB * 4, 2, 2, 2, HD])
            s.P = sb(f"{tag}_P", [128, 2, 512])
            s.PT = sb(f"{tag}_PT", [128, 2, 8, 2, 32])
            s.mx = sb(f"{tag}_mx", [128, 2, 8])
            s.rz = sb(f"{tag}_rz", [128, 2, SEQ])
            s.yT = sb(f"{tag}_yT", [128, GT])
            s.r = sb(f"{tag}_r", [128, TT, D])
            s.xb = sb(f"{tag}_xb", [128, TT, D])
            s.x = sb(f"{tag}_x", [128, TT, D])
            s.xT = sb(f"{tag}_xT", [128, GT])
            s.ctxT = sb(f"{tag}_ctxT", [128, GT])
            s.st = sb(f"{tag}_st", [128, TT, 6])
            s.mv = sb(f"{tag}_mv", [128, TT, 2])
            s.ve = sb(f"{tag}_ve", [128, TT])
            s.rstd = sb(f"{tag}_rstd", [128, TT])
            return s

        A = stream("f", FIRST)
        Z = stream("s", SECOND)
        xin = sb("xin", [128, TT, D])
        xinT = sb("xinT", [128, GT])
        hand_x = sb("hand_x", [128, TT, D])
        hand_xT = sb("hand_xT", [128, GT])
        mask_i = sb("mask_i", [128, GT], I32)
        keep = sb("keep", [128, GT])
        mbias = sb("mbias", [128, GB, SEQ])
        kz = sb("kz", [128, GT])
        lg = sb("lg", [128, TT, E0])
        lmx = sb("lmx", [128, TT])
        lsum = sb("lsum", [128, TT])
        lrec = sb("lrec", [128, TT])
        prob = sb("prob", [128, TT, E0])
        top = sb("top", [128, TT, 8])
        topi = sb("topi", [128, TT, 8], U32)
        topf = sb("topf", [128, TT, 2])
        wsum = sb("wsum", [128, TT])
        wrec = sb("wrec", [128, TT])
        wn = sb("wn", [128, TT, 2])
        pick = sb("pick", [128, TT, 2, E0])
        comb = sb("comb", [128, TT, E0])
        hr = sb("hr", [128, 2, 512])
        hid = sb("hid", [128, 2, 512])
        rt1 = sb("rt1", [128, 2, GT])
        rt2 = sb("rt2", [128, 2, GT])
        hT = sb("hT", [128, GT])
        gz = sb("gz", [128, TT, D])
        gt = sb("gt", [128, TT, D])
        gate = sb("gate", [128, TT, D])
        gh = sb("gh", [128, GT])
        hm = sb("hm", [128, GB])
        gcol = sb("gcol", [128, 2, GB])
        gdiag = sb("gdiag", [128, 2, GB, 32])
        mb = sb("mb", [128, TT, FT, 2])
        mW1 = sb("mW1", [128, GB, HID1])
        mW2 = sb("mW2", [128, GB, HID1])
        us = sb("us", [128, 2, HID1])
        z = sb("z", [128, 2, HID1])
        zz = sb("zz", [128, 2, HID1])
        ug = sb("ug", [128, 2, HID1])
        xo = sb("xo", [128, TT, D])
        scratch = sb("scratch", [128, 1])

        loaded0 = semaphore("loaded0")
        loaded1 = semaphore("loaded1")
        loaded2 = semaphore("loaded2")
        zeroed = semaphore("zeroed")
        gexp = semaphore("gexp")
        nsig = semaphore("nsig")
        decayed = semaphore("decayed")
        made = semaphore("made")
        ZEROED = 6
        LOADED0, LOADED1, LOADED2 = 2 * 16, 5 * 16, (8 + 8) * 16

        order = merged(FIRST, SECOND)
        first_only = [(0, s) for s in FIRST]
        second_only = [(1, s) for s in SECOND]
        streams = (A, Z)

        class Due:

            def __init__(self, count):
                self.count = count

        class Counts:

            def __init__(self, n_first, n_second):
                self.n, self.seen = {"f": n_first, "s": n_second}, {}

            def at(self, s, name, count, groups_back=0):
                n, total = self.n[s.tag], s.tally.total[name]
                mark = count - groups_back * total
                if isinstance(n, int) and n < groups_back or self.seen.get((s.tag, name), -10**9) >= mark:
                    return None
                self.seen[s.tag, name] = mark
                return Due(n * total + mark)

            def done(self, s, name, stage):
                return self.at(s, name, s.tally.after(name, stage))

            def step(self, s, name, stage, left):
                return self.at(s, name, s.tally.after(name, stage) - left)

            def before(self, s, name, stage):
                back, count = s.tally.previous(name, stage)
                return self.at(s, name, count, back)

            def same_kind(self, s, name, stage, lag):
                back, other = s.tally.same_kind(stage, lag)
                return self.at(s, name, s.tally.after(name, other), back)

            def last_group(self, s, name, stage):
                return self.at(s, name, s.tally.after(name, stage), 1)

            def handed(self, name, stage):
                return self.n["s"] * A.tally.total[name] + A.tally.after(name, stage)

        def program(eng, emit, before_experts=None, before_second=None):
            cut = [i for i, s in enumerate(first_only) if s[1][1] == "c0"][0]
            w = Counts(0, None)
            emit(first_only[:cut], w)
            if before_experts:
                before_experts()
            emit(first_only[cut:], w)
            if before_second:
                before_second()
            emit(order, Counts(1, 0))
            with eng.Fori(1, GROUPS - 1) as t:
                emit(order, Counts(t + 1, t))
            emit(second_only, Counts(None, GROUPS - 1))

        block = ctx.enter_context(nc.Block())

        @block.sync
        def _(sp):
            def load_first(n, w):
                if due := w.last_group(A, "xb", ("xb", "in", 0)):
                    sp.wait_ge(A.sem["xb"], due.count)
                sp.dma_start(xin[:, :, :], x_d[n]).then_inc(A.sem["loaded_x"], 16)
                if due := w.last_group(A, "full_M", ("projv", "a0", 0)):
                    sp.wait_ge(A.sem["full_M"], due.count)
                sp.dma_start(xinT[:, :], xT_d[n]).then_inc(A.sem["loaded_xT"], 16)
                if due := w.last_group(A, "keep", ("mask", "in", 0)):
                    sp.wait_ge(A.sem["keep"], due.count)
                sp.dma_start(mask_i[:, :], mask_d[n].partition_broadcast(128)).then_inc(A.sem["loaded_mask"], 16)
                if due := w.last_group(A, "full_M", ("projv", "c0", 0)):
                    sp.wait_ge(A.sem["full_M"], due.count)
                sp.dma_start(A.ctxT[:, :], ctxT_d[n]).then_inc(A.sem["loaded_ctx"], 16)

            def load_second(n, w):
                if due := w.last_group(Z, "full_M", ("projv", "c1", 0)):
                    sp.wait_ge(Z.sem["full_M"], due.count)
                sp.dma_start(Z.ctxT[:, :], ctxT_d[n]).then_inc(Z.sem["loaded_ctx"], 16)

            sp.dma_start(sq[:, 0:4, :], squares[:, 0:4, :]).then_inc(loaded0, 16)
            sp.dma_start(con[:, :], consts).then_inc(loaded0, 16)
            load_first(0, Counts(0, None))
            sp.dma_start(row[:, :], rows.partition_broadcast(128)).then_inc(loaded1, 16)
            sp.dma_start(sq[:, 4:8, :], squares[:, 4:8, :]).then_inc(loaded1, 16)
            sp.dma_start(wg_sb[:, :], moe_g).then_inc(loaded1, 16)
            sp.dma_start(w1_sb[:, :, :], moe_w1).then_inc(loaded1, 16)
            sp.dma_start(w2_sb[:, :, :], moe_w2).then_inc(loaded1, 16)
            sp.dma_start(sq[:, N_SQ0:, :], squares[:, N_SQ0:, :]).then_inc(loaded2, 16)
            sp.dma_start(con1[:, :], consts1).then_inc(loaded2, 16)
            sp.dma_start(col[:, :], cols).then_inc(loaded2, 16)
            sp.dma_start(gw2_sb[:, :, :], gw2r).then_inc(loaded2, 16)
            sp.dma_start(base1[:, :], ff_w1).then_inc(loaded2, 16)
            sp.dma_start(base2[:, :], ff_w2).then_inc(loaded2, 16)
            sp.dma_start(tw1_sb[:, :, :, :], ff_tw1).then_inc(loaded2, 16)
            sp.dma_start(tw2_sb[:, :, :, :], ff_tw2).then_inc(loaded2, 16)
            sp.wait_ge(zeroed, ZEROED)
            for e in range(4):
                sp.dma_start(tb1_sb[32 * e:32 * e + 1, :, :], ff_tb1[e:e + 1]).then_inc(loaded2, 16)
                sp.dma_start(tb2_sb[32 * e:32 * e + 1, :, :], ff_tb2[e:e + 1]).then_inc(loaded2, 16)
            load_first(1, Counts(1, 0))
            load_second(0, Counts(1, 0))
            with sp.Fori(1, GROUPS - 1) as t:
                w = Counts(t + 1, t)
                load_first(t + 1, w)
                load_second(t, w)
            load_second(GROUPS - 1, Counts(None, GROUPS - 1))

        @block.tensor
        def _(pe):
            mm = nc.tensor.matmul

            def source(s, l):
                return {"a0": xinT, "r1": hand_xT, "c1": hT}.get(l, s.xT)

            def wait_source(s, l, w):
                if l == "a0":
                    if due := w.done(A, "loaded_xT", ("load", "in", 0)):
                        pe.wait_ge(A.sem["loaded_xT"], due.count)
                elif l == "c0":
                    if due := w.done(A, "free_M", ("xt", "a0", 0)):
                        pe.wait_ge(A.sem["free_M"], due.count)
                elif l == "m0":
                    if due := w.done(A, "free_M", ("xt", "c0", 0)):
                        pe.wait_ge(A.sem["free_M"], due.count)
                elif l == "r1":
                    pe.wait_ge(A.sem["free_M"], w.handed("free_M", ("xt", "m0", 0)))
                elif l == "s1":
                    if due := w.done(Z, "free_M", ("xt", "r1", 0)):
                        pe.wait_ge(Z.sem["free_M"], due.count)
                elif l == "c1":
                    if due := w.done(Z, "free_M", ("oproj", "s1", 0)):
                        pe.wait_ge(Z.sem["free_M"], due.count)
                elif l == "f1":
                    if due := w.done(Z, "free_M", ("xt", "c1", 0)):
                        pe.wait_ge(Z.sem["free_M"], due.count)

            def emit(stages, w):
                for who, stage in stages:
                    s = streams[who]
                    name, l, b = stage
                    M, S, T, Y = (s.bank[k] for k in "MSTY")
                    X = source(s, l)
                    if name == "proj":
                        wait_source(s, l, w)
                        kX = X
                        if l in ("c0", "c1"):
                            if due := w.done(s, "loaded_ctx", ("load", "in", 0)):
                                pe.wait_ge(s.sem["loaded_ctx"], due.count)
                            kX = s.ctxT
                        if due := w.before(s, "free_M", stage):
                            pe.wait_ge(s.sem["free_M"], due.count)
                        mq = mm(M[:, 0:GT], W(l + "q"), X[:, :], start=True, stop=True)
                        if l == "r1":
                            mm(M[:, GT:2 * GT], W(l + "k"), kX[:, :], start=True, stop=True).then_inc(s.sem["full_M"], 1)
                            if due := w.before(s, "free_T", stage):
                                pe.wait_ge(s.sem["free_T"], due.count)
                            mm(T[:, 0:GT], wrot[:, 0, :], X[:, :], start=True, stop=True)
                            mm(T[:, GT:2 * GT], wrot[:, 1, :], X[:, :], start=True, stop=True).then_inc(s.sem["full_T"], 1)
                        else:
                            mq.then_inc(s.sem["full_M"], 1)
                            if due := w.before(s, "free_T", stage):
                                pe.wait_ge(s.sem["free_T"], due.count)
                            mm(T[:, 0:GT], W(l + "k"), kX[:, :], start=True, stop=True).then_inc(s.sem["full_T"], 1)
                    elif name == "projv":
                        vX = s.ctxT if l in ("c0", "c1") else X
                        if due := w.before(s, "free_M", stage):
                            pe.wait_ge(s.sem["free_M"], due.count)
                        for q in range(GB):
                            for j2 in range(2):
                                last = mm(M[64 * j2:64 * j2 + 64, 64 * q:64 * q + 64], vX[:, 64 * q:64 * q + 64],
                                          W(l + "v")[:, 64 * j2:64 * j2 + 64], start=True, stop=True)
                        last.then_inc(s.sem["full_M"], 1)
                    elif name == "gate":
                        if due := w.before(s, "free_Y", stage):
                            pe.wait_ge(s.sem["free_Y"], due.count)
                        for t in range(TT):
                            last = mm(Y[:, 128 * t:128 * t + 128], X[:, 128 * t:128 * t + 128], W("r1g"), start=True, stop=True)
                        last.then_inc(s.sem["full_Y"], 1)
                    elif name == "qk":
                        if l != "r1":
                            if due := w.done(s, "free_M", ("proj", l, 0)):
                                pe.wait_ge(s.sem["free_M"], due.count)
                            if due := w.done(s, "free_T", ("proj", l, 0)):
                                pe.wait_ge(s.sem["free_T"], due.count)
                        if l in ("r1", "c0"):
                            if due := w.done(s, "blocks", ("proj", l, 0)):
                                pe.wait_ge(s.sem["blocks"], due.count)
                        if due := w.before(s, "free_S", stage):
                            pe.wait_ge(s.sem["free_S"], due.count)
                        for qh in range(2):
                            last = mm(S[:, 256 * qh:256 * qh + 256], s.Q[:, 2 * b + qh, :, :].rearrange("p g q -> p (g q)"),
                                      s.K[:, b, :, :].rearrange("p j k -> p (j k)"), start=True, stop=True)
                        last.then_inc(s.sem["full_S"], 1)
                    elif name == "tp":
                        if due := w.done(s, "free_S" if l == "r1" else "p", ("qk", l, b)):
                            pe.wait_ge(s.sem["free_S" if l == "r1" else "p"], due.count)
                        if due := w.before(s, "free_T", stage):
                            pe.wait_ge(s.sem["free_T"], due.count)
                        for n in range(4):
                            last = nc.tensor.transpose(T[:, 128 * n:128 * n + 128], s.P[:, b % 2, 128 * n:128 * n + 128], ident)
                        last.then_inc(s.sem["full_T"], 1)
                    elif name == "pv":
                        if due := w.done(s, "free_T", ("tp", l, b)):
                            pe.wait_ge(s.sem["free_T"], due.count)
                        if b == 0:
                            if due := w.done(s, "free_M", ("projv", l, 0)):
                                pe.wait_ge(s.sem["free_M"], due.count)
                        if b % 2 == 0:
                            if due := w.before(s, "free_Y", ("norm", l, b // 2)):
                                pe.wait_ge(s.sem["free_Y"], due.count)
                        for part in range(1 if l == "r1" else 2):
                            c0 = 128 * (b % 2) + 64 * part
                            for jp in range(2):
                                for g in range(4):
                                    lhs = s.V[:, 4 * b + g, jp, :, :, :] if part == 0 else C("ones")[:, 32 * jp:32 * jp + 32]
                                    if part == 0:
                                        lhs = lhs.rearrange("p a b d -> p (a b d)")
                                    last = mm(Y[32 * g:32 * g + 32, c0:c0 + 64], lhs,
                                              s.PT[:, b % 2, 4 * jp + g, :, :].rearrange("p a q -> p (a q)"),
                                              start=(jp == 0), stop=(jp == 1))
                        if b % 2:
                            last.then_inc(s.sem["full_Y"], 1)
                    elif name == "oproj":
                        if due := w.done(s, "free_Y", ("norm", l, 1)):
                            pe.wait_ge(s.sem["free_Y"], due.count)
                        if due := w.before(s, "free_M", stage):
                            pe.wait_ge(s.sem["free_M"], due.count)
                        if l == "s1":
                            last = mm(M[:, 0:GT], W("s1o"), s.yT[:, :], start=True, stop=True)
                        for t in range(0 if l == "s1" else TT):
                            part = slice(128 * t, 128 * t + 128)
                            if l == "r1":
                                last = nc.tensor.transpose(M[:, part], s.yT[:, part], ident)
                            else:
                                last = mm(M[:, part], s.yT[:, part], W(l + "o"), start=True, stop=True)
                        last.then_inc(s.sem["full_M"], 1)
                    elif name == "xt":
                        if due := w.done(s, "x", ("ln2", l, 0)):
                            pe.wait_ge(s.sem["x"], due.count)
                        if due := w.before(s, "free_M", stage):
                            pe.wait_ge(s.sem["free_M"], due.count)
                        xs = hand_x if l == "m0" else s.x
                        for t in range(TT):
                            last = nc.tensor.transpose(M[:, 128 * t:128 * t + 128], xs[:, t, :], ident)
                        last.then_inc(s.sem["full_M"], 1)
                    elif name == "logit":
                        wait_source(s, l, w)
                        if due := w.before(s, "free_M", stage):
                            pe.wait_ge(s.sem["free_M"], due.count)
                        for t in range(TT):
                            last = mm(M[:, E0 * t:E0 * t + E0], X[:, 128 * t:128 * t + 128], wg_sb[:, :], start=True, stop=True)
                        last.then_inc(s.sem["full_M"], 1)
                    elif name == "w1":
                        k = "ST"[b % 2]
                        if due := w.before(s, "free_" + k, stage):
                            pe.wait_ge(s.sem["free_" + k], due.count)
                        for n in range(2):
                            last = mm(s.bank[k][:, GT * n:GT * n + GT], w1_sb[:, b, 128 * n:128 * n + 128], X[:, :], start=True, stop=True)
                        last.then_inc(s.sem["full_" + k], 1)
                    elif name == "w2":
                        k = "YM"[b % 2]
                        if due := w.done(s, "hid", ("w1", l, b)):
                            pe.wait_ge(s.sem["hid"], due.count)
                        if due := w.before(s, "free_" + k, stage):
                            pe.wait_ge(s.sem["free_" + k], due.count)
                        for t in range(TT):
                            for n in range(2):
                                last = mm(s.bank[k][:, 128 * t:128 * t + 128], hid[:, b % 2, GT * n + 128 * t:GT * n + 128 * t + 128],
                                          w2_sb[:, 2 * b + n, :], start=(n == 0), stop=(n == 1))
                        last.then_inc(s.sem["full_" + k], 1)
                    elif name == "g1":
                        wait_source(s, l, w)
                        if due := w.before(s, "free_M", stage):
                            pe.wait_ge(s.sem["free_M"], due.count)
                        mm(M[:, 0:GT], W("f1g"), X[:, :], start=True, stop=True).then_inc(s.sem["full_M"], 1)
                    elif name == "gcol":
                        if due := w.done(s, "hmean", ("g1", l, 0)):
                            pe.wait_ge(s.sem["hmean"], due.count)
                        if due := w.before(s, "free_M", stage):
                            pe.wait_ge(s.sem["free_M"], due.count)
                        for n in range(2):
                            last = mm(M[:, GB * n:GB * n + GB], gw2_sb[:, n, :], hm[:, :], start=True, stop=True)
                        last.then_inc(s.sem["full_M"], 1)
                    elif name == "mb":
                        if due := w.before(s, "free_M", stage):
                            pe.wait_ge(s.sem["free_M"], due.count)
                        for f in range(FT):
                            o = M[:, 0:TT * FT * 2].rearrange("p (t f b) -> p t f b", t=TT, f=FT)[:, :, f, :]
                            for n in range(2):
                                last = mm(o, tb1_sb[:, n, 128 * f:128 * f + 128], gcol[:, n, :].rearrange("p (t b) -> p t b", t=TT),
                                          start=(n == 0), stop=(n == 1))
                        last.then_inc(s.sem["full_M"], 1)
                    elif name in ("gen1", "gen2"):
                        k, tw = ("S", tw1_sb) if name == "gen1" else ("T", tw2_sb)
                        if due := w.done(s, "gdiag", ("gcol", l, 0)):
                            pe.wait_ge(s.sem["gdiag"], due.count)
                        if due := w.before(s, "free_" + k, stage):
                            pe.wait_ge(s.sem["free_" + k], due.count)
                        for n in range(2):
                            for c in range(4):
                                last = mm(s.bank[k][32 * c:32 * c + 32, :], gdiag[:, n, b, :], tw[:, c, n, :], start=(n == 0), stop=(n == 1))
                        last.then_inc(s.sem["full_" + k], 1)
                    elif name == "u":
                        if due := w.done(s, "free_S", ("gen1", l, 2 * b + 1)):
                            pe.wait_ge(s.sem["free_S"], due.count)
                        if due := w.before(s, "free_M", stage):
                            pe.wait_ge(s.sem["free_M"], due.count)
                        for n in range(2):
                            q = 2 * b + n
                            last = mm(M[64 * n:64 * n + 64, :], X[:, 64 * q:64 * q + 64], mW1[:, q, :], start=True, stop=True)
                        last.then_inc(s.sem["full_M"], 1)
                    elif name == "ut":
                        if due := w.done(s, "free_M", ("u", l, b)):
                            pe.wait_ge(s.sem["free_M"], due.count)
                        if due := w.before(s, "free_Y", stage):
                            pe.wait_ge(s.sem["free_Y"], due.count)
                        for f in range(FT):
                            last = nc.tensor.transpose(Y[:, 128 * f:128 * f + 128], us[:, b, 128 * f:128 * f + 128], ident)
                        last.then_inc(s.sem["full_Y"], 1)
                    elif name == "out":
                        if due := w.done(s, "act", ("act", l, b)):
                            pe.wait_ge(s.sem["act"], due.count)
                        if due := w.done(s, "free_T", ("gen2", l, 2 * b + 1)):
                            pe.wait_ge(s.sem["free_T"], due.count)
                        if due := w.before(s, "free_M", stage):
                            pe.wait_ge(s.sem["free_M"], due.count)
                        for n in range(2):
                            q = 2 * b + n
                            o = M[64 * n:64 * n + 64, 0:D]
                            for f in range(FT):
                                mm(o, ug[:, b, 128 * f + 64 * n:128 * f + 64 * n + 64], mW2[:, q, 128 * f:128 * f + 128], start=(f == 0), stop=False)
                            for m in range(2):
                                last = mm(o, gcol[:, m, q:q + 1].to_broadcast([128, 64]), tb2_sb[:, m, :], start=False, stop=(m == 1))
                        last.then_inc(s.sem["full_M"], 1)

            def before_second():
                pe.wait_ge(loaded2, LOADED2)
                pe.wait_ge(made, 1)

            pe.wait_ge(loaded0, LOADED0)
            pe.wait_ge(zeroed, ZEROED)
            program(pe, emit, lambda: pe.wait_ge(loaded1, LOADED1), before_second)

        @block.scalar
        def _(act):
            fn = nc.scalar.activation

            def emit(stages, w):
                for who, stage in stages:
                    s = streams[who]
                    name, l, b = stage
                    M, S, T, Y = (s.bank[k] for k in "MSTY")
                    if name == "proj":
                        if l == "r1":
                            if due := w.done(s, "rope", stage):
                                act.wait_ge(s.sem["rope"], due.count)
                            src = rt1[:, 0, :]
                        else:
                            if due := w.done(s, "full_M", stage):
                                act.wait_ge(s.sem["full_M"], due.count)
                            src = M[:, 0:GT]
                        for g in range(4):
                            p = slice(32 * g, 32 * g + 32)
                            i = src[p, :].rearrange("p (a q) -> p a q", q=32)
                            o = s.Q[p, :, g, :]
                            if l in ("s1", "c1"):
                                last = fn(o, i, ACT.Identity, bias=V("bq_" + l[0], 32 * g, 32 * g + 32))
                            else:
                                last = fn(o, i, ACT.Copy)
                        last.then_inc(s.sem["blocks" if l == "r1" else "free_M"], 1)
                    elif name == "gate":
                        if due := w.done(s, "free_Y", stage):
                            act.wait_ge(s.sem["free_Y"], due.count)
                        fn(gt[:, :, :], gz[:, :, :], ACT.Tanh, scale=0.5).then_inc(s.sem["gtanh"], 1)
                    elif name == "qk" and l != "r1":
                        if due := w.done(s, "free_S" if l == "c1" else "shifted", stage):
                            act.wait_ge(s.sem["free_S" if l == "c1" else "shifted"], due.count)
                        fn(s.P[:, b % 2, :], s.P[:, b % 2, :], ACT.Exp, scale=SCALE).then_inc(s.sem["p"], 1)
                    elif name == "tp":
                        if due := w.done(s, "full_T", stage):
                            act.wait_ge(s.sem["full_T"], due.count)
                        i = T[:, :].rearrange("p (a g q) -> p a g q", a=2, q=32)
                        o = s.PT[:, b % 2, :, :, :].rearrange("p g a q -> p a g q")
                        fn(o, i, ACT.Copy).then_inc(s.sem["free_T"], 1)
                    elif name == "norm" and l == "r1":
                        if due := w.done(s, "full_Y", ("pv", l, 2 * b + 1)):
                            act.wait_ge(s.sem["full_Y"], due.count)
                        i = Y[:, 0:256].rearrange("p (b c) -> p b c", b=2)[:, :, 0:64]
                        fn(s.yT[:, 128 * b:128 * b + 128].rearrange("p (b c) -> p b c", b=2), i, ACT.Copy).then_inc(s.sem["free_Y"], 1)
                    elif name == "oproj" and l == "s1":
                        if due := w.done(s, "full_M", stage):
                            act.wait_ge(s.sem["full_M"], due.count)
                        fn(hT[:, :], M[:, 0:GT], ACT.Identity, bias=V("bo_s")).then_inc(s.sem["free_M"], 1)
                    elif name == "xt":
                        if due := w.done(s, "full_M", stage):
                            act.wait_ge(s.sem["full_M"], due.count)
                        if l == "m0" and w.n["s"] is not None:
                            if due := w.done(Z, "full_M", ("projv", "r1", 0)):
                                act.wait_ge(Z.sem["full_M"], due.count)
                            if due := w.done(Z, "full_Y", ("gate", "r1", 0)):
                                act.wait_ge(Z.sem["full_Y"], due.count)
                        dst = hand_xT if l == "m0" else s.xT
                        fn(dst[:, :], M[:, 0:GT], ACT.Copy).then_inc(s.sem["free_M"], 1)
                    elif name == "logit":
                        if due := w.done(s, "free_M", stage):
                            act.wait_ge(s.sem["free_M"], due.count)
                        fn(lg[:, :, :], lg[:, :, :], ACT.Exp).then_inc(s.sem["lexp"], 1)
                    elif name == "w1":
                        k = "ST"[b % 2]
                        if due := w.done(s, "full_" + k, stage):
                            act.wait_ge(s.sem["full_" + k], due.count)
                        if due := w.same_kind(s, "hid", stage, 2):
                            act.wait_ge(s.sem["hid"], due.count)
                        fn(hr[:, b % 2, :], s.bank[k][:, :], ACT.Relu).then_inc(s.sem["free_" + k], 1)
                    elif name == "g1":
                        if due := w.done(s, "full_M", stage):
                            act.wait_ge(s.sem["full_M"], due.count)
                        fn(gh[:, :], M[:, 0:GT], ACT.Relu, bias=V("gb1")).then_inc(s.sem["free_M"], 1)
                    elif name == "u":
                        if due := w.done(s, "full_M", stage):
                            act.wait_ge(s.sem["full_M"], due.count)
                        fn(us[:, b, :], M[:, :], ACT.Copy).then_inc(s.sem["free_M"], 1)
                    elif name == "gelu":
                        if due := w.done(s, "zcub", stage):
                            act.wait_ge(s.sem["zcub"], due.count)
                        fn(zz[:, b, :], zz[:, b, :], ACT.Tanh, scale=GELU_A * GELU_C).then_inc(s.sem["tanh"], 1)
                    elif name == "store":
                        if due := w.done(s, "x", ("ln2", l, 0)):
                            act.wait_ge(s.sem["x"], due.count)
                        act.dma_start(out_d[w.n["s"]], xo[:, :, :]).then_inc(s.sem["stored"], 16)

            def before_second():
                act.wait_ge(loaded2, LOADED2)
                fn(dtmp[:, 0, :], V("gamma"), ACT.Exp, scale=-1.0).then_inc(gexp, 1)
                act.wait_ge(nsig, 3)
                for j in range(4):
                    dst = decay[:, :].rearrange("p (a j k) -> p a j k", a=2, j=4)[:, :, j, :]
                    src = C1("diff").rearrange("p (a j k) -> p a j k", a=2, j=4)[:, :, j, :]
                    last = fn(dst, src, ACT.Exp, scale=dtmp[:, 2, j:j + 1])
                last.then_inc(decayed, 1)

            act.wait_ge(zeroed, ZEROED)
            program(act, emit, None, before_second)
            act.wait_ge(Z.sem["stored"], 16 * GROUPS)

        @block.vector
        def _(dve):
            v = nc.vector
            tt = v.tensor_tensor
            ts = v.tensor_scalar
            stt = v.scalar_tensor_tensor

            def take_wait():
                v.memset(scratch[:, :], 0.0)

            def emit(stages, w):
                for who, stage in stages:
                    s = streams[who]
                    name, l, b = stage
                    M, S, T, Y = (s.bank[k] for k in "MSTY")
                    P = s.P[:, b % 2, :]
                    if name == "mask":
                        if due := w.done(s, "loaded_mask", ("load", "in", 0)):
                            dve.wait_ge(s.sem["loaded_mask"], due.count)
                        ts(keep[:, :], mask_i[:, :], 0, None, ALU.not_equal).then_inc(s.sem["keep"], 1)
                        ts(mbias[:, :, :].rearrange("p b k -> p (b k)"), mask_i[:, :], 0, -1e9 * ROOT8, ALU.is_equal, ALU.mult)\
                            .then_inc(s.sem["keep"], 1)
                    elif name == "proj":
                        src = T[:, 0:GT]
                        if due := w.done(s, "full_M" if l == "r1" else "full_T", stage):
                            dve.wait_ge(s.sem["full_M" if l == "r1" else "full_T"], due.count)
                        if l == "r1":
                            cos = C1("cos").unsqueeze(1).to_broadcast([128, GB, SEQ])
                            sin = C1("sin").unsqueeze(1).to_broadcast([128, GB, SEQ])
                            for n, bias in ((0, "bq_r"), (1, "bk_r")):
                                last = stt(out=rt1[:, n, :].rearrange("p (b s) -> p b s", b=GB),
                                           in0=M[:, GT * n:GT * n + GT].rearrange("p (b s) -> p b s", b=GB),
                                           scalar=V(bias), in1=cos, op0=ALU.add, op1=ALU.mult)
                            last.then_inc(s.sem["free_M"], 1)
                            if due := w.done(s, "full_T", stage):
                                dve.wait_ge(s.sem["full_T"], due.count)
                            for n in range(2):
                                last = stt(out=rt2[:, n, :].rearrange("p (b s) -> p b s", b=GB),
                                           in0=T[:, GT * n:GT * n + GT].rearrange("p (b s) -> p b s", b=GB),
                                           scalar=brot[:, n:n + 1], in1=sin, op0=ALU.add, op1=ALU.mult)
                            last.then_inc(s.sem["free_T"], 1)
                            if due := w.done(s, "rope", stage):
                                dve.wait_ge(s.sem["rope"], due.count)
                            src = rt1[:, 1, :]
                        elif l == "c0":
                            if due := w.done(s, "keep", ("mask", "in", 0)):
                                dve.wait_ge(s.sem["keep"], due.count)
                            tt(kz[:, :], src, keep[:, :], ALU.mult).then_inc(s.sem["free_T"], 1)
                            if due := w.done(s, "free_T", stage):
                                dve.wait_ge(s.sem["free_T"], due.count)
                            src = kz[:, :]
                        bias = {"s1": bk_s, "c1": bk_c}.get(l)
                        for j in range(4):
                            last = ts(s.K[:, :, j, :], src.rearrange("p (b k) -> p b k", b=GB), C("jmask")[:, j:j + 1],
                                      None if bias is None else bias[:, j:j + 1], ALU.mult, *([] if bias is None else [ALU.add]))
                        last.then_inc(s.sem["blocks" if l in ("r1", "c0") else "free_T"], 1)
                    elif name == "projv":
                        if due := w.done(s, "full_M", stage):
                            dve.wait_ge(s.sem["full_M"], due.count)
                        for j2 in range(2):
                            p = slice(64 * j2, 64 * j2 + 64)
                            i = M[p, 0:GT].rearrange("p (m a d) -> p m a d", a=2, d=HD)
                            o = s.V[p, :, :, :, :, :].rearrange("p m a b c d -> p m (a b) c d")[:, :, 0:4:3, j2, :]
                            if l in ("r1", "s1", "c1"):
                                bv = r_at["bv_" + l[0]][0] + 64 * j2
                                rowv = row[p, bv:bv + 64].unsqueeze(1).to_broadcast([64, GB, 64])
                                for jp in range(2):
                                    last = tt(o[:, :, jp, :].rearrange("p (b g) d -> p b g d", b=GB),
                                              i[:, :, jp, :].rearrange("p (b g) d -> p b g d", b=GB),
                                              rowv.rearrange("p b (g a d) -> p b g a d", a=2, d=HD)[:, :, :, jp, :], ALU.add)
                            else:
                                last = v.tensor_copy(o, i)
                        last.then_inc(s.sem["free_M"], 1)
                    elif name == "gate":
                        if due := w.done(s, "full_Y", stage):
                            dve.wait_ge(s.sem["full_Y"], due.count)
                        tt(gz[:, :, :], Y[:, 0:GT].rearrange("p (t d) -> p t d", t=TT),
                           R("bg_r").unsqueeze(1).to_broadcast([128, TT, D]), ALU.add).then_inc(s.sem["free_Y"], 1)
                        if due := w.done(s, "gtanh", stage):
                            dve.wait_ge(s.sem["gtanh"], due.count)
                        stt(out=gate[:, :, :], in0=gt[:, :, :], scalar=1.0, in1=gz[:, :, :], op0=ALU.add, op1=ALU.mult)\
                            .then_inc(s.sem["gate"], 1)
                    elif name == "qk":
                        if due := w.done(s, "full_S", stage):
                            dve.wait_ge(s.sem["full_S"], due.count)
                        if due := w.same_kind(s, "full_T", ("tp", l, b), 2):
                            dve.wait_ge(s.sem["full_T"], due.count)
                        mx = s.mx[:, b % 2, :]
                        rows8 = "p (a k) -> p a k"
                        if l == "r1":
                            tt(P, S[:, :], decay[:, :], ALU.mult).then_inc(s.sem["free_S"], 1)
                            continue
                        if l == "c1":
                            v.tensor_reduce(mx, S[:, :].rearrange(rows8, k=SEQ), AX.X, ALU.max).then_inc(s.sem["rowmax"], 1)
                            if due := w.done(s, "rowmax", stage):
                                dve.wait_ge(s.sem["rowmax"], due.count)
                            tt(P.rearrange(rows8, k=SEQ), S[:, :].rearrange(rows8, k=SEQ), mx.unsqueeze(2).to_broadcast([128, 8, SEQ]),
                               ALU.subtract).then_inc(s.sem["free_S"], 1)
                            continue
                        if l == "c0":
                            tt(P.rearrange(rows8, k=SEQ), S[:, :].rearrange(rows8, k=SEQ),
                               mbias[:, b, :].unsqueeze(1).to_broadcast([128, 8, SEQ]), ALU.add).then_inc(s.sem["free_S"], 1)
                        else:
                            tt(P, S[:, :], C("causal"), ALU.add).then_inc(s.sem["free_S"], 1)
                        if due := w.done(s, "free_S", stage):
                            dve.wait_ge(s.sem["free_S"], due.count)
                        v.tensor_reduce(mx, P.rearrange(rows8, k=SEQ), AX.X, ALU.max).then_inc(s.sem["rowmax"], 1)
                    elif name == "norm" and l != "r1":
                        if due := w.done(s, "full_Y", ("pv", l, 2 * b + 1)):
                            dve.wait_ge(s.sem["full_Y"], due.count)
                        both = Y[:, 0:256].rearrange("p (b c q) -> p b c q", b=2, c=2)
                        v.reciprocal(s.rz[:, :, :], both[:, :, 1, :]).then_inc(s.sem["recip"], 1)
                        if due := w.done(s, "recip", stage):
                            dve.wait_ge(s.sem["recip"], due.count)
                        tt(s.yT[:, 128 * b:128 * b + 128].rearrange("p (b q) -> p b q", b=2), both[:, :, 0, :], s.rz[:, :, :], ALU.mult)\
                            .then_inc(s.sem["free_Y"], 1)
                    elif name == "oproj" and l != "s1":
                        if due := w.done(s, "full_M", stage):
                            dve.wait_ge(s.sem["full_M"], due.count)
                        new = M[:, 0:GT].rearrange("p (t d) -> p t d", t=TT)
                        if l == "r1":
                            if due := w.done(s, "gate", ("gate", l, 0)):
                                dve.wait_ge(s.sem["gate"], due.count)
                            stt(out=s.r[:, :, :], in0=new, scalar=0.5, in1=gate[:, :, :], op0=ALU.mult, op1=ALU.mult)\
                                .then_inc(s.sem["free_M"], 1)
                            if due := w.done(s, "free_M", stage):
                                dve.wait_ge(s.sem["free_M"], due.count)
                            dve.wait_ge(A.sem["x"], w.handed("x", ("ln2", "m0", 0)))
                            tt(s.r[:, :, :], s.r[:, :, :], hand_x[:, :, :], ALU.add).then_inc(s.sem["resid"], 1)
                        else:
                            if due := w.done(s, "xb", ("xb", {"a0": "in", "c0": "a0", "c1": "r1"}[l], 0)):
                                dve.wait_ge(s.sem["xb"], due.count)
                            tt(s.r[:, :, :], new, s.xb[:, :, :], ALU.add).then_inc(s.sem["free_M"], 1)
                    elif name == "ln1":
                        if l == "r1":
                            if due := w.done(s, "resid", ("oproj", l, 0)):
                                dve.wait_ge(s.sem["resid"], due.count)
                        elif l == "m0":
                            if due := w.done(s, "free_M", ("w2", l, E0 - 1)):
                                dve.wait_ge(s.sem["free_M"], due.count)
                        elif l == "f1":
                            if due := w.done(s, "free_M", ("out", l, 1)):
                                dve.wait_ge(s.sem["free_M"], due.count)
                        else:
                            if due := w.done(s, "free_M", ("oproj", l, 0)):
                                dve.wait_ge(s.sem["free_M"], due.count)
                        for t in range(TT):
                            last = v.bn_stats(s.st[:, t, :], s.r[:, t, :])
                        last.then_inc(s.sem["stats"], 1)
                        if due := w.done(s, "stats", stage):
                            dve.wait_ge(s.sem["stats"], due.count)
                        take_wait()
                        for t in range(TT):
                            last = v.bn_aggr(s.mv[:, t, :], s.st[:, t, :])
                        last.then_inc(s.sem["moments"], 1)
                        if due := w.done(s, "moments", stage):
                            dve.wait_ge(s.sem["moments"], due.count)
                        ts(s.ve[:, :], s.mv[:, :, 1], EPS, None, ALU.add).then_inc(s.sem["vareps"], 1)
                    elif name == "ln2":
                        if due := w.done(s, "rstd", ("ln1", l, 0)):
                            dve.wait_ge(s.sem["rstd"], due.count)
                        if l == "f1":
                            if due := w.last_group(s, "stored", ("store", l, 0)):
                                dve.wait_ge(s.sem["stored"], due.count)
                        dst = {"m0": hand_x, "f1": xo}.get(l, s.x)
                        for t in range(TT):
                            last = ts(dst[:, t, :], s.r[:, t, :], s.mv[:, t, 0:1], s.rstd[:, t:t + 1], ALU.subtract, ALU.mult)
                        last.then_inc(s.sem["x"], 1)
                    elif name == "logit":
                        if due := w.done(s, "full_M", stage):
                            dve.wait_ge(s.sem["full_M"], due.count)
                        i = M[:, 0:TT * E0].rearrange("p (t e) -> p t e", t=TT)
                        v.tensor_reduce(lmx[:, :], i, AX.X, ALU.max).then_inc(s.sem["lmax"], 1)
                        if due := w.done(s, "lmax", stage):
                            dve.wait_ge(s.sem["lmax"], due.count)
                        tt(lg[:, :, :], i, lmx[:, :].unsqueeze(2).to_broadcast([128, TT, E0]), ALU.subtract).then_inc(s.sem["free_M"], 1)
                    elif name == "route":
                        step = [0]

                        def then(ins):
                            step[0] += 1
                            ins.then_inc(s.sem["routed"], 1)
                            if due := w.step(s, "routed", stage, ROUTE_STEPS - step[0]):
                                dve.wait_ge(s.sem["routed"], due.count)

                        if due := w.done(s, "lexp", ("logit", l, 0)):
                            dve.wait_ge(s.sem["lexp"], due.count)
                        then(v.tensor_reduce(lsum[:, :], lg[:, :, :], AX.X, ALU.add))
                        then(v.reciprocal(lrec[:, :], lsum[:, :]))
                        then(tt(prob[:, :, :], lg[:, :, :], lrec[:, :].unsqueeze(2).to_broadcast([128, TT, E0]), ALU.mult))
                        take_wait()
                        for t in range(TT):
                            last = v.max(out=top[:, t, :], in_=prob[:, t, :])
                        then(last)
                        take_wait()
                        for t in range(TT):
                            last = v.max_index(topi[:, t, :], top[:, t, :], prob[:, t, :])
                        then(last)
                        v.tensor_copy(topf[:, :, :], topi[:, :, 0:2])
                        then(tt(wsum[:, :], top[:, :, 0], top[:, :, 1], ALU.add))
                        then(ts(wrec[:, :], wsum[:, :], 1e-8, None, ALU.add))
                        then(v.reciprocal(wsum[:, :], wrec[:, :]))
                        then(tt(wn[:, :, :], top[:, :, 0:2], wsum[:, :].unsqueeze(2).to_broadcast([128, TT, 2]), ALU.mult))
                        for t in range(TT):
                            for k in range(2):
                                last = ts(pick[:, t, k, :], C("iota"), topf[:, t, k:k + 1], wn[:, t, k:k + 1], ALU.is_equal, ALU.mult)
                        then(last)
                        tt(comb[:, :, :], pick[:, :, 0, :], pick[:, :, 1, :], ALU.add).then_inc(s.sem["comb"], 1)
                    elif name == "w2":
                        k = "YM"[b % 2]
                        if due := w.done(s, "full_" + k, stage):
                            dve.wait_ge(s.sem["full_" + k], due.count)
                        if due := w.done(s, "comb", ("route", l, 0)):
                            dve.wait_ge(s.sem["comb"], due.count)
                        if b:
                            if due := w.done(s, "free_" + "YM"[1 - b % 2], ("w2", l, b - 1)):
                                dve.wait_ge(s.sem["free_" + "YM"[1 - b % 2]], due.count)
                        else:
                            if due := w.done(s, "x", ("ln2", "c0", 0)):
                                dve.wait_ge(s.sem["x"], due.count)
                        for t in range(TT):
                            last = stt(out=s.r[:, t, :], in0=s.bank[k][:, D * t:D * t + D], scalar=comb[:, t, b:b + 1],
                                       in1=(s.r if b else s.x)[:, t, :], op0=ALU.mult, op1=ALU.add)
                        last.then_inc(s.sem["free_" + k], 1)
                    elif name == "g1":
                        if due := w.done(s, "free_M", stage):
                            dve.wait_ge(s.sem["free_M"], due.count)
                        v.tensor_reduce(hm[:, :], gh[:, :].rearrange("p (b k) -> p b k", k=SEQ), AX.X, ALU.add).then_inc(s.sem["hmean"], 1)
                    elif name == "gcol":
                        if due := w.done(s, "full_M", stage):
                            dve.wait_ge(s.sem["full_M"], due.count)
                        for n in range(2):
                            last = ts(gcol[:, n, :], M[:, GB * n:GB * n + GB], 1.0 / SEQ, V("gb2")[:, n:n + 1], ALU.mult, ALU.add)
                        last.then_inc(s.sem["free_M"], 1)
                    elif name == "mb":
                        if due := w.done(s, "full_M", stage):
                            dve.wait_ge(s.sem["full_M"], due.count)
                        i = M[:, 0:TT * FT * 2].rearrange("p (t f b) -> p t f b", t=TT, f=FT)
                        tt(mb[:, :, :, :], i, V("b1").unsqueeze(1).unsqueeze(3).to_broadcast([128, TT, FT, 2]), ALU.add)\
                            .then_inc(s.sem["free_M"], 1)
                    elif name == "gen1":
                        if due := w.done(s, "full_S", stage):
                            dve.wait_ge(s.sem["full_S"], due.count)
                        tt(mW1[:, b, :], S[:, :], base1[:, :], ALU.add).then_inc(s.sem["free_S"], 1)
                    elif name == "gen2":
                        if due := w.done(s, "full_T", stage):
                            dve.wait_ge(s.sem["full_T"], due.count)
                        stt(out=mW2[:, b, :], in0=T[:, :], scalar=0.5, in1=half2[:, :], op0=ALU.mult, op1=ALU.add)\
                            .then_inc(s.sem["free_T"], 1)
                    elif name == "ut":
                        if due := w.done(s, "full_Y", stage):
                            dve.wait_ge(s.sem["full_Y"], due.count)
                        if due := w.done(s, "free_M", ("mb", l, 0)):
                            dve.wait_ge(s.sem["free_M"], due.count)
                        tt(z[:, b, :].rearrange("p (a k) -> p a k", k=SEQ), Y[:, :].rearrange("p (a k) -> p a k", k=SEQ),
                           mb[:, b, :, :].rearrange("p f b -> p (f b)").unsqueeze(2).to_broadcast([128, 2 * FT, SEQ]), ALU.add)\
                            .then_inc(s.sem["free_Y"], 1)
                    elif name == "gelu":
                        if due := w.done(s, "zsq", stage):
                            dve.wait_ge(s.sem["zsq"], due.count)
                        stt(out=zz[:, b, :], in0=zz[:, b, :], scalar=1.0 / GELU_A, in1=z[:, b, :], op0=ALU.add, op1=ALU.mult)\
                            .then_inc(s.sem["zcub"], 1)
                    elif name == "act":
                        if due := w.done(s, "tanh", ("gelu", l, b)):
                            dve.wait_ge(s.sem["tanh"], due.count)
                        stt(out=ug[:, b, :], in0=zz[:, b, :], scalar=1.0, in1=z[:, b, :], op0=ALU.add, op1=ALU.mult)\
                            .then_inc(s.sem["act"], 1)
                    elif name == "out":
                        if due := w.done(s, "full_M", stage):
                            dve.wait_ge(s.sem["full_M"], due.count)
                        if due := w.done(s, "xb", ("xb", "c1", 0)):
                            dve.wait_ge(s.sem["xb"], due.count)
                        tt(s.r[:, b, :], M[:, 0:D], s.xb[:, b, :], ALU.add).then_inc(s.sem["free_M"], 1)

            def before_second():
                dve.wait_ge(loaded2, LOADED2)
                for n, wname in ((0, "r1q"), (1, "r1k")):
                    pair = W(wname).rearrange("p (i a) -> p i a", a=2)
                    turned = wrot[:, n, :].rearrange("p (i a) -> p i a", a=2)
                    ts(turned[:, :, 0], pair[:, :, 1], -1.0, None, ALU.mult)
                    v.tensor_copy(turned[:, :, 1], pair[:, :, 0])
                for n, bname in ((0, "bqp_r"), (1, "bkp_r")):
                    tt(brot[:, n:n + 1], V(bname), C1("sign"), ALU.mult)
                ts(bk_s[:, :], C("jmask"), V("bk_s"), None, ALU.mult)
                ts(bk_c[:, :], C("jmask"), V("bk_c"), None, ALU.mult)
                ts(half2[:, :], base2[:, :], 0.5, None, ALU.mult)
                dve.wait_ge(gexp, 1)
                ts(dtmp[:, 1, :], dtmp[:, 0, :], 1.0, None, ALU.add).then_inc(nsig, 1)
                dve.wait_ge(nsig, 1)
                v.reciprocal(dtmp[:, 3, :], dtmp[:, 1, :]).then_inc(nsig, 1)
                dve.wait_ge(nsig, 2)
                ts(dtmp[:, 2, :], dtmp[:, 3, :], -1.0, None, ALU.mult).then_inc(nsig, 1)
                dve.wait_ge(decayed, 1)
                ts(decay[:, :], decay[:, :], SCALE, None, ALU.mult).then_inc(made, 1)
                dve.wait_ge(made, 1)

            dve.wait_ge(loaded0, LOADED0)
            dve.wait_ge(zeroed, ZEROED)
            program(dve, emit, lambda: dve.wait_ge(loaded1, LOADED1), before_second)

        @block.gpsimd
        def _(pool):
            tt = nc.gpsimd.tensor_tensor

            def emit(stages, w):
                for who, stage in stages:
                    s = streams[who]
                    name, l, b = stage
                    if name == "xb":
                        if l == "in":
                            if due := w.done(s, "loaded_x", ("load", "in", 0)):
                                pool.wait_ge(s.sem["loaded_x"], due.count)
                            if due := w.last_group(s, "free_M", ("oproj", "c0", 0)):
                                pool.wait_ge(s.sem["free_M"], due.count)
                        else:
                            if due := w.done(s, "x", ("ln2", l, 0)):
                                pool.wait_ge(s.sem["x"], due.count)
                        bias = {"in": "bo_a", "a0": "bo_c0", "r1": "bo_c1", "c1": "b2"}[l]
                        tt(s.xb[:, :, :], (xin if l == "in" else s.x)[:, :, :], R(bias).unsqueeze(1).to_broadcast([128, TT, D]), ALU.add)\
                            .then_inc(s.sem["xb"], 1)
                    elif name == "proj" and l == "r1":
                        if due := w.done(s, "free_M", stage):
                            pool.wait_ge(s.sem["free_M"], due.count)
                        if due := w.done(s, "free_T", stage):
                            pool.wait_ge(s.sem["free_T"], due.count)
                        tt(rt1[:, :, :], rt1[:, :, :], rt2[:, :, :], ALU.add).then_inc(s.sem["rope"], 1)
                    elif name == "qk" and l in MASKED:
                        if due := w.done(s, "rowmax", stage):
                            pool.wait_ge(s.sem["rowmax"], due.count)
                        P = s.P[:, b % 2, :].rearrange("p (a k) -> p a k", k=SEQ)
                        tt(P, P, s.mx[:, b % 2, :].unsqueeze(2).to_broadcast([128, 8, SEQ]), ALU.subtract).then_inc(s.sem["shifted"], 1)
                    elif name == "ln1":
                        if due := w.done(s, "vareps", stage):
                            pool.wait_ge(s.sem["vareps"], due.count)
                        tt(s.rstd[:, :], s.ve[:, :], C("neghalf"), ALU.pow).then_inc(s.sem["rstd"], 1)
                    elif name == "w1":
                        if due := w.done(s, "free_" + "ST"[b % 2], stage):
                            pool.wait_ge(s.sem["free_" + "ST"[b % 2]], due.count)
                        k = "YM"[b % 2]
                        if due := w.same_kind(s, "full_" + k, ("w2", l, b), 2):
                            pool.wait_ge(s.sem["full_" + k], due.count)
                        tt(hid[:, b % 2, :], hr[:, b % 2, :], hr[:, b % 2, :], ALU.mult).then_inc(s.sem["hid"], 1)
                    elif name == "gcol":
                        if due := w.done(s, "free_M", stage):
                            pool.wait_ge(s.sem["free_M"], due.count)
                        o = gdiag[:, :, :, :].rearrange("p n b k -> p (n b) k")
                        tt(o, C1("id32").unsqueeze(1).to_broadcast([128, 2 * GB, 32]),
                           gcol[:, :, :].rearrange("p n b -> p (n b)").unsqueeze(2).to_broadcast([128, 2 * GB, 32]), ALU.mult)\
                            .then_inc(s.sem["gdiag"], 1)
                    elif name == "gelu":
                        if due := w.done(s, "free_Y", ("ut", l, b)):
                            pool.wait_ge(s.sem["free_Y"], due.count)
                        if due := w.same_kind(s, "act", ("act", l, b), 2):
                            pool.wait_ge(s.sem["act"], due.count)
                        tt(zz[:, b, :], z[:, b, :], z[:, b, :], ALU.mult).then_inc(s.sem["zsq"], 1)

            for buf in (A.Q, A.V, Z.Q, Z.V, tb1_sb, tb2_sb):
                nc.gpsimd.memset(buf[:], 0.0).then_inc(zeroed, 1)
            pool.wait_ge(loaded0, LOADED0)
            pool.wait_ge(loaded1, LOADED1)
            program(pool, emit, None, lambda: pool.wait_ge(loaded2, LOADED2))


def _lay_out(i):
    f = lambda a: np.ascontiguousarray(np.asarray(a))

    def parity(w):
        return w.reshape(w.shape[:-1] + (H // 2, 2, HD)).swapaxes(-3, -2).reshape(w.shape)

    heads = lambda w: np.asarray(w).transpose(1, 0, 2).reshape(D, D)
    T = lambda name: np.asarray(i[name]).T
    sq = {"a0q": T("L0_attn_Wq"), "a0k": T("L0_attn_Wk"), "a0v": parity(T("L0_attn_Wv")), "a0o": T("L0_attn_Wo"),
          "c0q": T("L0_xattn_Wq"), "c0k": T("L0_xattn_Wk"), "c0v": parity(T("L0_xattn_Wv")), "c0o": T("L0_xattn_Wo"),
          "r1q": T("L1_attn_Wq"), "r1k": T("L1_attn_Wk"), "r1v": parity(T("L1_attn_Wv")), "r1g": T("L1_attn_Wg"),
          "s1q": heads(i["L1_xattn_Wq1"]), "s1k": heads(i["L1_xattn_Wk1"]), "s1v": parity(heads(i["L1_xattn_Wv1"])),
          "s1o": np.asarray(i["L1_xattn_Wo1"]),
          "c1q": heads(i["L1_xattn_Wq2"]), "c1k": heads(i["L1_xattn_Wk2"]), "c1v": parity(heads(i["L1_xattn_Wv2"])),
          "c1o": np.asarray(i["L1_xattn_Wo2"]), "f1g": T("L1_ffn_gate_w1")}
    p = np.arange(128)
    q = np.arange(2)[None, :, None, None] * 32 + (p % 32)[:, None, None, None]
    k = np.arange(SEQ)[None, None, None, :]
    full = np.zeros((128, 2, 4, SEQ), np.float32)
    ones = np.zeros((128, 2, 2, 2, HD), np.float32)
    for jp in range(2):
        for j2 in range(2):
            ones[64 * j2:64 * j2 + 64, jp, jp, j2] = 1.0
    con = {"ident": np.eye(128), "causal": (full + np.where(k <= q, 0.0, MINUS)).reshape(128, 512),
           "jmask": (p[:, None] // HD) % 4 == np.arange(4)[None, :], "ones": ones.reshape(128, 64),
           "iota": np.broadcast_to(np.arange(8), (128, 8)), "neghalf": np.full((128, 2), -0.5)}
    inv = (1.0 / 10000.0 ** (np.arange(0, HD, 2, dtype=np.float32) / HD)).astype(np.float32)
    ang = (np.arange(SEQ, dtype=np.float32)[None, :] * inv[(p % HD) % (HD // 2)][:, None]).astype(np.float32)
    con1 = {"cos": np.cos(ang), "sin": np.sin(ang), "diff": (full + np.maximum(q - k, 0)).reshape(128, 512),
            "id32": p[:, None] % 32 == np.arange(32)[None, :], "sign": np.where(p % 2 == 0, -1.0, 1.0)[:, None]}
    pack = lambda parts, names: f(np.concatenate([np.asarray(parts[n]).astype(np.float32).reshape(-1, w) for n, w in names.items()], axis=1))
    c = lambda name: np.asarray(i[name]).reshape(-1, 1)
    gb2 = np.asarray(i["L1_ffn_gate_b2"]).reshape(2, 4)
    col = {"bq_r": c("L1_attn_bq"), "bk_r": c("L1_attn_bk"), "bqp_r": c("L1_attn_bq")[p ^ 1], "bkp_r": c("L1_attn_bk")[p ^ 1],
           "bq_s": c("L1_xattn_bq1"), "bk_s": c("L1_xattn_bk1"), "bo_s": c("L1_xattn_bo1"), "bq_c": c("L1_xattn_bq2"),
           "bk_c": c("L1_xattn_bk2"), "gb1": c("L1_ffn_gate_b1"), "b1": np.asarray(i["L1_ffn_b1"]).reshape(FT, 128).T,
           "gb2": gb2.T[p // 32], "gamma": np.asarray(i["L1_attn_gamma"]).reshape(4, 4)[p // 32]}
    r = lambda name: np.asarray(i[name]).reshape(1, -1)
    row = {"bo_a": r("L0_attn_bo"), "bo_c0": r("L0_xattn_bo"), "bg_r": r("L1_attn_bg"), "bo_c1": r("L1_xattn_bo2"),
           "b2": r("L1_ffn_b2"), "bv_r": parity(r("L1_attn_bv")), "bv_s": parity(r("L1_xattn_bv1")), "bv_c": parity(r("L1_xattn_bv2"))}
    same = lambda parts, names: f(np.concatenate([parts[n] for n in names], axis=1))
    x, cx = np.asarray(i["x"]).reshape(-1, D), np.asarray(i["ctx_1024"]).reshape(-1, D)
    tw1 = np.asarray(i["L1_ffn_TW1"]).reshape(2, 4, HID1, 4, 32)
    tw2 = np.asarray(i["L1_ffn_TW2"]).reshape(2, 4, D, FT, 4, 32)
    return {
        "x": f(x), "xT": f(x.T), "ctxT": f(cx.T), "mask": f(i["mask_BxS2_ik0"]),
        "squares": f(np.stack([sq[n] for n in SQUARES], axis=1)),
        "consts": pack(con, CONSTS), "consts1": pack(con1, CONSTS1),
        "cols": same(col, COLS), "rows": same(row, ROWS).reshape(-1),
        "moe_g": f(i["L0_ffn_Wg"]), "moe_w1": f(np.asarray(i["L0_ffn_W1"]).transpose(1, 0, 2)),
        "moe_w2": f(np.asarray(i["L0_ffn_W2"]).reshape(2 * E0, 128, D).transpose(1, 0, 2)),
        "gw2r": f(np.repeat(np.asarray(i["L1_ffn_gate_w2"]).T.reshape(128, 2, 4), 32, axis=2)),
        "ff_w1": f(T("L1_ffn_W1")), "ff_w2": f(T("L1_ffn_W2").reshape(FT, 128, D).transpose(1, 0, 2).reshape(128, HID1)),
        "ff_tw1": f(tw1.transpose(1, 4, 3, 0, 2).reshape(128, 4, 2, HID1)),
        "ff_tw2": f(tw2.transpose(1, 5, 4, 0, 3, 2).reshape(128, 4, 2, HID1)),
        "ff_tb1": f(np.asarray(i["L1_ffn_Tb1"]).reshape(2, 4, HID1).transpose(1, 0, 2)),
        "ff_tb2": f(np.asarray(i["L1_ffn_Tb2"]).reshape(2, 4, D).transpose(1, 0, 2)),
    }


def kernel(**inputs):
    import concourse.bacc as bacc
    from concourse.bass_utils import run_bass_kernel_spmd

    nc = bacc.Bacc("TRN2", target_bir_lowering=False, num_devices=1)
    arrays = {f"in_{k}": a for k, a in _lay_out(inputs).items()}
    args = [nc.dram_tensor(k, a.shape, mybir.dt.from_np(a.dtype), kind="ExternalInput").ap() for k, a in arrays.items()]
    out = nc.dram_tensor("out_dram", (B * SEQ, D), F32, kind="ExternalOutput").ap()
    decoder_kernel(nc, *args, out)
    got = run_bass_kernel_spmd(nc, [arrays], core_ids=[0]).results[0]["out_dram"]
    return got.reshape(B, SEQ, D)
```

```python
from contextlib import ExitStack

import numpy as np
import concourse.bass as bass
from concourse import mybir

ALU = mybir.AluOpType
ACT = mybir.ActivationFunctionType
AX = mybir.AxisListType
F32 = mybir.dt.float32
I32 = mybir.dt.int32
U32 = mybir.dt.uint32

B, SEQ, D, H = 32, 64, 128, 16
HD = D // H
GB = 4
GT = GB * SEQ
TT = GT // 128
PAIR = 2
STREAMS = 2
STEPS = B // (GB * PAIR * STREAMS)
E0, HID0 = 8, 256
E1, HID1 = 8, 512
FT = HID1 // 128
ROOT8 = float(np.sqrt(np.float32(HD)))
SCALE = 1.0 / ROOT8
EPS = 1e-5
GELU_A, GELU_C = 0.044715, float(np.sqrt(2.0 / np.pi))
MINUS = -1e30
MASKED = ("a0", "c0", "s1")
ROUTE_STEPS = 10

SQUARES = ["a0q", "a0k", "a0v", "a0o", "c0q", "c0k", "c0v", "c0o", "r1q", "r1k", "r1v", "r1g",
           "s1q", "s1k", "s1v", "s1o", "c1q", "c1k", "c1v", "c1o", "f1g"]
N_SQ0 = 8
CONSTS = {"ident": 128, "causal": 512, "jmask": 4, "ones": 64, "iota": 8, "neghalf": 2}
CONSTS1 = {"cos": 64, "sin": 64, "diff": 512, "id32": 32, "sign": 1}
COLS = {"bq_r": 1, "bk_r": 1, "bqp_r": 1, "bkp_r": 1, "bq_s": 1, "bk_s": 1, "bo_s": 1, "bq_c": 1,
        "bk_c": 1, "gb1": 1, "b1": 4, "gb2": 2, "gamma": 4}
ROWS = {"bo_a": 128, "bo_c0": 128, "bg_r": 128, "bo_c1": 128, "b2": 128, "bv_r": 128, "bv_s": 128,
        "bv_c": 128}


def places(widths):
    at, out = 0, {}
    for name, w in widths.items():
        out[name] = (at, at + w)
        at += w
    return out, at


def attention(l):
    o = [("proj", l, 0), ("projv", l, 0), ("qk", l, 0), ("qk", l, 1), ("tp", l, 0)]
    if l == "r1":
        o.insert(2, ("gate", l, 0))
    o += [("qk", l, 2), ("pv", l, 0), ("tp", l, 1), ("qk", l, 3), ("pv", l, 1),
          ("tp", l, 2), ("pv", l, 2), ("tp", l, 3), ("pv", l, 3), ("oproj", l, 0)]
    if l == "s1":
        return o
    o += [("ln1", l, 0), ("ln2", l, 0), ("xt", l, 0)]
    return o + ([] if l == "c0" else [("xb", l, 0)])


def experts():
    o = [("logit", "m0", 0), ("w1", "m0", 0), ("route", "m0", 0), ("w1", "m0", 1)]
    for e in range(E0):
        o.append(("w2", "m0", e))
        if e + 2 < E0:
            o.append(("w1", "m0", e + 2))
    return o + [("ln1", "m0", 0), ("ln2", "m0", 0), ("xt", "m0", 0)]


def feedforward():
    f = "f1"
    return [("g1", f, 0), ("gcol", f, 0), ("mb", f, 0), ("gen1", f, 0), ("gen1", f, 1), ("u", f, 0), ("gen2", f, 0),
            ("ut", f, 0), ("gelu", f, 0), ("gen2", f, 1), ("gen1", f, 2), ("act", f, 0), ("gen1", f, 3), ("u", f, 1),
            ("out", f, 0), ("gen2", f, 2), ("ut", f, 1), ("gelu", f, 1), ("gen2", f, 3), ("act", f, 1), ("out", f, 1),
            ("ln1", f, 0), ("ln2", f, 0), ("store", f, 0)]


STAGES = ([("load", "in", 0), ("xb", "in", 0)] + attention("a0") + [("mask", "in", 0)] + attention("c0") + experts()
          + attention("r1") + attention("s1") + attention("c1") + feedforward())
COST = {"proj": 90, "projv": 110, "gate": 45, "qk": 90, "tp": 50, "pv": 110, "oproj": 45,
        "ln1": 1, "ln2": 60, "xt": 30, "logit": 20, "w1": 90, "w2": 90, "route": 1, "g1": 45,
        "gcol": 20, "mb": 60, "gen1": 190, "gen2": 190, "u": 90, "ut": 50, "gelu": 1, "out": 140,
        "store": 1, "act": 1, "xb": 1, "mask": 1, "load": 1}
LATE = (0.0, 0.004, 0.008, 0.012)


def paced(stages, late):
    whole = sum(COST[s[0]] for s in stages)
    done, out = 0, []
    for s in stages:
        out.append(done / whole + late)
        done += COST[s[0]]
    return out


def merged():
    both = [(at, late, stream, stage + (k,)) for stream in range(STREAMS) for k in range(PAIR)
            for late in (LATE[STREAMS * k + stream],) for at, stage in zip(paced(STAGES, late), STAGES)]
    both.sort(key=lambda x: x[:2])
    return [(stream, stage) for _, _, stream, stage in both]


def signals(stage):
    s, l, b, k = stage
    if s == "load":
        return {f"loaded_{what}{k}": 16 for what in ("x", "xT", "mask", "ctx")}
    if s == "xb":
        return {"xb": 1}
    if s == "mask":
        return {"keep": 2}
    if s == "proj":
        return {"r1": {"full_M": 1, "free_M": 1, "full_T": 1, "free_T": 1, "rope": 1, "blocks": 1, "blocks_q": 1},
                "c0": {"full_M": 1, "free_M": 1, "full_T": 1, "free_T": 1, "blocks": 1}}.get(
                    l, {"full_M": 1, "free_M": 1, "full_T": 1, "free_T": 1})
    if s == "gate":
        return {"full_Y": 1, "free_Y": 1, "gtanh": 1, "gate": 1}
    if s == "qk":
        return {"full_S": 1, "free_S": 1} | ({} if l == "r1" else {"rowmax": 1, "p": 1}) | (
            {"shifted": 1} if l in MASKED else {})
    if s == "pv":
        return {"full_Y": 1, "free_Y": 1} | ({} if l == "r1" else {"recip": 1})
    if s == "oproj":
        return {"full_M": 1, "free_M": 1} | ({"resid": 1} if l == "r1" else {})
    if s == "ln1":
        return {"stats": 1, "moments": 1, "vareps": 1, "rstd": 1}
    if s == "ln2":
        return {"x": 1}
    if s == "logit":
        return {"full_M": 1, "lmax": 1, "free_M": 1, "lexp": 1}
    if s == "route":
        return {"routed": ROUTE_STEPS, "comb": 1}
    if s == "w1":
        return {f"full_{'ST'[b % 2]}": 1, f"free_{'ST'[b % 2]}": 1, "hid": 1}
    if s == "w2":
        return {f"full_{'YM'[b % 2]}": 1, f"free_{'YM'[b % 2]}": 1}
    if s == "g1":
        return {"full_M": 1, "free_M": 1, "hmean": 1}
    if s == "gcol":
        return {"full_M": 1, "free_M": 1, "gdiag": 1}
    if s == "gelu":
        return {"zsq": 1, "zcub": 1, "tanh": 1}
    if s == "act":
        return {"act": 1}
    if s == "store":
        return {f"stored{k}": 16}
    bank = {"projv": "M", "xt": "M", "tp": "T", "mb": "M", "gen1": "S", "gen2": "T", "u": "M", "ut": "Y", "out": "M"}[s]
    return {"full_" + bank: 1, "free_" + bank: 1}


class Tally:

    def __init__(self, stages):
        self.stages, self.total, self.events = stages, {}, {}
        for stage in stages:
            for name, k in signals(stage).items():
                self.total[name] = self.total.get(name, 0) + k
                self.events.setdefault(name, []).append((stage, self.total[name]))

    def after(self, name, stage):
        return dict(self.events[name])[stage]

    def previous(self, name, stage):
        ev = self.events[name]
        i = [s for s, _ in ev].index(stage) - 1
        return (0, ev[i][1]) if i >= 0 else (1, ev[-1][1])

    def same_kind(self, stage, lag):
        kind = [s for s in self.stages if (s[0], s[3]) == (stage[0], stage[3])]
        i = kind.index(stage) - lag
        return (0, kind[i]) if i >= 0 else (1, kind[i])


def decoder_kernel(nc, x, xT, ctxT, mask, squares, consts, consts1, cols, rows, moe_g, moe_w1, moe_w2,
                   gw2r, ff_w1, ff_w2, ff_tw1, ff_tw2, ff_tb1, ff_tb2, out):
    c_at, c_n = places(CONSTS)
    c1_at, c1_n = places(CONSTS1)
    v_at, v_n = places(COLS)
    r_at, r_n = places(ROWS)

    x_d = x.rearrange("(g w k tt p) d -> g w k p tt d", w=STREAMS, k=PAIR, tt=TT, p=128)
    xT_d = xT.rearrange("d (g w k t) -> g w k d t", w=STREAMS, k=PAIR, t=GT)
    ctxT_d = ctxT.rearrange("d (g w k t) -> g w k d t", w=STREAMS, k=PAIR, t=GT)
    mask_d = mask.rearrange("(g w k b) s -> g w k (b s)", w=STREAMS, k=PAIR, b=GB)
    out_d = out.rearrange("(g w k tt p) d -> g w k p tt d", w=STREAMS, k=PAIR, tt=TT, p=128)

    with ExitStack() as ctx:
        def sb(name, shape, dt=F32):
            return ctx.enter_context(nc.sbuf_tensor(name, shape, dt))

        def semaphore(name):
            return ctx.enter_context(nc.semaphore(name))

        sq = sb("sq", [128, len(SQUARES), 128])
        con = sb("con", [128, c_n])
        con1 = sb("con1", [128, c1_n])
        col = sb("col", [128, v_n])
        row = sb("row", [128, r_n])
        wg_sb = sb("wg_sb", [128, E0])
        w1_sb = sb("w1_sb", [128, E0, HID0])
        w2_sb = sb("w2_sb", [128, 2 * E0, D])
        gw2_sb = sb("gw2_sb", [128, 2, 128])
        base1 = sb("base1", [128, HID1])
        base2 = sb("base2", [128, HID1])
        tw1_sb = sb("tw1_sb", [128, 4, 2, HID1])
        tw2_sb = sb("tw2_sb", [128, 4, 2, HID1])
        tb1_sb = sb("tb1_sb", [128, 2, HID1])
        tb2_sb = sb("tb2_sb", [128, 2, D])
        wrot = sb("wrot", [128, 2, 128])
        brot = sb("brot", [128, 2])
        bk_s = sb("bk_s", [128, 4])
        bk_c = sb("bk_c", [128, 4])
        b1h = sb("b1h", [128, FT])
        dtmp = sb("dtmp", [128, 4, 4])

        def W(name):
            return sq[:, SQUARES.index(name), :]

        def C(name):
            a, b = c_at[name]
            return con[:, a:b]

        def C1(name):
            a, b = c1_at[name]
            return con1[:, a:b]

        def V(name, p0=0, p1=128):
            a, b = v_at[name]
            return col[p0:p1, a:b]

        decay = C1("diff")

        def R(name, p0=0, p1=128, n=128):
            a, _ = r_at[name]
            return row[p0:p1, a:a + n]

        ident = C("ident")

        class Stream:
            pass

        order = merged()

        def stream(tag, number):
            s = Stream()
            s.tag, s.number = tag, number
            s.tally = Tally([stage for stream, stage in order if stream == number])
            s.sem = {k: semaphore(f"{tag}_{k}") for k in s.tally.total}
            s.bank = {k: ctx.enter_context(nc.psum_tensor(f"{tag}_{k}", [128, 512], F32)) for k in "MSTY"}
            s.own = [group(f"{tag}{k}") for k in range(PAIR)]
            return s

        def group(tag):
            u = Stream()
            u.tag = tag
            u.Q = sb(f"{tag}_Q", [128, GB * 2, 4, 32])
            u.K = sb(f"{tag}_K", [128, GB, 4, SEQ])
            u.V = sb(f"{tag}_V", [128, GB * 4, 2, 2, 2, HD])
            u.P = sb(f"{tag}_P", [128, 2, 512])
            u.PT = sb(f"{tag}_PT", [128, 8, 2, 32])
            u.mx = sb(f"{tag}_mx", [128, 2, 8])
            u.rz = sb(f"{tag}_rz", [128, 2, SEQ])
            u.yT = sb(f"{tag}_yT", [128, GT])
            u.xb = sb(f"{tag}_xb", [128, TT, D])
            u.x = sb(f"{tag}_x", [128, TT, D])
            u.xT = sb(f"{tag}_xT", [128, GT])
            u.ctxT = sb(f"{tag}_ctxT", [128, GT])
            u.st = sb(f"{tag}_st", [128, TT, 6])
            u.mv = sb(f"{tag}_mv", [128, TT, 2])
            u.ve = sb(f"{tag}_ve", [128, TT])
            u.rstd = sb(f"{tag}_rstd", [128, TT])
            u.mW1b = sb(f"{tag}_mW1b", [128, HID1])
            u.mW2 = sb(f"{tag}_mW2", [128, 2, HID1])
            u.lg = sb(f"{tag}_lg", [128, TT, E0])
            u.lmx = sb(f"{tag}_lmx", [128, TT])
            u.lsum = sb(f"{tag}_lsum", [128, TT])
            u.lrec = sb(f"{tag}_lrec", [128, TT])
            u.prob = sb(f"{tag}_prob", [128, TT, E0])
            u.top = sb(f"{tag}_top", [128, TT, 8])
            u.topi = sb(f"{tag}_topi", [128, TT, 8], U32)
            u.topf = sb(f"{tag}_topf", [128, TT, 2])
            u.wsum = sb(f"{tag}_wsum", [128, TT])
            u.wrec = sb(f"{tag}_wrec", [128, TT])
            u.wn = sb(f"{tag}_wn", [128, TT, 2])
            u.pick = sb(f"{tag}_pick", [128, TT, 2, E0])
            u.comb = sb(f"{tag}_comb", [128, TT, E0])
            u.hm = sb(f"{tag}_hm", [128, GB])
            u.gcol = sb(f"{tag}_gcol", [128, 2, GB])
            u.mb = sb(f"{tag}_mb", [128, TT, FT, 2])
            PT = u.PT[:, :, :, :].rearrange("p a b c -> p (a b c)")
            K = u.K[:, :, :, :].rearrange("p (e b) j k -> p e (b j k)", e=2)
            u.r = u.xb
            u.xinT = u.hT = u.gh = u.yT
            u.gate = u.mW2[:, 0, 0:GT].rearrange("p (t d) -> p t d", t=TT)
            u.mbias = u.mW2[:, 0, GT:2 * GT].rearrange("p (b k) -> p b k", b=GB)
            u.keep = u.mW2[:, 1, 0:GT]
            u.mask_i = u.keep.bitcast(I32)
            u.kz = PT[:, 0:GT]
            u.hr, u.hid = K, u.P
            u.rt1 = u.P[:, 0, :].rearrange("p (n t) -> p n t", n=2)
            u.rt2 = u.P[:, 1, :].rearrange("p (n t) -> p n t", n=2)
            u.gz = PT[:, 0:GT].rearrange("p (t d) -> p t d", t=TT)
            u.gdiag = u.ctxT[:, :].rearrange("p (n b k) -> p n b k", n=2, b=GB)
            u.mW1 = [PT, u.mW1b[:, :]]
            u.us = u.zz = K
            u.z = u.P
            return u

        streams = (stream("f", 0), stream("s", 1))
        scratch = sb("scratch", [128, 1])

        loaded0 = semaphore("loaded0")
        loaded1 = semaphore("loaded1")
        loadedp = semaphore("loadedp")
        loaded2 = semaphore("loaded2")
        zeroed = semaphore("zeroed")
        gexp = semaphore("gexp")
        nsig = semaphore("nsig")
        decayed = semaphore("decayed")
        made = semaphore("made")
        ZEROED = 2 * STREAMS * PAIR + 2
        LOADED0, LOADEDP, LOADED1, LOADED2 = 2 * 16, 3 * 16, 5 * 16, (6 + 8) * 16


        class Due:

            def __init__(self, count):
                self.count = count

        class Counts:

            def __init__(self, n):
                self.n, self.seen = n, {}

            def at(self, s, name, count, groups_back=0):
                n, total = self.n, s.tally.total[name]
                mark = count - groups_back * total
                if isinstance(n, int) and n < groups_back or self.seen.get((s.tag, name), -10**9) >= mark:
                    return None
                self.seen[s.tag, name] = mark
                return Due(n * total + mark)

            def done(self, s, name, stage):
                return self.at(s, name, s.tally.after(name, stage))

            def step(self, s, name, stage, left):
                return self.at(s, name, s.tally.after(name, stage) - left)

            def before(self, s, name, stage):
                back, count = s.tally.previous(name, stage)
                return self.at(s, name, count, back)

            def same_kind(self, s, name, stage, lag):
                back, other = s.tally.same_kind(stage, lag)
                return self.at(s, name, s.tally.after(name, other), back)

            def last_group(self, s, name, stage):
                return self.at(s, name, s.tally.after(name, stage), 1)

        def program(eng, emit):
            with eng.Fori(0, STEPS) as t:
                emit(t, Counts(t + 1))

        block = ctx.enter_context(nc.Block())

        @block.sync
        def _(sp):
            def load(step, w):
                for k in range(PAIR):
                    for s in streams:
                        u, at = s.own[k], (step, s.number, k)
                        if due := w.last_group(s, "hmean", ("g1", "f1", 0, k)):
                            sp.wait_ge(s.sem["hmean"], due.count)
                        sp.dma_start(u.xinT[:, :], xT_d[at]).then_inc(s.sem[f"loaded_xT{k}"], 16)
                        if due := w.last_group(s, "full_T", ("gen2", "f1", GB - 1, k)):
                            sp.wait_ge(s.sem["full_T"], due.count)
                        sp.dma_start(u.ctxT[:, :], ctxT_d[at]).then_inc(s.sem[f"loaded_ctx{k}"], 16)
                        if due := w.last_group(s, "full_M", ("out", "f1", 1, k)):
                            sp.wait_ge(s.sem["full_M"], due.count)
                        sp.dma_start(u.mask_i, mask_d[at].partition_broadcast(128)).then_inc(s.sem[f"loaded_mask{k}"], 16)
                        if due := w.last_group(s, f"stored{k}", ("store", "f1", 0, k)):
                            sp.wait_ge(s.sem[f"stored{k}"], due.count)
                        sp.dma_start(u.x[:, :, :], x_d[at]).then_inc(s.sem[f"loaded_x{k}"], 16)

            sp.dma_start(sq[:, 0:4, :], squares[:, 0:4, :]).then_inc(loaded0, 16)
            sp.dma_start(con[:, :], consts).then_inc(loaded0, 16)
            load(0, Counts(0))
            sp.dma_start(sq[:, N_SQ0:N_SQ0 + 2, :], squares[:, N_SQ0:N_SQ0 + 2, :]).then_inc(loadedp, 16)
            sp.dma_start(con1[:, :], consts1).then_inc(loadedp, 16)
            sp.dma_start(col[:, :], cols).then_inc(loadedp, 16)
            sp.dma_start(row[:, :], rows.partition_broadcast(128)).then_inc(loaded1, 16)
            sp.dma_start(sq[:, 4:8, :], squares[:, 4:8, :]).then_inc(loaded1, 16)
            sp.dma_start(wg_sb[:, :], moe_g).then_inc(loaded1, 16)
            sp.dma_start(w1_sb[:, :, :], moe_w1).then_inc(loaded1, 16)
            sp.dma_start(w2_sb[:, :, :], moe_w2).then_inc(loaded1, 16)
            sp.dma_start(sq[:, N_SQ0 + 2:, :], squares[:, N_SQ0 + 2:, :]).then_inc(loaded2, 16)
            sp.dma_start(gw2_sb[:, :, :], gw2r).then_inc(loaded2, 16)
            sp.dma_start(base1[:, :], ff_w1).then_inc(loaded2, 16)
            sp.dma_start(base2[:, :], ff_w2).then_inc(loaded2, 16)
            sp.dma_start(tw1_sb[:, :, :, :], ff_tw1).then_inc(loaded2, 16)
            sp.dma_start(tw2_sb[:, :, :, :], ff_tw2).then_inc(loaded2, 16)
            sp.wait_ge(zeroed, ZEROED)
            for e in range(4):
                sp.dma_start(tb1_sb[32 * e:32 * e + 1, :, :], ff_tb1[e:e + 1]).then_inc(loaded2, 16)
                sp.dma_start(tb2_sb[32 * e:32 * e + 1, :, :], ff_tb2[e:e + 1]).then_inc(loaded2, 16)
            with sp.Fori(0, STEPS - 1) as t:
                load(t + 1, Counts(t + 2))

        @block.tensor
        def _(pe):
            mm = nc.tensor.matmul

            def source(s, l, k):
                u = s.own[k]
                return {"a0": u.xinT, "c1": u.hT}.get(l, u.xT)

            def wait_source(s, l, k, w):
                if l == "a0":
                    if due := w.done(s, f"loaded_xT{k}", ("load", "in", 0, k)):
                        pe.wait_ge(s.sem[f"loaded_xT{k}"], due.count)
                else:
                    before = {"c0": ("xt", "a0", 0, k), "m0": ("xt", "c0", 0, k), "r1": ("xt", "m0", 0, k),
                              "s1": ("xt", "r1", 0, k), "c1": ("oproj", "s1", 0, k), "f1": ("xt", "c1", 0, k)}[l]
                    if due := w.done(s, "free_M", before):
                        pe.wait_ge(s.sem["free_M"], due.count)

            def emit(t, w):
                for who, stage in order:
                    s = streams[who]
                    name, l, b, k = stage
                    u = s.own[k]
                    M, S, T, Y = (s.bank[m] for m in "MSTY")
                    X = source(s, l, k)
                    if name == "proj":
                        if l == "c0":
                            pe.wait_ge(loaded1, LOADED1)
                        if l == "r1":
                            pe.wait_ge(made, 1)
                            pe.wait_ge(loaded2, LOADED2)
                        wait_source(s, l, k, w)
                        kX = X
                        if l in ("c0", "c1"):
                            if due := w.done(s, f"loaded_ctx{k}", ("load", "in", 0, k)):
                                pe.wait_ge(s.sem[f"loaded_ctx{k}"], due.count)
                            kX = u.ctxT
                        if due := w.before(s, "free_M", stage):
                            pe.wait_ge(s.sem["free_M"], due.count)
                        mq = mm(M[:, 0:GT], W(l + "q"), X[:, :], start=True, stop=True)
                        if l == "r1":
                            mm(M[:, GT:2 * GT], W(l + "k"), kX[:, :], start=True, stop=True).then_inc(s.sem["full_M"], 1)
                            if due := w.before(s, "free_T", stage):
                                pe.wait_ge(s.sem["free_T"], due.count)
                            mm(T[:, 0:GT], wrot[:, 0, :], X[:, :], start=True, stop=True)
                            mm(T[:, GT:2 * GT], wrot[:, 1, :], X[:, :], start=True, stop=True).then_inc(s.sem["full_T"], 1)
                        else:
                            mq.then_inc(s.sem["full_M"], 1)
                            if due := w.before(s, "free_T", stage):
                                pe.wait_ge(s.sem["free_T"], due.count)
                            mm(T[:, 0:GT], W(l + "k"), kX[:, :], start=True, stop=True).then_inc(s.sem["full_T"], 1)
                    elif name == "projv":
                        vX = u.ctxT if l in ("c0", "c1") else X
                        if due := w.before(s, "free_M", stage):
                            pe.wait_ge(s.sem["free_M"], due.count)
                        for q in range(GB):
                            for j2 in range(2):
                                last = mm(M[64 * j2:64 * j2 + 64, 64 * q:64 * q + 64], vX[:, 64 * q:64 * q + 64],
                                          W(l + "v")[:, 64 * j2:64 * j2 + 64], start=True, stop=True)
                        last.then_inc(s.sem["full_M"], 1)
                    elif name == "gate":
                        if due := w.before(s, "free_Y", stage):
                            pe.wait_ge(s.sem["free_Y"], due.count)
                        for t in range(TT):
                            last = mm(Y[:, 128 * t:128 * t + 128], X[:, 128 * t:128 * t + 128], W("r1g"), start=True, stop=True)
                        last.then_inc(s.sem["full_Y"], 1)
                    elif name == "qk":
                        if l != "r1":
                            if due := w.done(s, "free_M", ("proj", l, 0, k)):
                                pe.wait_ge(s.sem["free_M"], due.count)
                            if due := w.done(s, "free_T", ("proj", l, 0, k)):
                                pe.wait_ge(s.sem["free_T"], due.count)
                        if l in ("r1", "c0"):
                            if due := w.done(s, "blocks", ("proj", l, 0, k)):
                                pe.wait_ge(s.sem["blocks"], due.count)
                        if l == "r1":
                            if due := w.done(s, "blocks_q", ("proj", l, 0, k)):
                                pe.wait_ge(s.sem["blocks_q"], due.count)
                        if due := w.before(s, "free_S", stage):
                            pe.wait_ge(s.sem["free_S"], due.count)
                        for qh in range(2):
                            last = mm(S[:, 256 * qh:256 * qh + 256], u.Q[:, 2 * b + qh, :, :].rearrange("p g q -> p (g q)"),
                                      u.K[:, b, :, :].rearrange("p j k -> p (j k)"), start=True, stop=True)
                        last.then_inc(s.sem["full_S"], 1)
                    elif name == "tp":
                        if due := w.done(s, "free_S" if l == "r1" else "p", ("qk", l, b, k)):
                            pe.wait_ge(s.sem["free_S" if l == "r1" else "p"], due.count)
                        if due := w.before(s, "free_T", stage):
                            pe.wait_ge(s.sem["free_T"], due.count)
                        for n in range(4):
                            last = nc.tensor.transpose(T[:, 128 * n:128 * n + 128], u.P[:, b % 2, 128 * n:128 * n + 128], ident)
                        last.then_inc(s.sem["full_T"], 1)
                    elif name == "pv":
                        if due := w.done(s, "free_T", ("tp", l, b, k)):
                            pe.wait_ge(s.sem["free_T"], due.count)
                        if b == 0:
                            if due := w.done(s, "free_M", ("projv", l, 0, k)):
                                pe.wait_ge(s.sem["free_M"], due.count)
                        if due := w.before(s, "free_Y", ("pv", l, b, k)):
                            pe.wait_ge(s.sem["free_Y"], due.count)
                        for part in range(1 if l == "r1" else 2):
                            c0 = 64 * part
                            for jp in range(2):
                                for g in range(4):
                                    lhs = u.V[:, 4 * b + g, jp, :, :, :] if part == 0 else C("ones")[:, 32 * jp:32 * jp + 32]
                                    if part == 0:
                                        lhs = lhs.rearrange("p a b d -> p (a b d)")
                                    last = mm(Y[32 * g:32 * g + 32, c0:c0 + 64], lhs,
                                              u.PT[:, 4 * jp + g, :, :].rearrange("p a q -> p (a q)"),
                                              start=(jp == 0), stop=(jp == 1))
                        last.then_inc(s.sem["full_Y"], 1)
                    elif name == "oproj":
                        if due := w.done(s, "free_Y", ("pv", l, GB - 1, k)):
                            pe.wait_ge(s.sem["free_Y"], due.count)
                        if due := w.before(s, "free_M", stage):
                            pe.wait_ge(s.sem["free_M"], due.count)
                        if l == "s1":
                            last = mm(M[:, 0:GT], W("s1o"), u.yT[:, :], start=True, stop=True)
                        for t in range(0 if l == "s1" else TT):
                            part = slice(128 * t, 128 * t + 128)
                            if l == "r1":
                                last = nc.tensor.transpose(M[:, part], u.yT[:, part], ident)
                            else:
                                last = mm(M[:, part], u.yT[:, part], W(l + "o"), start=True, stop=True)
                        last.then_inc(s.sem["full_M"], 1)
                    elif name == "xt":
                        if due := w.done(s, "x", ("ln2", l, 0, k)):
                            pe.wait_ge(s.sem["x"], due.count)
                        if due := w.before(s, "free_M", stage):
                            pe.wait_ge(s.sem["free_M"], due.count)
                        for t in range(TT):
                            last = nc.tensor.transpose(M[:, 128 * t:128 * t + 128], u.x[:, t, :], ident)
                        last.then_inc(s.sem["full_M"], 1)
                    elif name == "logit":
                        wait_source(s, l, k, w)
                        if due := w.before(s, "free_M", stage):
                            pe.wait_ge(s.sem["free_M"], due.count)
                        for t in range(TT):
                            last = mm(M[:, E0 * t:E0 * t + E0], X[:, 128 * t:128 * t + 128], wg_sb[:, :], start=True, stop=True)
                        last.then_inc(s.sem["full_M"], 1)
                    elif name == "w1":
                        bank = "ST"[b % 2]
                        if due := w.before(s, "free_" + bank, stage):
                            pe.wait_ge(s.sem["free_" + bank], due.count)
                        for n in range(2):
                            last = mm(s.bank[bank][:, GT * n:GT * n + GT], w1_sb[:, b, 128 * n:128 * n + 128], X[:, :], start=True, stop=True)
                        last.then_inc(s.sem["full_" + bank], 1)
                    elif name == "w2":
                        bank = "YM"[b % 2]
                        if due := w.done(s, "hid", ("w1", l, b, k)):
                            pe.wait_ge(s.sem["hid"], due.count)
                        if due := w.before(s, "free_" + bank, stage):
                            pe.wait_ge(s.sem["free_" + bank], due.count)
                        for t in range(TT):
                            for n in range(2):
                                last = mm(s.bank[bank][:, 128 * t:128 * t + 128], u.hid[:, b % 2, GT * n + 128 * t:GT * n + 128 * t + 128],
                                          w2_sb[:, 2 * b + n, :], start=(n == 0), stop=(n == 1))
                        last.then_inc(s.sem["full_" + bank], 1)
                    elif name == "g1":
                        wait_source(s, l, k, w)
                        if due := w.before(s, "free_M", stage):
                            pe.wait_ge(s.sem["free_M"], due.count)
                        mm(M[:, 0:GT], W("f1g"), X[:, :], start=True, stop=True).then_inc(s.sem["full_M"], 1)
                    elif name == "gcol":
                        if due := w.done(s, "hmean", ("g1", l, 0, k)):
                            pe.wait_ge(s.sem["hmean"], due.count)
                        if due := w.before(s, "free_M", stage):
                            pe.wait_ge(s.sem["free_M"], due.count)
                        for n in range(2):
                            last = mm(M[:, GB * n:GB * n + GB], gw2_sb[:, n, :], u.hm[:, :], start=True, stop=True)
                        last.then_inc(s.sem["full_M"], 1)
                    elif name == "mb":
                        if due := w.before(s, "free_M", stage):
                            pe.wait_ge(s.sem["free_M"], due.count)
                        for f in range(FT):
                            o = M[:, 0:TT * FT * 2].rearrange("p (t f b) -> p t f b", t=TT, f=FT)[:, :, f, :]
                            for n in range(2):
                                last = mm(o, tb1_sb[:, n, 128 * f:128 * f + 128], u.gcol[:, n, :].rearrange("p (t b) -> p t b", t=TT),
                                          start=(n == 0), stop=(n == 1))
                        last.then_inc(s.sem["full_M"], 1)
                    elif name in ("gen1", "gen2"):
                        bank, tw = ("S", tw1_sb) if name == "gen1" else ("T", tw2_sb)
                        if due := w.done(s, "gdiag", ("gcol", l, 0, k)):
                            pe.wait_ge(s.sem["gdiag"], due.count)
                        if due := w.before(s, "free_" + bank, stage):
                            pe.wait_ge(s.sem["free_" + bank], due.count)
                        for n in range(2):
                            for c in range(4):
                                last = mm(s.bank[bank][32 * c:32 * c + 32, :], u.gdiag[:, n, b, :], tw[:, c, n, :], start=(n == 0), stop=(n == 1))
                        last.then_inc(s.sem["full_" + bank], 1)
                    elif name == "u":
                        if due := w.done(s, "free_S", ("gen1", l, 2 * b + 1, k)):
                            pe.wait_ge(s.sem["free_S"], due.count)
                        if due := w.before(s, "free_M", stage):
                            pe.wait_ge(s.sem["free_M"], due.count)
                        for n in range(2):
                            q = 2 * b + n
                            last = mm(M[64 * n:64 * n + 64, :], X[:, 64 * q:64 * q + 64], u.mW1[n], start=True, stop=True)
                        last.then_inc(s.sem["full_M"], 1)
                    elif name == "ut":
                        if due := w.done(s, "free_M", ("u", l, b, k)):
                            pe.wait_ge(s.sem["free_M"], due.count)
                        if due := w.before(s, "free_Y", stage):
                            pe.wait_ge(s.sem["free_Y"], due.count)
                        for f in range(FT):
                            last = nc.tensor.transpose(Y[:, 128 * f:128 * f + 128], u.us[:, b, 128 * f:128 * f + 128], ident)
                        last.then_inc(s.sem["full_Y"], 1)
                    elif name == "out":
                        if due := w.done(s, "act", ("act", l, b, k)):
                            pe.wait_ge(s.sem["act"], due.count)
                        if due := w.done(s, "free_T", ("gen2", l, 2 * b + 1, k)):
                            pe.wait_ge(s.sem["free_T"], due.count)
                        if due := w.before(s, "free_M", stage):
                            pe.wait_ge(s.sem["free_M"], due.count)
                        for n in range(2):
                            q = 2 * b + n
                            o = M[64 * n:64 * n + 64, 0:D]
                            for f in range(FT):
                                mm(o, u.zz[:, b, 128 * f + 64 * n:128 * f + 64 * n + 64], u.mW2[:, n, 128 * f:128 * f + 128], start=(f == 0), stop=False)
                            for m in range(2):
                                last = mm(o, u.gcol[:, m, q:q + 1].to_broadcast([128, 64]), tb2_sb[:, m, :], start=False, stop=(m == 1))
                        last.then_inc(s.sem["full_M"], 1)

            pe.wait_ge(loaded0, LOADED0)
            pe.wait_ge(zeroed, ZEROED)
            program(pe, emit)

        @block.scalar
        def _(act):
            fn = nc.scalar.activation

            def emit(t, w):
                for who, stage in order:
                    s = streams[who]
                    name, l, b, k = stage
                    u = s.own[k]
                    M, S, T, Y = (s.bank[m] for m in "MSTY")
                    if name == "proj":
                        if l == "r1":
                            if due := w.done(s, "rope", stage):
                                act.wait_ge(s.sem["rope"], due.count)
                            src = u.rt1[:, 0, :]
                        else:
                            if due := w.done(s, "full_M", stage):
                                act.wait_ge(s.sem["full_M"], due.count)
                            src = M[:, 0:GT]
                        for g in range(4):
                            p = slice(32 * g, 32 * g + 32)
                            i = src[p, :].rearrange("p (a q) -> p a q", q=32)
                            o = u.Q[p, :, g, :]
                            if l in ("s1", "c1"):
                                last = fn(o, i, ACT.Identity, bias=V("bq_" + l[0], 32 * g, 32 * g + 32))
                            else:
                                last = fn(o, i, ACT.Copy)
                        last.then_inc(s.sem["blocks_q" if l == "r1" else "free_M"], 1)
                    elif name == "gate":
                        if due := w.done(s, "free_Y", stage):
                            act.wait_ge(s.sem["free_Y"], due.count)
                        fn(u.gate[:, :, :], u.gz[:, :, :], ACT.Tanh, scale=0.5).then_inc(s.sem["gtanh"], 1)
                    elif name == "qk" and l != "r1":
                        if due := w.done(s, "free_S" if l == "c1" else "shifted", stage):
                            act.wait_ge(s.sem["free_S" if l == "c1" else "shifted"], due.count)
                        fn(u.P[:, b % 2, :], u.P[:, b % 2, :], ACT.Exp, scale=SCALE).then_inc(s.sem["p"], 1)
                    elif name == "tp":
                        if due := w.done(s, "full_T", stage):
                            act.wait_ge(s.sem["full_T"], due.count)
                        i = T[:, :].rearrange("p (a g q) -> p a g q", a=2, q=32)
                        o = u.PT[:, :, :, :].rearrange("p g a q -> p a g q")
                        fn(o, i, ACT.Copy).then_inc(s.sem["free_T"], 1)
                    elif name == "pv" and l == "r1":
                        if due := w.done(s, "full_Y", ("pv", l, b, k)):
                            act.wait_ge(s.sem["full_Y"], due.count)
                        fn(u.yT[:, SEQ * b:SEQ * b + SEQ], Y[:, 0:SEQ], ACT.Copy).then_inc(s.sem["free_Y"], 1)
                    elif name == "oproj" and l == "s1":
                        if due := w.done(s, "full_M", stage):
                            act.wait_ge(s.sem["full_M"], due.count)
                        fn(u.hT[:, :], M[:, 0:GT], ACT.Identity, bias=V("bo_s")).then_inc(s.sem["free_M"], 1)
                    elif name == "xt":
                        if due := w.done(s, "full_M", stage):
                            act.wait_ge(s.sem["full_M"], due.count)
                        fn(u.xT[:, :], M[:, 0:GT], ACT.Copy).then_inc(s.sem["free_M"], 1)
                    elif name == "logit":
                        if due := w.done(s, "free_M", stage):
                            act.wait_ge(s.sem["free_M"], due.count)
                        fn(u.lg[:, :, :], u.lg[:, :, :], ACT.Exp).then_inc(s.sem["lexp"], 1)
                    elif name == "w1":
                        bank = "ST"[b % 2]
                        if due := w.done(s, "full_" + bank, stage):
                            act.wait_ge(s.sem["full_" + bank], due.count)
                        if due := w.same_kind(s, "hid", stage, 2):
                            act.wait_ge(s.sem["hid"], due.count)
                        fn(u.hr[:, b % 2, :], s.bank[bank][:, :], ACT.Relu).then_inc(s.sem["free_" + bank], 1)
                    elif name == "g1":
                        if due := w.done(s, "full_M", stage):
                            act.wait_ge(s.sem["full_M"], due.count)
                        fn(u.gh[:, :], M[:, 0:GT], ACT.Relu, bias=V("gb1")).then_inc(s.sem["free_M"], 1)
                    elif name == "u":
                        if due := w.done(s, "full_M", stage):
                            act.wait_ge(s.sem["full_M"], due.count)
                        fn(u.us[:, b, :], M[:, :], ACT.Copy).then_inc(s.sem["free_M"], 1)
                    elif name == "gelu":
                        if due := w.done(s, "zcub", stage):
                            act.wait_ge(s.sem["zcub"], due.count)
                        fn(u.zz[:, b, :], u.zz[:, b, :], ACT.Tanh, scale=8 * GELU_A * GELU_C).then_inc(s.sem["tanh"], 1)
                    elif name == "store":
                        if due := w.done(s, "x", ("ln2", l, 0, k)):
                            act.wait_ge(s.sem["x"], due.count)
                        act.dma_start(out_d[t, s.number, k], u.x[:, :, :]).then_inc(s.sem[f"stored{k}"], 16)

            act.wait_ge(loadedp, LOADEDP)
            fn(dtmp[:, 0, :], V("gamma"), ACT.Exp, scale=-1.0).then_inc(gexp, 1)
            act.wait_ge(nsig, 3)
            for j in range(4):
                dst = decay.rearrange("p (a j k) -> p a j k", a=2, j=4)[:, :, j, :]
                last = fn(dst, dst, ACT.Exp, scale=dtmp[:, 2, j:j + 1])
            last.then_inc(decayed, 1)
            act.wait_ge(zeroed, ZEROED)
            program(act, emit)
            for s in streams:
                for k in range(PAIR):
                    act.wait_ge(s.sem[f"stored{k}"], 16 * (STEPS + 1))

        @block.vector
        def _(dve):
            v = nc.vector
            tt = v.tensor_tensor
            ts = v.tensor_scalar
            stt = v.scalar_tensor_tensor

            def take_wait():
                v.memset(scratch[:, :], 0.0)

            def emit(t, w):
                for who, stage in order:
                    s = streams[who]
                    name, l, b, k = stage
                    u = s.own[k]
                    M, S, T, Y = (s.bank[m] for m in "MSTY")
                    P = u.P[:, b % 2, :]
                    if name == "mask":
                        if due := w.done(s, f"loaded_mask{k}", ("load", "in", 0, k)):
                            dve.wait_ge(s.sem[f"loaded_mask{k}"], due.count)
                        ts(u.mW2[:, 0, GT:2 * GT], u.mask_i, 0, -1e9 * ROOT8, ALU.is_equal, ALU.mult)\
                            .then_inc(s.sem["keep"], 1)
                        ts(u.keep, u.mask_i, 0, None, ALU.not_equal).then_inc(s.sem["keep"], 1)
                    elif name == "proj":
                        src = T[:, 0:GT]
                        if l == "r1":
                            dve.wait_ge(loaded1, LOADED1)
                            dve.wait_ge(loaded2, LOADED2)
                        if due := w.done(s, "full_M" if l == "r1" else "full_T", stage):
                            dve.wait_ge(s.sem["full_M" if l == "r1" else "full_T"], due.count)
                        if l == "r1":
                            cos = C1("cos").unsqueeze(1).to_broadcast([128, GB, SEQ])
                            sin = C1("sin").unsqueeze(1).to_broadcast([128, GB, SEQ])
                            for n, bias in ((0, "bq_r"), (1, "bk_r")):
                                last = stt(out=u.rt1[:, n, :].rearrange("p (b s) -> p b s", b=GB),
                                           in0=M[:, GT * n:GT * n + GT].rearrange("p (b s) -> p b s", b=GB),
                                           scalar=V(bias), in1=cos, op0=ALU.add, op1=ALU.mult)
                            last.then_inc(s.sem["free_M"], 1)
                            if due := w.done(s, "full_T", stage):
                                dve.wait_ge(s.sem["full_T"], due.count)
                            for n in range(2):
                                last = stt(out=u.rt2[:, n, :].rearrange("p (b s) -> p b s", b=GB),
                                           in0=T[:, GT * n:GT * n + GT].rearrange("p (b s) -> p b s", b=GB),
                                           scalar=brot[:, n:n + 1], in1=sin, op0=ALU.add, op1=ALU.mult)
                            last.then_inc(s.sem["free_T"], 1)
                            if due := w.done(s, "rope", stage):
                                dve.wait_ge(s.sem["rope"], due.count)
                            src = u.rt1[:, 1, :]
                        elif l == "c0":
                            if due := w.done(s, "keep", ("mask", "in", 0, k)):
                                dve.wait_ge(s.sem["keep"], due.count)
                            tt(u.kz, src, u.keep, ALU.mult).then_inc(s.sem["free_T"], 1)
                            if due := w.done(s, "free_T", stage):
                                dve.wait_ge(s.sem["free_T"], due.count)
                            src = u.kz
                        bias = {"s1": bk_s, "c1": bk_c}.get(l)
                        for j in range(4):
                            last = ts(u.K[:, :, j, :], src.rearrange("p (b k) -> p b k", b=GB), C("jmask")[:, j:j + 1],
                                      None if bias is None else bias[:, j:j + 1], ALU.mult, *([] if bias is None else [ALU.add]))
                        last.then_inc(s.sem["blocks" if l in ("r1", "c0") else "free_T"], 1)
                    elif name == "projv":
                        if due := w.done(s, "full_M", stage):
                            dve.wait_ge(s.sem["full_M"], due.count)
                        for j2 in range(2):
                            p = slice(64 * j2, 64 * j2 + 64)
                            i = M[p, 0:GT].rearrange("p (m a d) -> p m a d", a=2, d=HD)
                            o = u.V[p, :, :, :, :, :].rearrange("p m a b c d -> p m (a b) c d")[:, :, 0:4:3, j2, :]
                            if l in ("r1", "s1", "c1"):
                                bv = r_at["bv_" + l[0]][0] + 64 * j2
                                rowv = row[p, bv:bv + 64].unsqueeze(1).to_broadcast([64, GB, 64])
                                for jp in range(2):
                                    last = tt(o[:, :, jp, :].rearrange("p (b g) d -> p b g d", b=GB),
                                              i[:, :, jp, :].rearrange("p (b g) d -> p b g d", b=GB),
                                              rowv.rearrange("p b (g a d) -> p b g a d", a=2, d=HD)[:, :, :, jp, :], ALU.add)
                            else:
                                last = v.tensor_copy(o, i)
                        last.then_inc(s.sem["free_M"], 1)
                    elif name == "gate":
                        if due := w.done(s, "full_Y", stage):
                            dve.wait_ge(s.sem["full_Y"], due.count)
                        tt(u.gz[:, :, :], Y[:, 0:GT].rearrange("p (t d) -> p t d", t=TT),
                           R("bg_r").unsqueeze(1).to_broadcast([128, TT, D]), ALU.add).then_inc(s.sem["free_Y"], 1)
                        if due := w.done(s, "gtanh", stage):
                            dve.wait_ge(s.sem["gtanh"], due.count)
                        stt(out=u.gate[:, :, :], in0=u.gate[:, :, :], scalar=1.0, in1=u.gz[:, :, :], op0=ALU.add, op1=ALU.mult)\
                            .then_inc(s.sem["gate"], 1)
                    elif name == "qk":
                        if due := w.done(s, "full_S", stage):
                            dve.wait_ge(s.sem["full_S"], due.count)
                        if due := w.same_kind(s, "full_T", ("tp", l, b, k), 2):
                            dve.wait_ge(s.sem["full_T"], due.count)
                        mx = u.mx[:, b % 2, :]
                        rows8 = "p (a k) -> p a k"
                        if l == "r1":
                            tt(P, S[:, :], decay, ALU.mult).then_inc(s.sem["free_S"], 1)
                            continue
                        if l == "c1":
                            v.tensor_reduce(mx, S[:, :].rearrange(rows8, k=SEQ), AX.X, ALU.max).then_inc(s.sem["rowmax"], 1)
                            if due := w.done(s, "rowmax", stage):
                                dve.wait_ge(s.sem["rowmax"], due.count)
                            tt(P.rearrange(rows8, k=SEQ), S[:, :].rearrange(rows8, k=SEQ), mx.unsqueeze(2).to_broadcast([128, 8, SEQ]),
                               ALU.subtract).then_inc(s.sem["free_S"], 1)
                            continue
                        if l == "c0":
                            tt(P.rearrange(rows8, k=SEQ), S[:, :].rearrange(rows8, k=SEQ),
                               u.mbias[:, b, :].unsqueeze(1).to_broadcast([128, 8, SEQ]), ALU.add).then_inc(s.sem["free_S"], 1)
                        else:
                            tt(P, S[:, :], C("causal"), ALU.add).then_inc(s.sem["free_S"], 1)
                        if due := w.done(s, "free_S", stage):
                            dve.wait_ge(s.sem["free_S"], due.count)
                        v.tensor_reduce(mx, P.rearrange(rows8, k=SEQ), AX.X, ALU.max).then_inc(s.sem["rowmax"], 1)
                    elif name == "pv" and l != "r1":
                        if due := w.done(s, "full_Y", ("pv", l, b, k)):
                            dve.wait_ge(s.sem["full_Y"], due.count)
                        v.reciprocal(u.rz[:, b % 2, :], Y[:, SEQ:2 * SEQ]).then_inc(s.sem["recip"], 1)
                        if due := w.done(s, "recip", stage):
                            dve.wait_ge(s.sem["recip"], due.count)
                        tt(u.yT[:, SEQ * b:SEQ * b + SEQ], Y[:, 0:SEQ], u.rz[:, b % 2, :], ALU.mult)\
                            .then_inc(s.sem["free_Y"], 1)
                    elif name == "oproj" and l != "s1":
                        if due := w.done(s, "full_M", stage):
                            dve.wait_ge(s.sem["full_M"], due.count)
                        new = M[:, 0:GT].rearrange("p (t d) -> p t d", t=TT)
                        if l == "r1":
                            if due := w.done(s, "gate", ("gate", l, 0, k)):
                                dve.wait_ge(s.sem["gate"], due.count)
                            stt(out=u.r[:, :, :], in0=new, scalar=0.5, in1=u.gate[:, :, :], op0=ALU.mult, op1=ALU.mult)\
                                .then_inc(s.sem["free_M"], 1)
                            if due := w.done(s, "free_M", stage):
                                dve.wait_ge(s.sem["free_M"], due.count)
                            if due := w.done(s, "x", ("ln2", "m0", 0, k)):
                                dve.wait_ge(s.sem["x"], due.count)
                            tt(u.r[:, :, :], u.r[:, :, :], u.x[:, :, :], ALU.add).then_inc(s.sem["resid"], 1)
                        else:
                            if due := w.done(s, "xb", ("xb", {"a0": "in", "c0": "a0", "c1": "r1"}[l], 0, k)):
                                dve.wait_ge(s.sem["xb"], due.count)
                            tt(u.r[:, :, :], new, u.xb[:, :, :], ALU.add).then_inc(s.sem["free_M"], 1)
                    elif name == "ln1":
                        if l == "r1":
                            if due := w.done(s, "resid", ("oproj", l, 0, k)):
                                dve.wait_ge(s.sem["resid"], due.count)
                        elif l == "m0":
                            if due := w.done(s, "free_M", ("w2", l, E0 - 1, k)):
                                dve.wait_ge(s.sem["free_M"], due.count)
                        elif l == "f1":
                            if due := w.done(s, "free_M", ("out", l, 1, k)):
                                dve.wait_ge(s.sem["free_M"], due.count)
                        else:
                            if due := w.done(s, "free_M", ("oproj", l, 0, k)):
                                dve.wait_ge(s.sem["free_M"], due.count)
                        for t in range(TT):
                            last = v.bn_stats(u.st[:, t, :], u.r[:, t, :])
                        last.then_inc(s.sem["stats"], 1)
                        if due := w.done(s, "stats", stage):
                            dve.wait_ge(s.sem["stats"], due.count)
                        take_wait()
                        for t in range(TT):
                            last = v.bn_aggr(u.mv[:, t, :], u.st[:, t, :])
                        last.then_inc(s.sem["moments"], 1)
                        if due := w.done(s, "moments", stage):
                            dve.wait_ge(s.sem["moments"], due.count)
                        ts(u.ve[:, :], u.mv[:, :, 1], EPS, None, ALU.add).then_inc(s.sem["vareps"], 1)
                    elif name == "ln2":
                        if due := w.done(s, "rstd", ("ln1", l, 0, k)):
                            dve.wait_ge(s.sem["rstd"], due.count)
                        for t in range(TT):
                            last = ts(u.x[:, t, :], u.r[:, t, :], u.mv[:, t, 0:1], u.rstd[:, t:t + 1], ALU.subtract, ALU.mult)
                        last.then_inc(s.sem["x"], 1)
                    elif name == "logit":
                        if due := w.done(s, "full_M", stage):
                            dve.wait_ge(s.sem["full_M"], due.count)
                        i = M[:, 0:TT * E0].rearrange("p (t e) -> p t e", t=TT)
                        v.tensor_reduce(u.lmx[:, :], i, AX.X, ALU.max).then_inc(s.sem["lmax"], 1)
                        if due := w.done(s, "lmax", stage):
                            dve.wait_ge(s.sem["lmax"], due.count)
                        tt(u.lg[:, :, :], i, u.lmx[:, :].unsqueeze(2).to_broadcast([128, TT, E0]), ALU.subtract).then_inc(s.sem["free_M"], 1)
                    elif name == "route":
                        step = [0]

                        def then(ins):
                            step[0] += 1
                            ins.then_inc(s.sem["routed"], 1)
                            if due := w.step(s, "routed", stage, ROUTE_STEPS - step[0]):
                                dve.wait_ge(s.sem["routed"], due.count)

                        if due := w.done(s, "lexp", ("logit", l, 0, k)):
                            dve.wait_ge(s.sem["lexp"], due.count)
                        then(v.tensor_reduce(u.lsum[:, :], u.lg[:, :, :], AX.X, ALU.add))
                        then(v.reciprocal(u.lrec[:, :], u.lsum[:, :]))
                        then(tt(u.prob[:, :, :], u.lg[:, :, :], u.lrec[:, :].unsqueeze(2).to_broadcast([128, TT, E0]), ALU.mult))
                        take_wait()
                        for t in range(TT):
                            last = v.max(out=u.top[:, t, :], in_=u.prob[:, t, :])
                        then(last)
                        take_wait()
                        for t in range(TT):
                            last = v.max_index(u.topi[:, t, :], u.top[:, t, :], u.prob[:, t, :])
                        then(last)
                        v.tensor_copy(u.topf[:, :, :], u.topi[:, :, 0:2])
                        then(tt(u.wsum[:, :], u.top[:, :, 0], u.top[:, :, 1], ALU.add))
                        then(ts(u.wrec[:, :], u.wsum[:, :], 1e-8, None, ALU.add))
                        then(v.reciprocal(u.wsum[:, :], u.wrec[:, :]))
                        then(tt(u.wn[:, :, :], u.top[:, :, 0:2], u.wsum[:, :].unsqueeze(2).to_broadcast([128, TT, 2]), ALU.mult))
                        for t in range(TT):
                            for k in range(2):
                                last = ts(u.pick[:, t, k, :], C("iota"), u.topf[:, t, k:k + 1], u.wn[:, t, k:k + 1], ALU.is_equal, ALU.mult)
                        then(last)
                        tt(u.comb[:, :, :], u.pick[:, :, 0, :], u.pick[:, :, 1, :], ALU.add).then_inc(s.sem["comb"], 1)
                    elif name == "w2":
                        bank = "YM"[b % 2]
                        if due := w.done(s, "full_" + bank, stage):
                            dve.wait_ge(s.sem["full_" + bank], due.count)
                        if due := w.done(s, "comb", ("route", l, 0, k)):
                            dve.wait_ge(s.sem["comb"], due.count)
                        if b:
                            if due := w.done(s, "free_" + "YM"[1 - b % 2], ("w2", l, b - 1, k)):
                                dve.wait_ge(s.sem["free_" + "YM"[1 - b % 2]], due.count)
                        else:
                            if due := w.done(s, "x", ("ln2", "c0", 0, k)):
                                dve.wait_ge(s.sem["x"], due.count)
                        for t in range(TT):
                            last = stt(out=u.r[:, t, :], in0=s.bank[bank][:, D * t:D * t + D], scalar=u.comb[:, t, b:b + 1],
                                       in1=(u.r if b else u.x)[:, t, :], op0=ALU.mult, op1=ALU.add)
                        last.then_inc(s.sem["free_" + bank], 1)
                    elif name == "g1":
                        if due := w.done(s, "free_M", stage):
                            dve.wait_ge(s.sem["free_M"], due.count)
                        v.tensor_reduce(u.hm[:, :], u.gh[:, :].rearrange("p (b k) -> p b k", k=SEQ), AX.X, ALU.add).then_inc(s.sem["hmean"], 1)
                    elif name == "gcol":
                        if due := w.done(s, "full_M", stage):
                            dve.wait_ge(s.sem["full_M"], due.count)
                        for n in range(2):
                            last = ts(u.gcol[:, n, :], M[:, GB * n:GB * n + GB], 1.0 / SEQ, V("gb2")[:, n:n + 1], ALU.mult, ALU.add)
                        last.then_inc(s.sem["free_M"], 1)
                    elif name == "mb":
                        if due := w.done(s, "full_M", stage):
                            dve.wait_ge(s.sem["full_M"], due.count)
                        i = M[:, 0:TT * FT * 2].rearrange("p (t f b) -> p t f b", t=TT, f=FT)
                        for t2 in range(TT):
                            last = stt(out=u.mb[:, t2, :, :], in0=i[:, t2, :, :], scalar=0.5,
                                       in1=b1h[:, :].unsqueeze(2).to_broadcast([128, FT, 2]), op0=ALU.mult, op1=ALU.add)
                        last.then_inc(s.sem["free_M"], 1)
                    elif name == "gen1":
                        if due := w.done(s, "full_S", stage):
                            dve.wait_ge(s.sem["full_S"], due.count)
                        tt(u.mW1[b % 2], S[:, :], base1[:, :], ALU.add).then_inc(s.sem["free_S"], 1)
                    elif name == "gen2":
                        if due := w.done(s, "full_T", stage):
                            dve.wait_ge(s.sem["full_T"], due.count)
                        tt(u.mW2[:, b % 2, :], T[:, :], base2[:, :], ALU.add)\
                            .then_inc(s.sem["free_T"], 1)
                    elif name == "ut":
                        if due := w.done(s, "full_Y", stage):
                            dve.wait_ge(s.sem["full_Y"], due.count)
                        if due := w.done(s, "free_M", ("mb", l, 0, k)):
                            dve.wait_ge(s.sem["free_M"], due.count)
                        stt(out=u.z[:, b, :].rearrange("p (a k) -> p a k", k=SEQ), in0=Y[:, :].rearrange("p (a k) -> p a k", k=SEQ), scalar=0.5,
                            in1=u.mb[:, b, :, :].rearrange("p f b -> p (f b)").unsqueeze(2).to_broadcast([128, 2 * FT, SEQ]),
                            op0=ALU.mult, op1=ALU.add)\
                            .then_inc(s.sem["free_Y"], 1)
                    elif name == "gelu":
                        if due := w.done(s, "zsq", stage):
                            dve.wait_ge(s.sem["zsq"], due.count)
                        stt(out=u.zz[:, b, :], in0=u.zz[:, b, :], scalar=0.25 / GELU_A, in1=u.z[:, b, :], op0=ALU.add, op1=ALU.mult)\
                            .then_inc(s.sem["zcub"], 1)
                    elif name == "act":
                        if due := w.done(s, "tanh", ("gelu", l, b, k)):
                            dve.wait_ge(s.sem["tanh"], due.count)
                        stt(out=u.zz[:, b, :], in0=u.zz[:, b, :], scalar=1.0, in1=u.z[:, b, :], op0=ALU.add, op1=ALU.mult)\
                            .then_inc(s.sem["act"], 1)
                    elif name == "out":
                        if due := w.done(s, "full_M", stage):
                            dve.wait_ge(s.sem["full_M"], due.count)
                        if due := w.done(s, "xb", ("xb", "c1", 0, k)):
                            dve.wait_ge(s.sem["xb"], due.count)
                        tt(u.r[:, b, :], M[:, 0:D], u.xb[:, b, :], ALU.add).then_inc(s.sem["free_M"], 1)

            dve.wait_ge(loadedp, LOADEDP)
            for n, wname in ((0, "r1q"), (1, "r1k")):
                pair = W(wname).rearrange("p (i a) -> p i a", a=2)
                turned = wrot[:, n, :].rearrange("p (i a) -> p i a", a=2)
                ts(turned[:, :, 0], pair[:, :, 1], -1.0, None, ALU.mult)
                v.tensor_copy(turned[:, :, 1], pair[:, :, 0])
            for n, bname in ((0, "bqp_r"), (1, "bkp_r")):
                tt(brot[:, n:n + 1], V(bname), C1("sign"), ALU.mult)
            ts(bk_s[:, :], C("jmask"), V("bk_s"), None, ALU.mult)
            ts(bk_c[:, :], C("jmask"), V("bk_c"), None, ALU.mult)
            ts(b1h[:, :], V("b1"), 0.5, None, ALU.mult)
            dve.wait_ge(gexp, 1)
            ts(dtmp[:, 1, :], dtmp[:, 0, :], 1.0, None, ALU.add).then_inc(nsig, 1)
            dve.wait_ge(nsig, 1)
            v.reciprocal(dtmp[:, 3, :], dtmp[:, 1, :]).then_inc(nsig, 1)
            dve.wait_ge(nsig, 2)
            ts(dtmp[:, 2, :], dtmp[:, 3, :], -1.0, None, ALU.mult).then_inc(nsig, 1)
            dve.wait_ge(decayed, 1)
            ts(decay, decay, SCALE, None, ALU.mult).then_inc(made, 1)
            dve.wait_ge(made, 1)

            dve.wait_ge(loaded0, LOADED0)
            dve.wait_ge(zeroed, ZEROED)
            program(dve, emit)

        @block.gpsimd
        def _(pool):
            tt = nc.gpsimd.tensor_tensor

            def emit(t, w):
                for who, stage in order:
                    s = streams[who]
                    name, l, b, k = stage
                    u = s.own[k]
                    if name == "xb":
                        if l == "in":
                            if due := w.done(s, f"loaded_x{k}", ("load", "in", 0, k)):
                                pool.wait_ge(s.sem[f"loaded_x{k}"], due.count)
                            if due := w.last_group(s, "x", ("ln2", "f1", 0, k)):
                                pool.wait_ge(s.sem["x"], due.count)
                        else:
                            if due := w.done(s, "x", ("ln2", l, 0, k)):
                                pool.wait_ge(s.sem["x"], due.count)
                        bias = {"in": "bo_a", "a0": "bo_c0", "r1": "bo_c1", "c1": "b2"}[l]
                        tt(u.xb[:, :, :], u.x[:, :, :], R(bias).unsqueeze(1).to_broadcast([128, TT, D]), ALU.add)\
                            .then_inc(s.sem["xb"], 1)
                    elif name == "proj" and l == "r1":
                        if due := w.done(s, "free_M", stage):
                            pool.wait_ge(s.sem["free_M"], due.count)
                        if due := w.done(s, "free_T", stage):
                            pool.wait_ge(s.sem["free_T"], due.count)
                        tt(u.rt1[:, :, :], u.rt1[:, :, :], u.rt2[:, :, :], ALU.add).then_inc(s.sem["rope"], 1)
                    elif name == "qk" and l in MASKED:
                        if due := w.done(s, "rowmax", stage):
                            pool.wait_ge(s.sem["rowmax"], due.count)
                        P = u.P[:, b % 2, :].rearrange("p (a k) -> p a k", k=SEQ)
                        tt(P, P, u.mx[:, b % 2, :].unsqueeze(2).to_broadcast([128, 8, SEQ]), ALU.subtract).then_inc(s.sem["shifted"], 1)
                    elif name == "ln1":
                        if due := w.done(s, "vareps", stage):
                            pool.wait_ge(s.sem["vareps"], due.count)
                        tt(u.rstd[:, :], u.ve[:, :], C("neghalf"), ALU.pow).then_inc(s.sem["rstd"], 1)
                    elif name == "w1":
                        if due := w.done(s, "free_" + "ST"[b % 2], stage):
                            pool.wait_ge(s.sem["free_" + "ST"[b % 2]], due.count)
                        bank = "YM"[b % 2]
                        if due := w.same_kind(s, "full_" + bank, ("w2", l, b, k), 2):
                            pool.wait_ge(s.sem["full_" + bank], due.count)
                        tt(u.hid[:, b % 2, :], u.hr[:, b % 2, :], u.hr[:, b % 2, :], ALU.mult).then_inc(s.sem["hid"], 1)
                    elif name == "gcol":
                        if due := w.done(s, "free_M", stage):
                            pool.wait_ge(s.sem["free_M"], due.count)
                        o = u.gdiag[:, :, :, :].rearrange("p n b k -> p (n b) k")
                        tt(o, C1("id32").unsqueeze(1).to_broadcast([128, 2 * GB, 32]),
                           u.gcol[:, :, :].rearrange("p n b -> p (n b)").unsqueeze(2).to_broadcast([128, 2 * GB, 32]), ALU.mult)\
                            .then_inc(s.sem["gdiag"], 1)
                    elif name == "gelu":
                        if due := w.done(s, "free_Y", ("ut", l, b, k)):
                            pool.wait_ge(s.sem["free_Y"], due.count)
                        if due := w.same_kind(s, "act", ("act", l, b, k), 2):
                            pool.wait_ge(s.sem["act"], due.count)
                        tt(u.zz[:, b, :], u.z[:, b, :], u.z[:, b, :], ALU.mult).then_inc(s.sem["zsq"], 1)

            for s in streams:
                for name, count in s.tally.total.items():
                    pool.nop().then_inc(s.sem[name], count)
            for buf in [b for s in streams for u in s.own for b in (u.Q, u.V)] + [tb1_sb, tb2_sb]:
                nc.gpsimd.memset(buf[:], 0.0).then_inc(zeroed, 1)
            pool.wait_ge(loaded0, LOADED0)
            pool.wait_ge(loadedp, LOADEDP)
            pool.wait_ge(loaded1, LOADED1)
            program(pool, emit)


def _lay_out(i):
    f = lambda a: np.ascontiguousarray(np.asarray(a))

    def parity(w):
        return w.reshape(w.shape[:-1] + (H // 2, 2, HD)).swapaxes(-3, -2).reshape(w.shape)

    heads = lambda w: np.asarray(w).transpose(1, 0, 2).reshape(D, D)
    T = lambda name: np.asarray(i[name]).T
    sq = {"a0q": T("L0_attn_Wq"), "a0k": T("L0_attn_Wk"), "a0v": parity(T("L0_attn_Wv")), "a0o": T("L0_attn_Wo"),
          "c0q": T("L0_xattn_Wq"), "c0k": T("L0_xattn_Wk"), "c0v": parity(T("L0_xattn_Wv")), "c0o": T("L0_xattn_Wo"),
          "r1q": T("L1_attn_Wq"), "r1k": T("L1_attn_Wk"), "r1v": parity(T("L1_attn_Wv")), "r1g": T("L1_attn_Wg"),
          "s1q": heads(i["L1_xattn_Wq1"]), "s1k": heads(i["L1_xattn_Wk1"]), "s1v": parity(heads(i["L1_xattn_Wv1"])),
          "s1o": np.asarray(i["L1_xattn_Wo1"]),
          "c1q": heads(i["L1_xattn_Wq2"]), "c1k": heads(i["L1_xattn_Wk2"]), "c1v": parity(heads(i["L1_xattn_Wv2"])),
          "c1o": np.asarray(i["L1_xattn_Wo2"]), "f1g": T("L1_ffn_gate_w1")}
    p = np.arange(128)
    q = np.arange(2)[None, :, None, None] * 32 + (p % 32)[:, None, None, None]
    k = np.arange(SEQ)[None, None, None, :]
    full = np.zeros((128, 2, 4, SEQ), np.float32)
    ones = np.zeros((128, 2, 2, 2, HD), np.float32)
    for jp in range(2):
        for j2 in range(2):
            ones[64 * j2:64 * j2 + 64, jp, jp, j2] = 1.0
    con = {"ident": np.eye(128), "causal": (full + np.where(k <= q, 0.0, MINUS)).reshape(128, 512),
           "jmask": (p[:, None] // HD) % 4 == np.arange(4)[None, :], "ones": ones.reshape(128, 64),
           "iota": np.broadcast_to(np.arange(8), (128, 8)), "neghalf": np.full((128, 2), -0.5)}
    inv = (1.0 / 10000.0 ** (np.arange(0, HD, 2, dtype=np.float32) / HD)).astype(np.float32)
    ang = (np.arange(SEQ, dtype=np.float32)[None, :] * inv[(p % HD) % (HD // 2)][:, None]).astype(np.float32)
    con1 = {"cos": np.cos(ang), "sin": np.sin(ang), "diff": (full + np.maximum(q - k, 0)).reshape(128, 512),
            "id32": p[:, None] % 32 == np.arange(32)[None, :], "sign": np.where(p % 2 == 0, -1.0, 1.0)[:, None]}
    pack = lambda parts, names: f(np.concatenate([np.asarray(parts[n]).astype(np.float32).reshape(-1, w) for n, w in names.items()], axis=1))
    c = lambda name: np.asarray(i[name]).reshape(-1, 1)
    gb2 = np.asarray(i["L1_ffn_gate_b2"]).reshape(2, 4)
    col = {"bq_r": c("L1_attn_bq"), "bk_r": c("L1_attn_bk"), "bqp_r": c("L1_attn_bq")[p ^ 1], "bkp_r": c("L1_attn_bk")[p ^ 1],
           "bq_s": c("L1_xattn_bq1"), "bk_s": c("L1_xattn_bk1"), "bo_s": c("L1_xattn_bo1"), "bq_c": c("L1_xattn_bq2"),
           "bk_c": c("L1_xattn_bk2"), "gb1": c("L1_ffn_gate_b1"), "b1": np.asarray(i["L1_ffn_b1"]).reshape(FT, 128).T,
           "gb2": gb2.T[p // 32], "gamma": np.asarray(i["L1_attn_gamma"]).reshape(4, 4)[p // 32]}
    r = lambda name: np.asarray(i[name]).reshape(1, -1)
    row = {"bo_a": r("L0_attn_bo"), "bo_c0": r("L0_xattn_bo"), "bg_r": r("L1_attn_bg"), "bo_c1": r("L1_xattn_bo2"),
           "b2": r("L1_ffn_b2"), "bv_r": parity(r("L1_attn_bv")), "bv_s": parity(r("L1_xattn_bv1")), "bv_c": parity(r("L1_xattn_bv2"))}
    same = lambda parts, names: f(np.concatenate([parts[n] for n in names], axis=1))
    x, cx = np.asarray(i["x"]).reshape(-1, D), np.asarray(i["ctx_1024"]).reshape(-1, D)
    tw1 = np.asarray(i["L1_ffn_TW1"]).reshape(2, 4, HID1, 4, 32)
    tw2 = np.asarray(i["L1_ffn_TW2"]).reshape(2, 4, D, FT, 4, 32)
    return {
        "x": f(x), "xT": f(x.T), "ctxT": f(cx.T), "mask": f(i["mask_BxS2_ik0"]),
        "squares": f(np.stack([sq[n] for n in SQUARES], axis=1)),
        "consts": pack(con, CONSTS), "consts1": pack(con1, CONSTS1),
        "cols": same(col, COLS), "rows": same(row, ROWS).reshape(-1),
        "moe_g": f(i["L0_ffn_Wg"]), "moe_w1": f(np.asarray(i["L0_ffn_W1"]).transpose(1, 0, 2)),
        "moe_w2": f(np.asarray(i["L0_ffn_W2"]).reshape(2 * E0, 128, D).transpose(1, 0, 2)),
        "gw2r": f(np.repeat(np.asarray(i["L1_ffn_gate_w2"]).T.reshape(128, 2, 4), 32, axis=2)),
        "ff_w1": f(T("L1_ffn_W1")), "ff_w2": f(T("L1_ffn_W2").reshape(FT, 128, D).transpose(1, 0, 2).reshape(128, HID1)),
        "ff_tw1": f(tw1.transpose(1, 4, 3, 0, 2).reshape(128, 4, 2, HID1)),
        "ff_tw2": f(tw2.transpose(1, 5, 4, 0, 3, 2).reshape(128, 4, 2, HID1)),
        "ff_tb1": f(np.asarray(i["L1_ffn_Tb1"]).reshape(2, 4, HID1).transpose(1, 0, 2)),
        "ff_tb2": f(np.asarray(i["L1_ffn_Tb2"]).reshape(2, 4, D).transpose(1, 0, 2)),
    }


def kernel(**inputs):
    import concourse.bacc as bacc
    from concourse.bass_utils import run_bass_kernel_spmd

    nc = bacc.Bacc("TRN2", target_bir_lowering=False, num_devices=1)
    arrays = {f"in_{k}": a for k, a in _lay_out(inputs).items()}
    args = [nc.dram_tensor(k, a.shape, mybir.dt.from_np(a.dtype), kind="ExternalInput").ap() for k, a in arrays.items()]
    out = nc.dram_tensor("out_dram", (B * SEQ, D), F32, kind="ExternalOutput").ap()
    decoder_kernel(nc, *args, out)
    got = run_bass_kernel_spmd(nc, [arrays], core_ids=[0]).results[0]["out_dram"]
    return got.reshape(B, SEQ, D)
```

```python
from contextlib import ExitStack

import numpy as np
import concourse.bass as bass
from concourse import mybir

ALU = mybir.AluOpType
ACT = mybir.ActivationFunctionType
AX = mybir.AxisListType
F32 = mybir.dt.float32
I32 = mybir.dt.int32
U32 = mybir.dt.uint32

B, SEQ, D, H = 32, 64, 128, 16
HD = D // H
GB = 4
GT = GB * SEQ
TT = GT // 128
PAIR = 2
STREAMS = 2
STEPS = B // (GB * PAIR * STREAMS)
E0, HID0 = 8, 256
E1, HID1 = 8, 512
FT = HID1 // 128
ROOT8 = float(np.sqrt(np.float32(HD)))
SCALE = 1.0 / ROOT8
EPS = 1e-5
GELU_A, GELU_C = 0.044715, float(np.sqrt(2.0 / np.pi))
MINUS = -1e30
MASKED = ("a0", "c0", "s1")
CAUSAL = ("a0", "s1")
ROUTE_STEPS = 10

SQUARES = ["a0q", "a0k", "a0v", "a0o", "c0q", "c0k", "c0v", "c0o", "r1q", "r1k", "r1v", "r1g",
           "s1q", "s1k", "s1v", "s1o", "c1q", "c1k", "c1v", "c1o", "f1g"]
N_SQ0 = 8
CONSTS = {"ident": 128, "causal": 512, "jmask": 4, "ones": 64, "iota": 8, "neghalf": 2}
CONSTS1 = {"cos": 64, "sin": 64, "diff": 512, "id32": 32, "sign": 1}
COLS = {"bq_r": 1, "bk_r": 1, "bqp_r": 1, "bkp_r": 1, "bq_s": 1, "bk_s": 1, "bo_s": 1, "bq_c": 1,
        "bk_c": 1, "gb1": 1, "b1": 4, "gb2": 2, "gamma": 4}
ROWS = {"bo_a": 128, "bo_c0": 128, "bg_r": 128, "bo_c1": 128, "b2": 128, "bv_r": 128, "bv_s": 128,
        "bv_c": 128}


def places(widths):
    at, out = 0, {}
    for name, w in widths.items():
        out[name] = (at, at + w)
        at += w
    return out, at


def attention(l):
    o = [("proj", l, 0), ("projv", l, 0), ("qk", l, 0), ("qk", l, 1), ("tp", l, 0)]
    if l == "r1":
        o.insert(2, ("gate", l, 0))
    o += [("qk", l, 2), ("pv", l, 0), ("tp", l, 1), ("qk", l, 3), ("pv", l, 1),
          ("tp", l, 2), ("pv", l, 2), ("tp", l, 3), ("pv", l, 3), ("oproj", l, 0)]
    if l == "s1":
        return o
    o += [("ln1", l, 0), ("ln2", l, 0), ("xt", l, 0)]
    return o + ([] if l == "c0" else [("xb", l, 0)])


def experts():
    o = [("logit", "m0", 0), ("w1", "m0", 0), ("route", "m0", 0), ("w1", "m0", 1)]
    for e in range(E0):
        o.append(("w2", "m0", e))
        if e + 2 < E0:
            o.append(("w1", "m0", e + 2))
    return o + [("ln1", "m0", 0), ("ln2", "m0", 0), ("xt", "m0", 0)]


def feedforward():
    f = "f1"
    return [("g1", f, 0), ("gcol", f, 0), ("mb", f, 0), ("gen1", f, 0), ("gen1", f, 1), ("u", f, 0), ("gen2", f, 0),
            ("ut", f, 0), ("gelu", f, 0), ("gen2", f, 1), ("gen1", f, 2), ("act", f, 0), ("gen1", f, 3), ("u", f, 1),
            ("out", f, 0), ("gen2", f, 2), ("ut", f, 1), ("gelu", f, 1), ("gen2", f, 3), ("act", f, 1), ("out", f, 1),
            ("ln1", f, 0), ("ln2", f, 0), ("store", f, 0)]


STAGES = ([("load", "in", 0), ("xb", "in", 0)] + attention("a0") + [("mask", "in", 0)] + attention("c0") + experts()
          + attention("r1") + attention("s1") + attention("c1") + feedforward())


def work(stage):
    s, l, b = stage
    before = {"c0": ("xt", "a0", 0), "m0": ("xt", "c0", 0), "r1": ("xt", "m0", 0), "s1": ("xt", "r1", 0),
              "c1": ("oproj", "s1", 0), "f1": ("xt", "c1", 0)}
    src = [before[l]] if l in before else []
    on = lambda *names: [(n, l, i) for n, i in names]

    if s == "load":
        return [("SP", 1, [], [], None, None)]
    if s == "mask":
        return [("DVE", 540, [], [("load", l, 0)], None, None)]
    if s == "xb":
        return [("Pool", 680, [], [("load" if l == "in" else "ln2", l, 0)], None, None)]
    if s == "proj":
        if l == "r1":
            return [("PE", 860, [], src, "M", None), ("PE", 860, [], src, "T", None), ("DVE", 790, [0], [], None, "M"),
                    ("DVE", 790, [1], [], None, "T"), ("Pool", 1220, [2, 3], [], None, None), ("ACT", 2830, [4], [], None, None)]
        masked = [("DVE", 340, [1], [("mask", "in", 0)], None, "T"), ("ACT", 1600, [3], [], None, None)]
        return [("PE", 430, [], src, "M", None), ("PE", 430, [], src, "T", None), ("ACT", 1430 if l in ("s1", "c1") else 1060, [0], [], None, "M")] + (
            masked if l == "c0" else [("ACT", 1800 if l in ("s1", "c1") else 1430, [1], [], None, "T")])
    if s == "projv":
        return [("PE", 560, [], src + on(("proj", 0)), "M", None), ("DVE", 660 if l in ("a0", "c0") else 810, [0], [], None, "M")]
    if s == "gate":
        return [("PE", 440, [], src + on(("proj", 0)), "Y", None), ("DVE", 340, [0], [], None, "Y"), ("ACT", 320, [1], [], None, None),
                ("DVE", 350, [2], [], None, None)]
    if s == "qk":
        first = on(("proj", 0)) + (on(("tp", b - 2)) if b > 1 else [])
        product = [("PE", 640 if l in CAUSAL else 860, [], first, "S", None)]
        if l == "r1":
            return product + [("DVE", 620, [0], [], None, "S")]
        if l == "c1":
            return product + [("DVE", 1330, [0], [], None, "S"), ("ACT", 520, [1], [], None, None)]
        some = 540 if l in CAUSAL else 600
        return product + [("DVE", some + (140 if l in CAUSAL and b < 2 else 0), [0], [], None, "S"), ("DVE", some, [1], [], None, None),
                          ("Pool", 900 if l in CAUSAL else 1000, [2], [], None, None), ("ACT", 510, [3], [], None, None)]
    if s == "tp":
        first = on(("qk", b)) + (on(("gate", 0)) if l == "r1" else [])
        return [("PE", 435, [], first, "T", None), ("ACT", 500, [0], on(("pv", b - 1)) if b else [], None, "T")]
    if s == "pv":
        first = on(("tp", b)) + (on(("projv", 0)) if b == 0 else [])
        if l == "r1":
            return [("PE", 370, [], first, "Y", None), ("ACT", 100, [0], [], None, "Y")]
        return [("PE", 740, [], first, "Y", None), ("DVE", 730, [0], [], None, "Y")]
    if s == "oproj":
        first = on(("pv", GB - 1))
        if l == "s1":
            return [("PE", 440, [], first, "M", None), ("ACT", 300, [0], [], None, "M")]
        if l == "r1":
            return [("PE", 220, [], first, "M", None), ("DVE", 340, [0], on(("gate", 0)), None, "M"), ("DVE", 200, [1], [], None, None)]
        return [("PE", 440, [], first, "M", None), ("DVE", 340, [0], [("xb", {"a0": "in", "c0": "a0", "c1": "r1"}[l], 0)], None, "M")]
    if s == "ln1":
        first = {"m0": on(("w2", E0 - 1)), "f1": on(("out", 0), ("out", 1))}.get(l, on(("oproj", 0)))
        return [("DVE", 420, [], first, None, None), ("DVE", 180, [0], [], None, None), ("DVE", 80, [1], [], None, None),
                ("Pool", 640, [2], [], None, None)]
    if s == "ln2":
        return [("DVE", 520, [], on(("ln1", 0)), None, None)]
    if s == "xt":
        return [("PE", 300, [], on(("ln2", 0)), "M", None), ("ACT", 260, [0], [], None, "M")]
    if s == "store":
        return [("SP", 1, [], on(("ln2", 0)), None, None)]
    if s == "logit":
        return [("PE", 260, [], src, "M", None), ("DVE", 90, [0], [], None, None), ("DVE", 90, [1], [], None, "M"),
                ("ACT", 200, [2], [], None, None)]
    if s == "route":
        return [("DVE", 2800, [], on(("logit", 0)), None, None)]
    if s == "w1":
        bank = "ST"[b % 2]
        return [("PE", 860, [], src if b < 2 else on(("w2", b - 2)), bank, None), ("ACT", 500, [0], [], None, bank),
                ("Pool", 1240, [1], [], None, None)]
    if s == "w2":
        bank = "YM"[b % 2]
        return [("PE", 880, [], on(("w1", b)), bank, None), ("DVE", 540, [0], on(("w2", b - 1) if b else ("route", 0)), None, bank)]
    if s == "g1":
        return [("PE", 430, [], src, "M", None), ("ACT", 300, [0], [], None, "M"), ("DVE", 350, [1], [], None, None)]
    if s == "gcol":
        return [("PE", 100, [], on(("g1", 0)), "M", None), ("DVE", 240, [0], [], None, "M"), ("Pool", 600, [1], [], None, None)]
    if s == "mb":
        return [("PE", 300, [], on(("gcol", 0)), "M", None), ("DVE", 170, [0], [], None, "M")]
    if s == "gen1":
        return [("PE", 1860, [], on(("gcol", 0)) + (on(("u", b // 2 - 1)) if b > 1 else []), "S", None), ("DVE", 620, [0], [], None, "S")]
    if s == "gen2":
        return [("PE", 1860, [], on(("gcol", 0)) + (on(("out", b // 2 - 1)) if b > 1 else []), "T", None), ("DVE", 620, [0], [], None, "T")]
    if s == "u":
        return [("PE", 910, [], on(("gen1", 2 * b), ("gen1", 2 * b + 1)), "M", None), ("ACT", 500, [0], [], None, "M")]
    if s == "ut":
        return [("PE", 435, [], on(("u", b), ("mb", 0)), "Y", None), ("DVE", 620, [0], [], None, "Y")]
    if s == "gelu":
        return [("Pool", 1240, [], on(("ut", b)), None, None), ("DVE", 600, [0], [], None, None), ("ACT", 500, [1], [], None, None)]
    if s == "act":
        return [("DVE", 600, [], on(("gelu", b)), None, None)]
    assert s == "out"
    return [("PE", 1400, [], on(("act", b), ("gen2", 2 * b), ("gen2", 2 * b + 1)), "M", None), ("DVE", 200, [0], [("xb", "c1", 0)], None, "M")]


HOP = {"PE": 200, "DVE": 130, "ACT": 150, "Pool": 70, "SP": 0}
BEHIND = (0, 9000, 18000, 28000)
AHEAD = 0.02
WEIGHT = {"DVE": 0.2}
CLOSE = 60000
NEAR = 2


def merged():
    groups = [(stream, k) for k in range(PAIR) for stream in range(STREAMS)]
    steps = {stage: work(stage) for stage in STAGES}
    rest, left = {}, 0
    for stage in reversed(STAGES):
        left += sum(ns for _, ns, _, _, _, _ in steps[stage])
        rest[stage] = left
    todo = {g: list(STAGES) for g in groups}
    ended = {g: {} for g in groups}
    free, bank_free, order = dict.fromkeys(("SP", "PE", "DVE", "ACT", "Pool"), 0.0), {}, []

    def place(g, stage):
        engines, banks, ends, start, held = dict(free), {}, [], None, 0
        for engine, ns, after, first, take, give in steps[stage]:
            waits = [ends[i] for i in after] + [ended[g][f] for f in first] + [bank_free.get((g[0], take), (0, "SP"))]
            at = max([engines[engine]] + [end + HOP[e] + (50 if engine == "PE" and e != "PE" else 0) for end, e in waits])
            start = at if start is None else start
            held += WEIGHT.get(engine, 0) * (at - engines[engine])
            ends.append((at + ns, engine))
            engines[engine] = at + ns
            if give:
                banks[g[0], give] = ends[-1]
        return start, held, engines, banks, max(ends)

    while any(todo.values()):
        best = None
        for i, g in enumerate(groups):
            near = todo[g][:NEAR]
            for n, stage in enumerate(near):
                if any(f in todo[g] for step in steps[stage] for f in step[3]) or any(o[0] == stage[0] for o in near[:n]):
                    continue
                start, held = place(g, stage)[:2]
                idle = start - free["PE"] - (0 if steps[stage][0][0] == "PE" else 1000)
                behind = rest[stage] - BEHIND[i] * min(1.0, rest[stage] / CLOSE)
                rank = (max(0, idle) + held - AHEAD * behind, -behind)
                if best is None or rank < best[0]:
                    best = rank, g, stage
        _, g, stage = best
        _, _, engines, banks, end = place(g, stage)
        free.update(engines)
        bank_free.update(banks)
        ended[g][stage] = end
        todo[g].remove(stage)
        order.append((g[0], stage + (g[1],)))
    return order


def signals(stage):
    s, l, b, k = stage
    if s == "load":
        return {f"loaded_{what}{k}": 16 for what in ("x", "xT", "mask", "ctx")}
    if s == "xb":
        return {"xb": 1}
    if s == "mask":
        return {"keep": 2}
    if s == "proj":
        return {"r1": {"full_M": 1, "free_M": 1, "full_T": 1, "free_T": 1, "rope": 1, "blocks": 1, "blocks_q": 1},
                "c0": {"full_M": 1, "free_M": 1, "full_T": 1, "free_T": 1, "blocks": 1}}.get(
                    l, {"full_M": 1, "free_M": 1, "full_T": 1, "free_T": 1})
    if s == "gate":
        return {"full_Y": 1, "free_Y": 1, "gtanh": 1, "gate": 1}
    if s == "qk":
        return {"full_S": 1, "free_S": 1} | ({} if l == "r1" else {"rowmax": 1, "p": 1}) | (
            {"shifted": 1} if l in MASKED else {}) | ({"zeros": 1} if l in CAUSAL and b < 2 else {})
    if s == "pv":
        return {"full_Y": 1, "free_Y": 1} | ({} if l == "r1" else {"recip": 1})
    if s == "oproj":
        return {"full_M": 1, "free_M": 1} | ({"resid": 1} if l == "r1" else {})
    if s == "ln1":
        return {"stats": 1, "moments": 1, "vareps": 1, "rstd": 1}
    if s == "ln2":
        return {"x": 1}
    if s == "logit":
        return {"full_M": 1, "lmax": 1, "free_M": 1, "lexp": 1}
    if s == "route":
        return {"routed": ROUTE_STEPS, "comb": 1}
    if s == "w1":
        return {f"full_{'ST'[b % 2]}": 1, f"free_{'ST'[b % 2]}": 1, "hid": 1}
    if s == "w2":
        return {f"full_{'YM'[b % 2]}": 1, f"free_{'YM'[b % 2]}": 1}
    if s == "g1":
        return {"full_M": 1, "free_M": 1, "hmean": 1}
    if s == "gcol":
        return {"full_M": 1, "free_M": 1, "gdiag": 1}
    if s == "gelu":
        return {"zsq": 1, "zcub": 1, "tanh": 1}
    if s == "act":
        return {"act": 1}
    if s == "store":
        return {f"stored{k}": 16}
    bank = {"projv": "M", "xt": "M", "tp": "T", "mb": "M", "gen1": "S", "gen2": "T", "u": "M", "ut": "Y", "out": "M"}[s]
    return {"full_" + bank: 1, "free_" + bank: 1}


class Tally:

    def __init__(self, stages):
        self.stages, self.total, self.events = stages, {}, {}
        for stage in stages:
            for name, k in signals(stage).items():
                self.total[name] = self.total.get(name, 0) + k
                self.events.setdefault(name, []).append((stage, self.total[name]))

    def after(self, name, stage):
        return dict(self.events[name])[stage]

    def previous(self, name, stage):
        ev = self.events[name]
        i = [s for s, _ in ev].index(stage) - 1
        return (0, ev[i][1]) if i >= 0 else (1, ev[-1][1])

    def same_kind(self, stage, lag):
        kind = [s for s in self.stages if (s[0], s[3]) == (stage[0], stage[3])]
        i = kind.index(stage) - lag
        return (0, kind[i]) if i >= 0 else (1, kind[i])


def decoder_kernel(nc, x, xT, ctxT, mask, squares, consts, consts1, cols, rows, moe_g, moe_w1, moe_w2,
                   gw2r, ff_w1, ff_w2, ff_tw1, ff_tw2, ff_tb1, ff_tb2, out):
    c_at, c_n = places(CONSTS)
    c1_at, c1_n = places(CONSTS1)
    v_at, v_n = places(COLS)
    r_at, r_n = places(ROWS)

    x_d = x.rearrange("(g w k tt p) d -> g w k p tt d", w=STREAMS, k=PAIR, tt=TT, p=128)
    xT_d = xT.rearrange("d (g w k t) -> g w k d t", w=STREAMS, k=PAIR, t=GT)
    ctxT_d = ctxT.rearrange("d (g w k t) -> g w k d t", w=STREAMS, k=PAIR, t=GT)
    mask_d = mask.rearrange("(g w k b) s -> g w k (b s)", w=STREAMS, k=PAIR, b=GB)
    out_d = out.rearrange("(g w k tt p) d -> g w k p tt d", w=STREAMS, k=PAIR, tt=TT, p=128)

    with ExitStack() as ctx:
        def sb(name, shape, dt=F32):
            return ctx.enter_context(nc.sbuf_tensor(name, shape, dt))

        def semaphore(name):
            return ctx.enter_context(nc.semaphore(name))

        sq = sb("sq", [128, len(SQUARES), 128])
        con = sb("con", [128, c_n])
        con1 = sb("con1", [128, c1_n])
        col = sb("col", [128, v_n])
        row = sb("row", [128, r_n])
        wg_sb = sb("wg_sb", [128, E0])
        w1_sb = sb("w1_sb", [128, E0, HID0])
        w2_sb = sb("w2_sb", [128, 2 * E0, D])
        gw2_sb = sb("gw2_sb", [128, 2, 128])
        base1 = sb("base1", [128, HID1])
        base2 = sb("base2", [128, HID1])
        tw1_sb = sb("tw1_sb", [128, 4, 2, HID1])
        tw2_sb = sb("tw2_sb", [128, 4, 2, HID1])
        tb1_sb = sb("tb1_sb", [128, 2, HID1])
        tb2_sb = sb("tb2_sb", [128, 2, D])
        wrot = sb("wrot", [128, 2, 128])
        brot = sb("brot", [128, 2])
        bk_s = sb("bk_s", [128, 4])
        bk_c = sb("bk_c", [128, 4])
        b1h = sb("b1h", [128, FT])
        dtmp = sb("dtmp", [128, 4, 4])

        def W(name):
            return sq[:, SQUARES.index(name), :]

        def C(name):
            a, b = c_at[name]
            return con[:, a:b]

        def C1(name):
            a, b = c1_at[name]
            return con1[:, a:b]

        def V(name, p0=0, p1=128):
            a, b = v_at[name]
            return col[p0:p1, a:b]

        decay = C1("diff")

        def R(name, p0=0, p1=128, n=128):
            a, _ = r_at[name]
            return row[p0:p1, a:a + n]

        ident = C("ident")

        def seen(a, l):
            a = a.rearrange("p (a k) -> p a k", k=SEQ)
            return [a[:, 0:4, 0:SEQ // 2], a[:, 4:8, :]] if l in CAUSAL else [a]

        class Stream:
            pass

        order = merged()

        def stream(tag, number):
            s = Stream()
            s.tag, s.number = tag, number
            s.tally = Tally([stage for stream, stage in order if stream == number])
            s.sem = {k: semaphore(f"{tag}_{k}") for k in s.tally.total}
            s.bank = {k: ctx.enter_context(nc.psum_tensor(f"{tag}_{k}", [128, 512], F32)) for k in "MSTY"}
            s.own = [group(f"{tag}{k}") for k in range(PAIR)]
            return s

        def group(tag):
            u = Stream()
            u.tag = tag
            u.Q = sb(f"{tag}_Q", [128, GB * 2, 4, 32])
            u.K = sb(f"{tag}_K", [128, GB, 4, SEQ])
            u.V = sb(f"{tag}_V", [128, GB * 4, 2, 2, 2, HD])
            u.P = sb(f"{tag}_P", [128, 2, 512])
            u.PT = sb(f"{tag}_PT", [128, 8, 2, 32])
            u.mx = sb(f"{tag}_mx", [128, 2, 8])
            u.rz = sb(f"{tag}_rz", [128, 2, SEQ])
            u.yT = sb(f"{tag}_yT", [128, GT])
            u.xb = sb(f"{tag}_xb", [128, TT, D])
            u.x = sb(f"{tag}_x", [128, TT, D])
            u.xT = sb(f"{tag}_xT", [128, GT])
            u.ctxT = sb(f"{tag}_ctxT", [128, GT])
            u.st = sb(f"{tag}_st", [128, TT, 6])
            u.mv = sb(f"{tag}_mv", [128, TT, 2])
            u.ve = sb(f"{tag}_ve", [128, TT])
            u.rstd = sb(f"{tag}_rstd", [128, TT])
            u.mW1b = sb(f"{tag}_mW1b", [128, HID1])
            u.mW2 = sb(f"{tag}_mW2", [128, 2, HID1])
            u.lg = sb(f"{tag}_lg", [128, TT, E0])
            u.lmx = sb(f"{tag}_lmx", [128, TT])
            u.lsum = sb(f"{tag}_lsum", [128, TT])
            u.lrec = sb(f"{tag}_lrec", [128, TT])
            u.prob = sb(f"{tag}_prob", [128, TT, E0])
            u.top = sb(f"{tag}_top", [128, TT, 8])
            u.topi = sb(f"{tag}_topi", [128, TT, 8], U32)
            u.topf = sb(f"{tag}_topf", [128, TT, 2])
            u.wsum = sb(f"{tag}_wsum", [128, TT])
            u.wrec = sb(f"{tag}_wrec", [128, TT])
            u.wn = sb(f"{tag}_wn", [128, TT, 2])
            u.pick = sb(f"{tag}_pick", [128, TT, 2, E0])
            u.comb = sb(f"{tag}_comb", [128, TT, E0])
            u.hm = sb(f"{tag}_hm", [128, GB])
            u.gcol = sb(f"{tag}_gcol", [128, 2, GB])
            u.mb = sb(f"{tag}_mb", [128, TT, FT, 2])
            PT = u.PT[:, :, :, :].rearrange("p a b c -> p (a b c)")
            K = u.K[:, :, :, :].rearrange("p (e b) j k -> p e (b j k)", e=2)
            u.r = u.xb
            u.xinT = u.hT = u.gh = u.yT
            u.gate = u.mW2[:, 0, 0:GT].rearrange("p (t d) -> p t d", t=TT)
            u.mbias = u.mW2[:, 0, GT:2 * GT].rearrange("p (b k) -> p b k", b=GB)
            u.keep = u.mW2[:, 1, 0:GT]
            u.mask_i = u.keep.bitcast(I32)
            u.kz = PT[:, 0:GT]
            u.hr, u.hid = K, u.P
            u.rt1 = u.P[:, 0, :].rearrange("p (n t) -> p n t", n=2)
            u.rt2 = u.P[:, 1, :].rearrange("p (n t) -> p n t", n=2)
            u.gz = PT[:, 0:GT].rearrange("p (t d) -> p t d", t=TT)
            u.gdiag = u.ctxT[:, :].rearrange("p (n b k) -> p n b k", n=2, b=GB)
            u.mW1 = [PT, u.mW1b[:, :]]
            u.us = u.zz = K
            u.z = u.P
            return u

        streams = (stream("f", 0), stream("s", 1))
        scratch = sb("scratch", [128, 1])

        loaded0 = semaphore("loaded0")
        loaded1 = semaphore("loaded1")
        loadedp = semaphore("loadedp")
        loaded2 = semaphore("loaded2")
        loadedc = semaphore("loadedc")
        loadedr = semaphore("loadedr")
        zeroed_q = semaphore("zeroed_q")
        zeroed_v = semaphore("zeroed_v")
        zeroed_b = semaphore("zeroed_b")
        gexp = semaphore("gexp")
        nsig = semaphore("nsig")
        decayed = semaphore("decayed")
        made = semaphore("made")
        LOADED0, LOADEDP, LOADED1, LOADED2 = 16, 3 * 16, 4 * 16, (6 + 8) * 16


        class Due:

            def __init__(self, count):
                self.count = count

        class Counts:

            def __init__(self, n):
                self.n, self.seen = n, {}

            def at(self, s, name, count, groups_back=0):
                n, total = self.n, s.tally.total[name]
                mark = count - groups_back * total
                if isinstance(n, int) and n < groups_back or self.seen.get((s.tag, name), -10**9) >= mark:
                    return None
                self.seen[s.tag, name] = mark
                return Due(n * total + mark)

            def done(self, s, name, stage):
                return self.at(s, name, s.tally.after(name, stage))

            def step(self, s, name, stage, left):
                return self.at(s, name, s.tally.after(name, stage) - left)

            def before(self, s, name, stage):
                back, count = s.tally.previous(name, stage)
                return self.at(s, name, count, back)

            def same_kind(self, s, name, stage, lag):
                back, other = s.tally.same_kind(stage, lag)
                return self.at(s, name, s.tally.after(name, other), back)

            def last_group(self, s, name, stage):
                return self.at(s, name, s.tally.after(name, stage), 1)

        def program(eng, emit):
            with eng.Fori(0, STEPS) as t:
                emit(t, Counts(t + 1))

        block = ctx.enter_context(nc.Block())

        @block.sync
        def _(sp):
            def load(step, w):
                for k in range(PAIR):
                    for s in streams:
                        u, at = s.own[k], (step, s.number, k)
                        if due := w.last_group(s, "hmean", ("g1", "f1", 0, k)):
                            sp.wait_ge(s.sem["hmean"], due.count)
                        sp.dma_start(u.xinT[:, :], xT_d[at]).then_inc(s.sem[f"loaded_xT{k}"], 16)
                        if due := w.last_group(s, "full_T", ("gen2", "f1", GB - 1, k)):
                            sp.wait_ge(s.sem["full_T"], due.count)
                        sp.dma_start(u.ctxT[:, :], ctxT_d[at]).then_inc(s.sem[f"loaded_ctx{k}"], 16)
                        if due := w.last_group(s, "full_M", ("out", "f1", 1, k)):
                            sp.wait_ge(s.sem["full_M"], due.count)
                        sp.dma_start(u.mask_i, mask_d[at].partition_broadcast(128)).then_inc(s.sem[f"loaded_mask{k}"], 16)
                        if due := w.last_group(s, f"stored{k}", ("store", "f1", 0, k)):
                            sp.wait_ge(s.sem[f"stored{k}"], due.count)
                        sp.dma_start(u.x[:, :, :], x_d[at]).then_inc(s.sem[f"loaded_x{k}"], 16)

            sp.dma_start(sq[:, 0:4, :], squares[:, 0:4, :]).then_inc(loaded0, 16)
            load(0, Counts(0))
            sp.dma_start(sq[:, 4:8, :], squares[:, 4:8, :]).then_inc(loaded1, 16)
            sp.dma_start(wg_sb[:, :], moe_g).then_inc(loaded1, 16)
            sp.dma_start(w1_sb[:, :, :], moe_w1).then_inc(loaded1, 16)
            sp.dma_start(w2_sb[:, :, :], moe_w2).then_inc(loaded1, 16)
            sp.dma_start(sq[:, N_SQ0 + 2:, :], squares[:, N_SQ0 + 2:, :]).then_inc(loaded2, 16)
            sp.dma_start(gw2_sb[:, :, :], gw2r).then_inc(loaded2, 16)
            sp.dma_start(base1[:, :], ff_w1).then_inc(loaded2, 16)
            sp.dma_start(base2[:, :], ff_w2).then_inc(loaded2, 16)
            sp.dma_start(tw1_sb[:, :, :, :], ff_tw1).then_inc(loaded2, 16)
            sp.dma_start(tw2_sb[:, :, :, :], ff_tw2).then_inc(loaded2, 16)
            sp.wait_ge(zeroed_b, 2)
            for e in range(4):
                sp.dma_start(tb1_sb[32 * e:32 * e + 1, :, :], ff_tb1[e:e + 1]).then_inc(loaded2, 16)
                sp.dma_start(tb2_sb[32 * e:32 * e + 1, :, :], ff_tb2[e:e + 1]).then_inc(loaded2, 16)
            with sp.Fori(0, STEPS - 1) as t:
                load(t + 1, Counts(t + 2))

        @block.tensor
        def _(pe):
            mm = nc.tensor.matmul

            def source(s, l, k):
                u = s.own[k]
                return {"a0": u.xinT, "c1": u.hT}.get(l, u.xT)

            def wait_source(s, l, k, w):
                if l == "a0":
                    if due := w.done(s, f"loaded_xT{k}", ("load", "in", 0, k)):
                        pe.wait_ge(s.sem[f"loaded_xT{k}"], due.count)
                else:
                    before = {"c0": ("xt", "a0", 0, k), "m0": ("xt", "c0", 0, k), "r1": ("xt", "m0", 0, k),
                              "s1": ("xt", "r1", 0, k), "c1": ("oproj", "s1", 0, k), "f1": ("xt", "c1", 0, k)}[l]
                    if due := w.done(s, "free_M", before):
                        pe.wait_ge(s.sem["free_M"], due.count)

            def emit(t, w):
                for who, stage in order:
                    s = streams[who]
                    name, l, b, k = stage
                    u = s.own[k]
                    M, S, T, Y = (s.bank[m] for m in "MSTY")
                    X = source(s, l, k)
                    if name == "proj":
                        if l == "c0":
                            pe.wait_ge(loaded1, LOADED1)
                        if l == "r1":
                            pe.wait_ge(made, 1)
                            pe.wait_ge(loaded2, LOADED2)
                        wait_source(s, l, k, w)
                        kX = X
                        if l in ("c0", "c1"):
                            if due := w.done(s, f"loaded_ctx{k}", ("load", "in", 0, k)):
                                pe.wait_ge(s.sem[f"loaded_ctx{k}"], due.count)
                            kX = u.ctxT
                        if due := w.before(s, "free_M", stage):
                            pe.wait_ge(s.sem["free_M"], due.count)
                        mq = mm(M[:, 0:GT], W(l + "q"), X[:, :], start=True, stop=True)
                        if l == "r1":
                            mm(M[:, GT:2 * GT], W(l + "k"), kX[:, :], start=True, stop=True).then_inc(s.sem["full_M"], 1)
                            if due := w.before(s, "free_T", stage):
                                pe.wait_ge(s.sem["free_T"], due.count)
                            mm(T[:, 0:GT], wrot[:, 0, :], X[:, :], start=True, stop=True)
                            mm(T[:, GT:2 * GT], wrot[:, 1, :], X[:, :], start=True, stop=True).then_inc(s.sem["full_T"], 1)
                        else:
                            mq.then_inc(s.sem["full_M"], 1)
                            if due := w.before(s, "free_T", stage):
                                pe.wait_ge(s.sem["free_T"], due.count)
                            mm(T[:, 0:GT], W(l + "k"), kX[:, :], start=True, stop=True).then_inc(s.sem["full_T"], 1)
                    elif name == "projv":
                        vX = u.ctxT if l in ("c0", "c1") else X
                        if due := w.before(s, "free_M", stage):
                            pe.wait_ge(s.sem["free_M"], due.count)
                        for q in range(GB):
                            for j2 in range(2):
                                last = mm(M[64 * j2:64 * j2 + 64, 64 * q:64 * q + 64], vX[:, 64 * q:64 * q + 64],
                                          W(l + "v")[:, 64 * j2:64 * j2 + 64], start=True, stop=True)
                        last.then_inc(s.sem["full_M"], 1)
                    elif name == "gate":
                        if due := w.before(s, "free_Y", stage):
                            pe.wait_ge(s.sem["free_Y"], due.count)
                        for t in range(TT):
                            last = mm(Y[:, 128 * t:128 * t + 128], X[:, 128 * t:128 * t + 128], W("r1g"), start=True, stop=True)
                        last.then_inc(s.sem["full_Y"], 1)
                    elif name == "qk":
                        if l != "r1":
                            if due := w.done(s, "free_M", ("proj", l, 0, k)):
                                pe.wait_ge(s.sem["free_M"], due.count)
                            if due := w.done(s, "free_T", ("proj", l, 0, k)):
                                pe.wait_ge(s.sem["free_T"], due.count)
                        if l in ("r1", "c0"):
                            if due := w.done(s, "blocks", ("proj", l, 0, k)):
                                pe.wait_ge(s.sem["blocks"], due.count)
                        if l == "r1":
                            if due := w.done(s, "blocks_q", ("proj", l, 0, k)):
                                pe.wait_ge(s.sem["blocks_q"], due.count)
                        if due := w.before(s, "free_S", stage):
                            pe.wait_ge(s.sem["free_S"], due.count)
                        for qh in range(2):
                            seen = SEQ // 2 if l in CAUSAL and qh == 0 else SEQ
                            last = mm(S[:, 256 * qh:256 * qh + 256].rearrange("p (j k) -> p j k", k=SEQ)[:, :, 0:seen],
                                      u.Q[:, 2 * b + qh, :, :].rearrange("p g q -> p (g q)"), u.K[:, b, :, 0:seen], start=True, stop=True)
                        last.then_inc(s.sem["full_S"], 1)
                    elif name == "tp":
                        if l == "a0":
                            pe.wait_ge(loadedc, 16)
                        if due := w.done(s, "free_S" if l == "r1" else "p", ("qk", l, b, k)):
                            pe.wait_ge(s.sem["free_S" if l == "r1" else "p"], due.count)
                        if due := w.before(s, "free_T", stage):
                            pe.wait_ge(s.sem["free_T"], due.count)
                        for n in range(4):
                            last = nc.tensor.transpose(T[:, 128 * n:128 * n + 128], u.P[:, b % 2, 128 * n:128 * n + 128], ident)
                        last.then_inc(s.sem["full_T"], 1)
                    elif name == "pv":
                        if due := w.done(s, "free_T", ("tp", l, b, k)):
                            pe.wait_ge(s.sem["free_T"], due.count)
                        if b == 0:
                            if due := w.done(s, "free_M", ("projv", l, 0, k)):
                                pe.wait_ge(s.sem["free_M"], due.count)
                        if due := w.before(s, "free_Y", ("pv", l, b, k)):
                            pe.wait_ge(s.sem["free_Y"], due.count)
                        for part in range(1 if l == "r1" else 2):
                            c0 = 64 * part
                            for jp in range(2):
                                for g in range(4):
                                    lhs = u.V[:, 4 * b + g, jp, :, :, :] if part == 0 else C("ones")[:, 32 * jp:32 * jp + 32]
                                    if part == 0:
                                        lhs = lhs.rearrange("p a b d -> p (a b d)")
                                    last = mm(Y[32 * g:32 * g + 32, c0:c0 + 64], lhs,
                                              u.PT[:, 4 * jp + g, :, :].rearrange("p a q -> p (a q)"),
                                              start=(jp == 0), stop=(jp == 1))
                        last.then_inc(s.sem["full_Y"], 1)
                    elif name == "oproj":
                        if due := w.done(s, "free_Y", ("pv", l, GB - 1, k)):
                            pe.wait_ge(s.sem["free_Y"], due.count)
                        if due := w.before(s, "free_M", stage):
                            pe.wait_ge(s.sem["free_M"], due.count)
                        if l == "s1":
                            last = mm(M[:, 0:GT], W("s1o"), u.yT[:, :], start=True, stop=True)
                        for t in range(0 if l == "s1" else TT):
                            part = slice(128 * t, 128 * t + 128)
                            if l == "r1":
                                last = nc.tensor.transpose(M[:, part], u.yT[:, part], ident)
                            else:
                                last = mm(M[:, part], u.yT[:, part], W(l + "o"), start=True, stop=True)
                        last.then_inc(s.sem["full_M"], 1)
                    elif name == "xt":
                        if due := w.done(s, "x", ("ln2", l, 0, k)):
                            pe.wait_ge(s.sem["x"], due.count)
                        if due := w.before(s, "free_M", stage):
                            pe.wait_ge(s.sem["free_M"], due.count)
                        for t in range(TT):
                            last = nc.tensor.transpose(M[:, 128 * t:128 * t + 128], u.x[:, t, :], ident)
                        last.then_inc(s.sem["full_M"], 1)
                    elif name == "logit":
                        wait_source(s, l, k, w)
                        if due := w.before(s, "free_M", stage):
                            pe.wait_ge(s.sem["free_M"], due.count)
                        for t in range(TT):
                            last = mm(M[:, E0 * t:E0 * t + E0], X[:, 128 * t:128 * t + 128], wg_sb[:, :], start=True, stop=True)
                        last.then_inc(s.sem["full_M"], 1)
                    elif name == "w1":
                        bank = "ST"[b % 2]
                        wait_source(s, l, k, w)
                        if due := w.before(s, "free_" + bank, stage):
                            pe.wait_ge(s.sem["free_" + bank], due.count)
                        for n in range(2):
                            last = mm(s.bank[bank][:, GT * n:GT * n + GT], w1_sb[:, b, 128 * n:128 * n + 128], X[:, :], start=True, stop=True)
                        last.then_inc(s.sem["full_" + bank], 1)
                    elif name == "w2":
                        bank = "YM"[b % 2]
                        if due := w.done(s, "hid", ("w1", l, b, k)):
                            pe.wait_ge(s.sem["hid"], due.count)
                        if due := w.before(s, "free_" + bank, stage):
                            pe.wait_ge(s.sem["free_" + bank], due.count)
                        for t in range(TT):
                            for n in range(2):
                                last = mm(s.bank[bank][:, 128 * t:128 * t + 128], u.hid[:, b % 2, GT * n + 128 * t:GT * n + 128 * t + 128],
                                          w2_sb[:, 2 * b + n, :], start=(n == 0), stop=(n == 1))
                        last.then_inc(s.sem["full_" + bank], 1)
                    elif name == "g1":
                        wait_source(s, l, k, w)
                        if due := w.before(s, "free_M", stage):
                            pe.wait_ge(s.sem["free_M"], due.count)
                        mm(M[:, 0:GT], W("f1g"), X[:, :], start=True, stop=True).then_inc(s.sem["full_M"], 1)
                    elif name == "gcol":
                        if due := w.done(s, "hmean", ("g1", l, 0, k)):
                            pe.wait_ge(s.sem["hmean"], due.count)
                        if due := w.before(s, "free_M", stage):
                            pe.wait_ge(s.sem["free_M"], due.count)
                        for n in range(2):
                            last = mm(M[:, GB * n:GB * n + GB], gw2_sb[:, n, :], u.hm[:, :], start=True, stop=True)
                        last.then_inc(s.sem["full_M"], 1)
                    elif name == "mb":
                        if due := w.before(s, "free_M", stage):
                            pe.wait_ge(s.sem["free_M"], due.count)
                        for f in range(FT):
                            o = M[:, 0:TT * FT * 2].rearrange("p (t f b) -> p t f b", t=TT, f=FT)[:, :, f, :]
                            for n in range(2):
                                last = mm(o, tb1_sb[:, n, 128 * f:128 * f + 128], u.gcol[:, n, :].rearrange("p (t b) -> p t b", t=TT),
                                          start=(n == 0), stop=(n == 1))
                        last.then_inc(s.sem["full_M"], 1)
                    elif name in ("gen1", "gen2"):
                        bank, tw = ("S", tw1_sb) if name == "gen1" else ("T", tw2_sb)
                        if due := w.done(s, "gdiag", ("gcol", l, 0, k)):
                            pe.wait_ge(s.sem["gdiag"], due.count)
                        if due := w.before(s, "free_" + bank, stage):
                            pe.wait_ge(s.sem["free_" + bank], due.count)
                        for n in range(2):
                            for c in range(4):
                                last = mm(s.bank[bank][32 * c:32 * c + 32, :], u.gdiag[:, n, b, :], tw[:, c, n, :], start=(n == 0), stop=(n == 1))
                        last.then_inc(s.sem["full_" + bank], 1)
                    elif name == "u":
                        if due := w.done(s, "free_S", ("gen1", l, 2 * b + 1, k)):
                            pe.wait_ge(s.sem["free_S"], due.count)
                        if due := w.before(s, "free_M", stage):
                            pe.wait_ge(s.sem["free_M"], due.count)
                        for n in range(2):
                            q = 2 * b + n
                            last = mm(M[64 * n:64 * n + 64, :], X[:, 64 * q:64 * q + 64], u.mW1[n], start=True, stop=True)
                        last.then_inc(s.sem["full_M"], 1)
                    elif name == "ut":
                        if due := w.done(s, "free_M", ("u", l, b, k)):
                            pe.wait_ge(s.sem["free_M"], due.count)
                        if due := w.before(s, "free_Y", stage):
                            pe.wait_ge(s.sem["free_Y"], due.count)
                        for f in range(FT):
                            last = nc.tensor.transpose(Y[:, 128 * f:128 * f + 128], u.us[:, b, 128 * f:128 * f + 128], ident)
                        last.then_inc(s.sem["full_Y"], 1)
                    elif name == "out":
                        if due := w.done(s, "act", ("act", l, b, k)):
                            pe.wait_ge(s.sem["act"], due.count)
                        if due := w.done(s, "free_T", ("gen2", l, 2 * b + 1, k)):
                            pe.wait_ge(s.sem["free_T"], due.count)
                        if due := w.before(s, "free_M", stage):
                            pe.wait_ge(s.sem["free_M"], due.count)
                        for n in range(2):
                            q = 2 * b + n
                            o = M[64 * n:64 * n + 64, 0:D]
                            for f in range(FT):
                                mm(o, u.zz[:, b, 128 * f + 64 * n:128 * f + 64 * n + 64], u.mW2[:, n, 128 * f:128 * f + 128], start=(f == 0), stop=False)
                            for m in range(2):
                                last = mm(o, u.gcol[:, m, q:q + 1].to_broadcast([128, 64]), tb2_sb[:, m, :], start=False, stop=(m == 1))
                        last.then_inc(s.sem["full_M"], 1)

            pe.wait_ge(loaded0, LOADED0)
            program(pe, emit)

        @block.scalar
        def _(act):
            fn = nc.scalar.activation

            def emit(t, w):
                for who, stage in order:
                    s = streams[who]
                    name, l, b, k = stage
                    u = s.own[k]
                    M, S, T, Y = (s.bank[m] for m in "MSTY")
                    if name == "proj":
                        if l == "r1":
                            if due := w.done(s, "rope", stage):
                                act.wait_ge(s.sem["rope"], due.count)
                            src = u.rt1[:, 0, :]
                        else:
                            if due := w.done(s, "full_M", stage):
                                act.wait_ge(s.sem["full_M"], due.count)
                            src = M[:, 0:GT]
                        for g in range(4):
                            p = slice(32 * g, 32 * g + 32)
                            i = src[p, :].rearrange("p (a q) -> p a q", q=32)
                            o = u.Q[p, :, g, :]
                            if l in ("s1", "c1"):
                                last = fn(o, i, ACT.Identity, bias=V("bq_" + l[0], 32 * g, 32 * g + 32))
                            else:
                                last = fn(o, i, ACT.Copy)
                        last.then_inc(s.sem["blocks_q" if l == "r1" else "free_M"], 1)
                        src = T[:, 0:GT]
                        if l == "r1":
                            src = u.rt1[:, 1, :]
                        elif l == "c0":
                            if due := w.done(s, "free_T", stage):
                                act.wait_ge(s.sem["free_T"], due.count)
                            src = u.kz
                        else:
                            if due := w.done(s, "full_T", stage):
                                act.wait_ge(s.sem["full_T"], due.count)
                        bias = {"s1": bk_s, "c1": bk_c}.get(l)
                        for j in range(4):
                            o, i = u.K[:, :, j, :], src.rearrange("p (b k) -> p b k", b=GB)
                            if bias is None:
                                last = fn(o, i, ACT.Copy, scale=C("jmask")[:, j:j + 1])
                            else:
                                last = fn(o, i, ACT.Identity, bias=bias[:, j:j + 1], scale=C("jmask")[:, j:j + 1])
                        last.then_inc(s.sem["blocks" if l in ("r1", "c0") else "free_T"], 1)
                    elif name == "gate":
                        if due := w.done(s, "free_Y", stage):
                            act.wait_ge(s.sem["free_Y"], due.count)
                        fn(u.gate[:, :, :], u.gz[:, :, :], ACT.Tanh, scale=0.5).then_inc(s.sem["gtanh"], 1)
                    elif name == "qk" and l != "r1":
                        if due := w.done(s, "free_S" if l == "c1" else "shifted", stage):
                            act.wait_ge(s.sem["free_S" if l == "c1" else "shifted"], due.count)
                        for part in seen(u.P[:, b % 2, :], l):
                            last = fn(part, part, ACT.Exp, scale=SCALE)
                        last.then_inc(s.sem["p"], 1)
                    elif name == "tp":
                        if due := w.done(s, "full_T", stage):
                            act.wait_ge(s.sem["full_T"], due.count)
                        if l == "r1" and b == 0:
                            if due := w.done(s, "gate", ("gate", l, 0, k)):
                                act.wait_ge(s.sem["gate"], due.count)
                        i = T[:, :].rearrange("p (a g q) -> p a g q", a=2, q=32)
                        o = u.PT[:, :, :, :].rearrange("p g a q -> p a g q")
                        fn(o, i, ACT.Copy).then_inc(s.sem["free_T"], 1)
                    elif name == "pv" and l == "r1":
                        if due := w.done(s, "full_Y", ("pv", l, b, k)):
                            act.wait_ge(s.sem["full_Y"], due.count)
                        fn(u.yT[:, SEQ * b:SEQ * b + SEQ], Y[:, 0:SEQ], ACT.Copy).then_inc(s.sem["free_Y"], 1)
                    elif name == "oproj" and l == "s1":
                        if due := w.done(s, "full_M", stage):
                            act.wait_ge(s.sem["full_M"], due.count)
                        fn(u.hT[:, :], M[:, 0:GT], ACT.Identity, bias=V("bo_s")).then_inc(s.sem["free_M"], 1)
                    elif name == "xt":
                        if due := w.done(s, "full_M", stage):
                            act.wait_ge(s.sem["full_M"], due.count)
                        fn(u.xT[:, :], M[:, 0:GT], ACT.Copy).then_inc(s.sem["free_M"], 1)
                    elif name == "logit":
                        if due := w.done(s, "free_M", stage):
                            act.wait_ge(s.sem["free_M"], due.count)
                        fn(u.lg[:, :, :], u.lg[:, :, :], ACT.Exp).then_inc(s.sem["lexp"], 1)
                    elif name == "w1":
                        bank = "ST"[b % 2]
                        if due := w.done(s, "full_" + bank, stage):
                            act.wait_ge(s.sem["full_" + bank], due.count)
                        if due := w.same_kind(s, "hid", stage, 2):
                            act.wait_ge(s.sem["hid"], due.count)
                        fn(u.hr[:, b % 2, :], s.bank[bank][:, :], ACT.Relu).then_inc(s.sem["free_" + bank], 1)
                    elif name == "g1":
                        if due := w.done(s, "full_M", stage):
                            act.wait_ge(s.sem["full_M"], due.count)
                        fn(u.gh[:, :], M[:, 0:GT], ACT.Relu, bias=V("gb1")).then_inc(s.sem["free_M"], 1)
                    elif name == "u":
                        if due := w.done(s, "full_M", stage):
                            act.wait_ge(s.sem["full_M"], due.count)
                        fn(u.us[:, b, :], M[:, :], ACT.Copy).then_inc(s.sem["free_M"], 1)
                    elif name == "gelu":
                        if due := w.done(s, "zcub", stage):
                            act.wait_ge(s.sem["zcub"], due.count)
                        fn(u.zz[:, b, :], u.zz[:, b, :], ACT.Tanh, scale=8 * GELU_A * GELU_C).then_inc(s.sem["tanh"], 1)
                    elif name == "store":
                        if due := w.done(s, "x", ("ln2", l, 0, k)):
                            act.wait_ge(s.sem["x"], due.count)
                        act.dma_start(out_d[t, s.number, k], u.x[:, :, :]).then_inc(s.sem[f"stored{k}"], 16)

            act.dma_start(con1[:, :], consts1).then_inc(loadedp, 16)
            act.dma_start(col[:, :], cols).then_inc(loadedp, 16)
            act.dma_start(sq[:, N_SQ0:N_SQ0 + 2, :], squares[:, N_SQ0:N_SQ0 + 2, :]).then_inc(loadedp, 16)
            act.dma_start(con[:, :], consts).then_inc(loadedc, 16)
            act.dma_start(row[:, :], rows.partition_broadcast(128)).then_inc(loadedr, 16)
            act.wait_ge(loadedp, LOADEDP)
            fn(dtmp[:, 0, :], V("gamma"), ACT.Exp, scale=-1.0).then_inc(gexp, 1)
            act.wait_ge(nsig, 3)
            for j in range(4):
                dst = decay.rearrange("p (a j k) -> p a j k", a=2, j=4)[:, :, j, :]
                last = fn(dst, dst, ACT.Exp, scale=dtmp[:, 2, j:j + 1])
            last.then_inc(decayed, 1)
            act.wait_ge(loadedc, 16)
            act.wait_ge(zeroed_q, STREAMS * PAIR)
            program(act, emit)
            for s in streams:
                for k in range(PAIR):
                    act.wait_ge(s.sem[f"stored{k}"], 16 * (STEPS + 1))

        @block.vector
        def _(dve):
            v = nc.vector
            tt = v.tensor_tensor
            ts = v.tensor_scalar
            stt = v.scalar_tensor_tensor

            def take_wait():
                v.memset(scratch[:, :], 0.0)

            def emit(t, w):
                for who, stage in order:
                    s = streams[who]
                    name, l, b, k = stage
                    u = s.own[k]
                    M, S, T, Y = (s.bank[m] for m in "MSTY")
                    P = u.P[:, b % 2, :]
                    if name == "mask":
                        if due := w.done(s, f"loaded_mask{k}", ("load", "in", 0, k)):
                            dve.wait_ge(s.sem[f"loaded_mask{k}"], due.count)
                        ts(u.mW2[:, 0, GT:2 * GT], u.mask_i, 0, -1e9 * ROOT8, ALU.is_equal, ALU.mult)\
                            .then_inc(s.sem["keep"], 1)
                        ts(u.keep, u.mask_i, 0, None, ALU.not_equal).then_inc(s.sem["keep"], 1)
                    elif name == "proj" and l in ("r1", "c0"):
                        if l == "r1":
                            dve.wait_ge(loadedr, 16)
                            dve.wait_ge(loaded2, LOADED2)
                        if l == "r1":
                            if due := w.done(s, "full_M", stage):
                                dve.wait_ge(s.sem["full_M"], due.count)
                            cos = C1("cos").unsqueeze(1).to_broadcast([128, GB, SEQ])
                            sin = C1("sin").unsqueeze(1).to_broadcast([128, GB, SEQ])
                            for n, bias in ((0, "bq_r"), (1, "bk_r")):
                                last = stt(out=u.rt1[:, n, :].rearrange("p (b s) -> p b s", b=GB),
                                           in0=M[:, GT * n:GT * n + GT].rearrange("p (b s) -> p b s", b=GB),
                                           scalar=V(bias), in1=cos, op0=ALU.add, op1=ALU.mult)
                            last.then_inc(s.sem["free_M"], 1)
                            if due := w.done(s, "full_T", stage):
                                dve.wait_ge(s.sem["full_T"], due.count)
                            for n in range(2):
                                last = stt(out=u.rt2[:, n, :].rearrange("p (b s) -> p b s", b=GB),
                                           in0=T[:, GT * n:GT * n + GT].rearrange("p (b s) -> p b s", b=GB),
                                           scalar=brot[:, n:n + 1], in1=sin, op0=ALU.add, op1=ALU.mult)
                            last.then_inc(s.sem["free_T"], 1)
                        elif l == "c0":
                            if due := w.done(s, "keep", ("mask", "in", 0, k)):
                                dve.wait_ge(s.sem["keep"], due.count)
                            if due := w.done(s, "full_T", stage):
                                dve.wait_ge(s.sem["full_T"], due.count)
                            tt(u.kz, T[:, 0:GT], u.keep, ALU.mult).then_inc(s.sem["free_T"], 1)
                    elif name == "projv":
                        if due := w.done(s, "full_M", stage):
                            dve.wait_ge(s.sem["full_M"], due.count)
                        for j2 in range(2):
                            p = slice(64 * j2, 64 * j2 + 64)
                            i = M[p, 0:GT].rearrange("p (m a d) -> p m a d", a=2, d=HD)
                            o = u.V[p, :, :, :, :, :].rearrange("p m a b c d -> p m (a b) c d")[:, :, 0:4:3, j2, :]
                            if l in ("r1", "s1", "c1"):
                                bv = r_at["bv_" + l[0]][0] + 64 * j2
                                rowv = row[p, bv:bv + 64].unsqueeze(1).to_broadcast([64, GB, 64])
                                for jp in range(2):
                                    last = tt(o[:, :, jp, :].rearrange("p (b g) d -> p b g d", b=GB),
                                              i[:, :, jp, :].rearrange("p (b g) d -> p b g d", b=GB),
                                              rowv.rearrange("p b (g a d) -> p b g a d", a=2, d=HD)[:, :, :, jp, :], ALU.add)
                            else:
                                last = v.tensor_copy(o, i)
                        last.then_inc(s.sem["free_M"], 1)
                    elif name == "gate":
                        if due := w.done(s, "full_Y", stage):
                            dve.wait_ge(s.sem["full_Y"], due.count)
                        tt(u.gz[:, :, :], Y[:, 0:GT].rearrange("p (t d) -> p t d", t=TT),
                           R("bg_r").unsqueeze(1).to_broadcast([128, TT, D]), ALU.add).then_inc(s.sem["free_Y"], 1)
                        if due := w.done(s, "gtanh", stage):
                            dve.wait_ge(s.sem["gtanh"], due.count)
                        stt(out=u.gate[:, :, :], in0=u.gate[:, :, :], scalar=1.0, in1=u.gz[:, :, :], op0=ALU.add, op1=ALU.mult)\
                            .then_inc(s.sem["gate"], 1)
                    elif name == "qk":
                        if due := w.done(s, "full_S", stage):
                            dve.wait_ge(s.sem["full_S"], due.count)
                        if due := w.same_kind(s, "full_T", ("tp", l, b, k), 2):
                            dve.wait_ge(s.sem["full_T"], due.count)
                        mx = u.mx[:, b % 2, :]
                        rows8 = "p (a k) -> p a k"
                        if l == "r1":
                            tt(P, S[:, :], decay, ALU.mult).then_inc(s.sem["free_S"], 1)
                            continue
                        if l == "c1":
                            v.tensor_reduce(mx, S[:, :].rearrange(rows8, k=SEQ), AX.X, ALU.max).then_inc(s.sem["rowmax"], 1)
                            if due := w.done(s, "rowmax", stage):
                                dve.wait_ge(s.sem["rowmax"], due.count)
                            tt(P.rearrange(rows8, k=SEQ), S[:, :].rearrange(rows8, k=SEQ), mx.unsqueeze(2).to_broadcast([128, 8, SEQ]),
                               ALU.subtract).then_inc(s.sem["free_S"], 1)
                            continue
                        if l == "c0":
                            tt(P.rearrange(rows8, k=SEQ), S[:, :].rearrange(rows8, k=SEQ),
                               u.mbias[:, b, :].unsqueeze(1).to_broadcast([128, 8, SEQ]), ALU.add).then_inc(s.sem["free_S"], 1)
                        else:
                            if b < 2:
                                v.memset(P.rearrange(rows8, k=SEQ)[:, 0:4, SEQ // 2:], 0.0).then_inc(s.sem["zeros"], 1)
                            for o, i, c in zip(seen(P, l), seen(S[:, :], l), seen(C("causal"), l)):
                                last = tt(o, i, c, ALU.add)
                            last.then_inc(s.sem["free_S"], 1)
                        if due := w.done(s, "free_S", stage):
                            dve.wait_ge(s.sem["free_S"], due.count)
                        rows = [mx[:, 0:4], mx[:, 4:8]] if l in CAUSAL else [mx]
                        for o, i in zip(rows, seen(P, l)):
                            last = v.tensor_reduce(o, i, AX.X, ALU.max)
                        last.then_inc(s.sem["rowmax"], 1)
                    elif name == "pv" and l != "r1":
                        if due := w.done(s, "full_Y", ("pv", l, b, k)):
                            dve.wait_ge(s.sem["full_Y"], due.count)
                        v.reciprocal(u.rz[:, b % 2, :], Y[:, SEQ:2 * SEQ]).then_inc(s.sem["recip"], 1)
                        if due := w.done(s, "recip", stage):
                            dve.wait_ge(s.sem["recip"], due.count)
                        tt(u.yT[:, SEQ * b:SEQ * b + SEQ], Y[:, 0:SEQ], u.rz[:, b % 2, :], ALU.mult)\
                            .then_inc(s.sem["free_Y"], 1)
                    elif name == "oproj" and l != "s1":
                        if due := w.done(s, "full_M", stage):
                            dve.wait_ge(s.sem["full_M"], due.count)
                        new = M[:, 0:GT].rearrange("p (t d) -> p t d", t=TT)
                        if l == "r1":
                            if due := w.done(s, "gate", ("gate", l, 0, k)):
                                dve.wait_ge(s.sem["gate"], due.count)
                            stt(out=u.r[:, :, :], in0=new, scalar=0.5, in1=u.gate[:, :, :], op0=ALU.mult, op1=ALU.mult)\
                                .then_inc(s.sem["free_M"], 1)
                            if due := w.done(s, "free_M", stage):
                                dve.wait_ge(s.sem["free_M"], due.count)
                            if due := w.done(s, "x", ("ln2", "m0", 0, k)):
                                dve.wait_ge(s.sem["x"], due.count)
                            tt(u.r[:, :, :], u.r[:, :, :], u.x[:, :, :], ALU.add).then_inc(s.sem["resid"], 1)
                        else:
                            if due := w.done(s, "xb", ("xb", {"a0": "in", "c0": "a0", "c1": "r1"}[l], 0, k)):
                                dve.wait_ge(s.sem["xb"], due.count)
                            tt(u.r[:, :, :], new, u.xb[:, :, :], ALU.add).then_inc(s.sem["free_M"], 1)
                    elif name == "ln1":
                        if l == "r1":
                            if due := w.done(s, "resid", ("oproj", l, 0, k)):
                                dve.wait_ge(s.sem["resid"], due.count)
                        elif l == "m0":
                            if due := w.done(s, "free_M", ("w2", l, E0 - 1, k)):
                                dve.wait_ge(s.sem["free_M"], due.count)
                        elif l == "f1":
                            if due := w.done(s, "free_M", ("out", l, 1, k)):
                                dve.wait_ge(s.sem["free_M"], due.count)
                        else:
                            if due := w.done(s, "free_M", ("oproj", l, 0, k)):
                                dve.wait_ge(s.sem["free_M"], due.count)
                        for t in range(TT):
                            last = v.bn_stats(u.st[:, t, :], u.r[:, t, :])
                        last.then_inc(s.sem["stats"], 1)
                        if due := w.done(s, "stats", stage):
                            dve.wait_ge(s.sem["stats"], due.count)
                        take_wait()
                        for t in range(TT):
                            last = v.bn_aggr(u.mv[:, t, :], u.st[:, t, :])
                        last.then_inc(s.sem["moments"], 1)
                        if due := w.done(s, "moments", stage):
                            dve.wait_ge(s.sem["moments"], due.count)
                        ts(u.ve[:, :], u.mv[:, :, 1], EPS, None, ALU.add).then_inc(s.sem["vareps"], 1)
                    elif name == "ln2":
                        if due := w.done(s, "rstd", ("ln1", l, 0, k)):
                            dve.wait_ge(s.sem["rstd"], due.count)
                        for t in range(TT):
                            last = ts(u.x[:, t, :], u.r[:, t, :], u.mv[:, t, 0:1], u.rstd[:, t:t + 1], ALU.subtract, ALU.mult)
                        last.then_inc(s.sem["x"], 1)
                    elif name == "logit":
                        if due := w.done(s, "full_M", stage):
                            dve.wait_ge(s.sem["full_M"], due.count)
                        i = M[:, 0:TT * E0].rearrange("p (t e) -> p t e", t=TT)
                        v.tensor_reduce(u.lmx[:, :], i, AX.X, ALU.max).then_inc(s.sem["lmax"], 1)
                        if due := w.done(s, "lmax", stage):
                            dve.wait_ge(s.sem["lmax"], due.count)
                        tt(u.lg[:, :, :], i, u.lmx[:, :].unsqueeze(2).to_broadcast([128, TT, E0]), ALU.subtract).then_inc(s.sem["free_M"], 1)
                    elif name == "route":
                        step = [0]

                        def then(ins):
                            step[0] += 1
                            ins.then_inc(s.sem["routed"], 1)
                            if due := w.step(s, "routed", stage, ROUTE_STEPS - step[0]):
                                dve.wait_ge(s.sem["routed"], due.count)

                        if due := w.done(s, "lexp", ("logit", l, 0, k)):
                            dve.wait_ge(s.sem["lexp"], due.count)
                        then(v.tensor_reduce(u.lsum[:, :], u.lg[:, :, :], AX.X, ALU.add))
                        then(v.reciprocal(u.lrec[:, :], u.lsum[:, :]))
                        then(tt(u.prob[:, :, :], u.lg[:, :, :], u.lrec[:, :].unsqueeze(2).to_broadcast([128, TT, E0]), ALU.mult))
                        take_wait()
                        for t in range(TT):
                            last = v.max(out=u.top[:, t, :], in_=u.prob[:, t, :])
                        then(last)
                        take_wait()
                        for t in range(TT):
                            last = v.max_index(u.topi[:, t, :], u.top[:, t, :], u.prob[:, t, :])
                        then(last)
                        v.tensor_copy(u.topf[:, :, :], u.topi[:, :, 0:2])
                        then(tt(u.wsum[:, :], u.top[:, :, 0], u.top[:, :, 1], ALU.add))
                        then(ts(u.wrec[:, :], u.wsum[:, :], 1e-8, None, ALU.add))
                        then(v.reciprocal(u.wsum[:, :], u.wrec[:, :]))
                        then(tt(u.wn[:, :, :], u.top[:, :, 0:2], u.wsum[:, :].unsqueeze(2).to_broadcast([128, TT, 2]), ALU.mult))
                        for t in range(TT):
                            for k in range(2):
                                last = ts(u.pick[:, t, k, :], C("iota"), u.topf[:, t, k:k + 1], u.wn[:, t, k:k + 1], ALU.is_equal, ALU.mult)
                        then(last)
                        tt(u.comb[:, :, :], u.pick[:, :, 0, :], u.pick[:, :, 1, :], ALU.add).then_inc(s.sem["comb"], 1)
                    elif name == "w2":
                        bank = "YM"[b % 2]
                        if due := w.done(s, "full_" + bank, stage):
                            dve.wait_ge(s.sem["full_" + bank], due.count)
                        if due := w.done(s, "comb", ("route", l, 0, k)):
                            dve.wait_ge(s.sem["comb"], due.count)
                        if b:
                            if due := w.done(s, "free_" + "YM"[1 - b % 2], ("w2", l, b - 1, k)):
                                dve.wait_ge(s.sem["free_" + "YM"[1 - b % 2]], due.count)
                        else:
                            if due := w.done(s, "x", ("ln2", "c0", 0, k)):
                                dve.wait_ge(s.sem["x"], due.count)
                        for t in range(TT):
                            last = stt(out=u.r[:, t, :], in0=s.bank[bank][:, D * t:D * t + D], scalar=u.comb[:, t, b:b + 1],
                                       in1=(u.r if b else u.x)[:, t, :], op0=ALU.mult, op1=ALU.add)
                        last.then_inc(s.sem["free_" + bank], 1)
                    elif name == "g1":
                        if due := w.done(s, "free_M", stage):
                            dve.wait_ge(s.sem["free_M"], due.count)
                        v.tensor_reduce(u.hm[:, :], u.gh[:, :].rearrange("p (b k) -> p b k", k=SEQ), AX.X, ALU.add).then_inc(s.sem["hmean"], 1)
                    elif name == "gcol":
                        if due := w.done(s, "full_M", stage):
                            dve.wait_ge(s.sem["full_M"], due.count)
                        for n in range(2):
                            last = ts(u.gcol[:, n, :], M[:, GB * n:GB * n + GB], 1.0 / SEQ, V("gb2")[:, n:n + 1], ALU.mult, ALU.add)
                        last.then_inc(s.sem["free_M"], 1)
                    elif name == "mb":
                        if due := w.done(s, "full_M", stage):
                            dve.wait_ge(s.sem["full_M"], due.count)
                        i = M[:, 0:TT * FT * 2].rearrange("p (t f b) -> p t f b", t=TT, f=FT)
                        for t2 in range(TT):
                            last = stt(out=u.mb[:, t2, :, :], in0=i[:, t2, :, :], scalar=0.5,
                                       in1=b1h[:, :].unsqueeze(2).to_broadcast([128, FT, 2]), op0=ALU.mult, op1=ALU.add)
                        last.then_inc(s.sem["free_M"], 1)
                    elif name == "gen1":
                        if due := w.done(s, "full_S", stage):
                            dve.wait_ge(s.sem["full_S"], due.count)
                        tt(u.mW1[b % 2], S[:, :], base1[:, :], ALU.add).then_inc(s.sem["free_S"], 1)
                    elif name == "gen2":
                        if due := w.done(s, "full_T", stage):
                            dve.wait_ge(s.sem["full_T"], due.count)
                        tt(u.mW2[:, b % 2, :], T[:, :], base2[:, :], ALU.add)\
                            .then_inc(s.sem["free_T"], 1)
                    elif name == "ut":
                        if due := w.done(s, "full_Y", stage):
                            dve.wait_ge(s.sem["full_Y"], due.count)
                        if due := w.done(s, "free_M", ("mb", l, 0, k)):
                            dve.wait_ge(s.sem["free_M"], due.count)
                        stt(out=u.z[:, b, :].rearrange("p (a k) -> p a k", k=SEQ), in0=Y[:, :].rearrange("p (a k) -> p a k", k=SEQ), scalar=0.5,
                            in1=u.mb[:, b, :, :].rearrange("p f b -> p (f b)").unsqueeze(2).to_broadcast([128, 2 * FT, SEQ]),
                            op0=ALU.mult, op1=ALU.add)\
                            .then_inc(s.sem["free_Y"], 1)
                    elif name == "gelu":
                        if due := w.done(s, "zsq", stage):
                            dve.wait_ge(s.sem["zsq"], due.count)
                        stt(out=u.zz[:, b, :], in0=u.zz[:, b, :], scalar=0.25 / GELU_A, in1=u.z[:, b, :], op0=ALU.add, op1=ALU.mult)\
                            .then_inc(s.sem["zcub"], 1)
                    elif name == "act":
                        if due := w.done(s, "tanh", ("gelu", l, b, k)):
                            dve.wait_ge(s.sem["tanh"], due.count)
                        stt(out=u.zz[:, b, :], in0=u.zz[:, b, :], scalar=1.0, in1=u.z[:, b, :], op0=ALU.add, op1=ALU.mult)\
                            .then_inc(s.sem["act"], 1)
                    elif name == "out":
                        if due := w.done(s, "full_M", stage):
                            dve.wait_ge(s.sem["full_M"], due.count)
                        if due := w.done(s, "xb", ("xb", "c1", 0, k)):
                            dve.wait_ge(s.sem["xb"], due.count)
                        tt(u.r[:, b, :], M[:, 0:D], u.xb[:, b, :], ALU.add).then_inc(s.sem["free_M"], 1)

            for s in streams:
                for u in s.own:
                    v.memset(u.V[:], 0.0).then_inc(zeroed_v, 1)
            dve.wait_ge(loadedp, LOADEDP)
            dve.wait_ge(loadedc, 16)
            for n, wname in ((0, "r1q"), (1, "r1k")):
                pair = W(wname).rearrange("p (i a) -> p i a", a=2)
                turned = wrot[:, n, :].rearrange("p (i a) -> p i a", a=2)
                ts(turned[:, :, 0], pair[:, :, 1], -1.0, None, ALU.mult)
                v.tensor_copy(turned[:, :, 1], pair[:, :, 0])
            for n, bname in ((0, "bqp_r"), (1, "bkp_r")):
                tt(brot[:, n:n + 1], V(bname), C1("sign"), ALU.mult)
            ts(bk_s[:, :], C("jmask"), V("bk_s"), None, ALU.mult)
            ts(bk_c[:, :], C("jmask"), V("bk_c"), None, ALU.mult)
            ts(b1h[:, :], V("b1"), 0.5, None, ALU.mult)
            dve.wait_ge(gexp, 1)
            ts(dtmp[:, 1, :], dtmp[:, 0, :], 1.0, None, ALU.add).then_inc(nsig, 1)
            dve.wait_ge(nsig, 1)
            v.reciprocal(dtmp[:, 3, :], dtmp[:, 1, :]).then_inc(nsig, 1)
            dve.wait_ge(nsig, 2)
            ts(dtmp[:, 2, :], dtmp[:, 3, :], -1.0, None, ALU.mult).then_inc(nsig, 1)
            dve.wait_ge(decayed, 1)
            ts(decay, decay, SCALE, None, ALU.mult).then_inc(made, 1)
            dve.wait_ge(made, 1)

            dve.wait_ge(zeroed_v, STREAMS * PAIR)
            program(dve, emit)

        @block.gpsimd
        def _(pool):
            tt = nc.gpsimd.tensor_tensor

            def emit(t, w):
                for who, stage in order:
                    s = streams[who]
                    name, l, b, k = stage
                    u = s.own[k]
                    if name == "xb":
                        if l == "in":
                            if due := w.done(s, f"loaded_x{k}", ("load", "in", 0, k)):
                                pool.wait_ge(s.sem[f"loaded_x{k}"], due.count)
                            if due := w.last_group(s, "x", ("ln2", "f1", 0, k)):
                                pool.wait_ge(s.sem["x"], due.count)
                        else:
                            if due := w.done(s, "x", ("ln2", l, 0, k)):
                                pool.wait_ge(s.sem["x"], due.count)
                        bias = {"in": "bo_a", "a0": "bo_c0", "r1": "bo_c1", "c1": "b2"}[l]
                        tt(u.xb[:, :, :], u.x[:, :, :], R(bias).unsqueeze(1).to_broadcast([128, TT, D]), ALU.add)\
                            .then_inc(s.sem["xb"], 1)
                    elif name == "proj" and l == "r1":
                        if due := w.done(s, "free_M", stage):
                            pool.wait_ge(s.sem["free_M"], due.count)
                        if due := w.done(s, "free_T", stage):
                            pool.wait_ge(s.sem["free_T"], due.count)
                        tt(u.rt1[:, :, :], u.rt1[:, :, :], u.rt2[:, :, :], ALU.add).then_inc(s.sem["rope"], 1)
                    elif name == "qk" and l in MASKED:
                        if due := w.done(s, "rowmax", stage):
                            pool.wait_ge(s.sem["rowmax"], due.count)
                        mx = u.mx[:, b % 2, :]
                        rows = [mx[:, 0:4], mx[:, 4:8]] if l in CAUSAL else [mx]
                        for part, m in zip(seen(u.P[:, b % 2, :], l), rows):
                            last = tt(part, part, m.unsqueeze(2).to_broadcast([part.shape[0], part.shape[1], part.shape[2]]), ALU.subtract)
                        last.then_inc(s.sem["shifted"], 1)
                    elif name == "ln1":
                        if due := w.done(s, "vareps", stage):
                            pool.wait_ge(s.sem["vareps"], due.count)
                        tt(u.rstd[:, :], u.ve[:, :], C("neghalf"), ALU.pow).then_inc(s.sem["rstd"], 1)
                    elif name == "w1":
                        if due := w.done(s, "free_" + "ST"[b % 2], stage):
                            pool.wait_ge(s.sem["free_" + "ST"[b % 2]], due.count)
                        bank = "YM"[b % 2]
                        if due := w.same_kind(s, "full_" + bank, ("w2", l, b, k), 2):
                            pool.wait_ge(s.sem["full_" + bank], due.count)
                        tt(u.hid[:, b % 2, :], u.hr[:, b % 2, :], u.hr[:, b % 2, :], ALU.mult).then_inc(s.sem["hid"], 1)
                    elif name == "gcol":
                        if due := w.done(s, "free_M", stage):
                            pool.wait_ge(s.sem["free_M"], due.count)
                        o = u.gdiag[:, :, :, :].rearrange("p n b k -> p (n b) k")
                        tt(o, C1("id32").unsqueeze(1).to_broadcast([128, 2 * GB, 32]),
                           u.gcol[:, :, :].rearrange("p n b -> p (n b)").unsqueeze(2).to_broadcast([128, 2 * GB, 32]), ALU.mult)\
                            .then_inc(s.sem["gdiag"], 1)
                    elif name == "gelu":
                        if due := w.done(s, "free_Y", ("ut", l, b, k)):
                            pool.wait_ge(s.sem["free_Y"], due.count)
                        if due := w.same_kind(s, "act", ("act", l, b, k), 2):
                            pool.wait_ge(s.sem["act"], due.count)
                        tt(u.zz[:, b, :], u.z[:, b, :], u.z[:, b, :], ALU.mult).then_inc(s.sem["zsq"], 1)

            for s in streams:
                for name, count in s.tally.total.items():
                    pool.nop().then_inc(s.sem[name], count)
            for s in streams:
                for u in s.own:
                    nc.gpsimd.memset(u.Q[:], 0.0).then_inc(zeroed_q, 1)
            for buf in (tb1_sb, tb2_sb):
                nc.gpsimd.memset(buf[:], 0.0).then_inc(zeroed_b, 1)
            pool.wait_ge(loadedc, 16)
            pool.wait_ge(loadedp, LOADEDP)
            pool.wait_ge(loadedr, 16)
            program(pool, emit)


def _lay_out(i):
    f = lambda a: np.ascontiguousarray(np.asarray(a))

    def parity(w):
        return w.reshape(w.shape[:-1] + (H // 2, 2, HD)).swapaxes(-3, -2).reshape(w.shape)

    heads = lambda w: np.asarray(w).transpose(1, 0, 2).reshape(D, D)
    T = lambda name: np.asarray(i[name]).T
    sq = {"a0q": T("L0_attn_Wq"), "a0k": T("L0_attn_Wk"), "a0v": parity(T("L0_attn_Wv")), "a0o": T("L0_attn_Wo"),
          "c0q": T("L0_xattn_Wq"), "c0k": T("L0_xattn_Wk"), "c0v": parity(T("L0_xattn_Wv")), "c0o": T("L0_xattn_Wo"),
          "r1q": T("L1_attn_Wq"), "r1k": T("L1_attn_Wk"), "r1v": parity(T("L1_attn_Wv")), "r1g": T("L1_attn_Wg"),
          "s1q": heads(i["L1_xattn_Wq1"]), "s1k": heads(i["L1_xattn_Wk1"]), "s1v": parity(heads(i["L1_xattn_Wv1"])),
          "s1o": np.asarray(i["L1_xattn_Wo1"]),
          "c1q": heads(i["L1_xattn_Wq2"]), "c1k": heads(i["L1_xattn_Wk2"]), "c1v": parity(heads(i["L1_xattn_Wv2"])),
          "c1o": np.asarray(i["L1_xattn_Wo2"]), "f1g": T("L1_ffn_gate_w1")}
    p = np.arange(128)
    q = np.arange(2)[None, :, None, None] * 32 + (p % 32)[:, None, None, None]
    k = np.arange(SEQ)[None, None, None, :]
    full = np.zeros((128, 2, 4, SEQ), np.float32)
    ones = np.zeros((128, 2, 2, 2, HD), np.float32)
    for jp in range(2):
        for j2 in range(2):
            ones[64 * j2:64 * j2 + 64, jp, jp, j2] = 1.0
    con = {"ident": np.eye(128), "causal": (full + np.where(k <= q, 0.0, MINUS)).reshape(128, 512),
           "jmask": (p[:, None] // HD) % 4 == np.arange(4)[None, :], "ones": ones.reshape(128, 64),
           "iota": np.broadcast_to(np.arange(8), (128, 8)), "neghalf": np.full((128, 2), -0.5)}
    inv = (1.0 / 10000.0 ** (np.arange(0, HD, 2, dtype=np.float32) / HD)).astype(np.float32)
    ang = (np.arange(SEQ, dtype=np.float32)[None, :] * inv[(p % HD) % (HD // 2)][:, None]).astype(np.float32)
    con1 = {"cos": np.cos(ang), "sin": np.sin(ang), "diff": (full + np.maximum(q - k, 0)).reshape(128, 512),
            "id32": p[:, None] % 32 == np.arange(32)[None, :], "sign": np.where(p % 2 == 0, -1.0, 1.0)[:, None]}
    pack = lambda parts, names: f(np.concatenate([np.asarray(parts[n]).astype(np.float32).reshape(-1, w) for n, w in names.items()], axis=1))
    c = lambda name: np.asarray(i[name]).reshape(-1, 1)
    gb2 = np.asarray(i["L1_ffn_gate_b2"]).reshape(2, 4)
    col = {"bq_r": c("L1_attn_bq"), "bk_r": c("L1_attn_bk"), "bqp_r": c("L1_attn_bq")[p ^ 1], "bkp_r": c("L1_attn_bk")[p ^ 1],
           "bq_s": c("L1_xattn_bq1"), "bk_s": c("L1_xattn_bk1"), "bo_s": c("L1_xattn_bo1"), "bq_c": c("L1_xattn_bq2"),
           "bk_c": c("L1_xattn_bk2"), "gb1": c("L1_ffn_gate_b1"), "b1": np.asarray(i["L1_ffn_b1"]).reshape(FT, 128).T,
           "gb2": gb2.T[p // 32], "gamma": np.asarray(i["L1_attn_gamma"]).reshape(4, 4)[p // 32]}
    r = lambda name: np.asarray(i[name]).reshape(1, -1)
    row = {"bo_a": r("L0_attn_bo"), "bo_c0": r("L0_xattn_bo"), "bg_r": r("L1_attn_bg"), "bo_c1": r("L1_xattn_bo2"),
           "b2": r("L1_ffn_b2"), "bv_r": parity(r("L1_attn_bv")), "bv_s": parity(r("L1_xattn_bv1")), "bv_c": parity(r("L1_xattn_bv2"))}
    same = lambda parts, names: f(np.concatenate([parts[n] for n in names], axis=1))
    x, cx = np.asarray(i["x"]).reshape(-1, D), np.asarray(i["ctx_1024"]).reshape(-1, D)
    tw1 = np.asarray(i["L1_ffn_TW1"]).reshape(2, 4, HID1, 4, 32)
    tw2 = np.asarray(i["L1_ffn_TW2"]).reshape(2, 4, D, FT, 4, 32)
    return {
        "x": f(x), "xT": f(x.T), "ctxT": f(cx.T), "mask": f(i["mask_BxS2_ik0"]),
        "squares": f(np.stack([sq[n] for n in SQUARES], axis=1)),
        "consts": pack(con, CONSTS), "consts1": pack(con1, CONSTS1),
        "cols": same(col, COLS), "rows": same(row, ROWS).reshape(-1),
        "moe_g": f(i["L0_ffn_Wg"]), "moe_w1": f(np.asarray(i["L0_ffn_W1"]).transpose(1, 0, 2)),
        "moe_w2": f(np.asarray(i["L0_ffn_W2"]).reshape(2 * E0, 128, D).transpose(1, 0, 2)),
        "gw2r": f(np.repeat(np.asarray(i["L1_ffn_gate_w2"]).T.reshape(128, 2, 4), 32, axis=2)),
        "ff_w1": f(T("L1_ffn_W1")), "ff_w2": f(T("L1_ffn_W2").reshape(FT, 128, D).transpose(1, 0, 2).reshape(128, HID1)),
        "ff_tw1": f(tw1.transpose(1, 4, 3, 0, 2).reshape(128, 4, 2, HID1)),
        "ff_tw2": f(tw2.transpose(1, 5, 4, 0, 3, 2).reshape(128, 4, 2, HID1)),
        "ff_tb1": f(np.asarray(i["L1_ffn_Tb1"]).reshape(2, 4, HID1).transpose(1, 0, 2)),
        "ff_tb2": f(np.asarray(i["L1_ffn_Tb2"]).reshape(2, 4, D).transpose(1, 0, 2)),
    }


def kernel(**inputs):
    import concourse.bacc as bacc
    from concourse.bass_utils import run_bass_kernel_spmd

    nc = bacc.Bacc("TRN2", target_bir_lowering=False, num_devices=1)
    arrays = {f"in_{k}": a for k, a in _lay_out(inputs).items()}
    args = [nc.dram_tensor(k, a.shape, mybir.dt.from_np(a.dtype), kind="ExternalInput").ap() for k, a in arrays.items()]
    out = nc.dram_tensor("out_dram", (B * SEQ, D), F32, kind="ExternalOutput").ap()
    decoder_kernel(nc, *args, out)
    got = run_bass_kernel_spmd(nc, [arrays], core_ids=[0]).results[0]["out_dram"]
    return got.reshape(B, SEQ, D)
```
